# Optimizing a Trainium2 kernel written in Bass

```python
import numpy as np
import jax
import jax.numpy as jnp

def _softmax(x, axis=-1):
    return jax.nn.softmax(x, axis=axis)
def _gelu(x):
    return jax.nn.gelu(x, approximate=True)
def _silu(x):
    return jax.nn.silu(x)
def _sigmoid(x):
    return jax.nn.sigmoid(x)
def _layernorm(x, axis=-1, eps=1e-5):
    m = jnp.mean(x, axis=axis, keepdims=True)
    v = jnp.var(x, axis=axis, keepdims=True)
    return (x - m) / jnp.sqrt(v + eps)
def _scatter_add(tgt, idx, src, axis=0):
    return tgt.at[idx].add(src)
def _segment_sum(src, seg, n):
    return jax.ops.segment_sum(src, seg, n)

kernel_name = 'mk_conv_preact_d4_conv_nhwc128_e787d1'

def setup_inputs(seed: int = 0):
    np.random.seed(seed)
    _w = jnp.asarray
    def _rec_inputs():
        import jax
        import jax.numpy as jnp
        _gk = jax.random.key(seed)
        x = -0.0002928 + 1 * jax.random.normal(jax.random.fold_in(_gk, 1), (2, 128, 128, 128), jnp.float32)
        return x
    x = _rec_inputs()
    def _L0_conv_setup():
        import jax, jax.numpy as jnp
        import numpy as np
        WS = 16
        HS = 8
        NH = 4
        DIM = 128
        WSH = WS + 2 * HS
        B, H, W = (2, 128, 128)

        def _rel_pos_index():
            r = np.arange(-HS, WS + HS)
            coords = np.stack(np.meshgrid(r, r, indexing='ij'))
            cf = coords.reshape(2, -1)
            rel = (cf[:, :, None] - cf[:, None, :]).transpose(1, 2, 0)
            rel = rel.copy()
            rel[..., 0] += WS + HS - 1
            rel[..., 1] += WS + HS - 1
            rel[..., 0] *= 2 * WS + 2 * HS - 1
            return rel.sum(-1)
        _RPI = _rel_pos_index()
        key = jax.random.key(seed)
        ks = jax.random.split(key, 10)
        p = lambda k, shp: jax.random.normal(k, shp, dtype=jnp.float32) * 0.02
        return {'x': jax.random.normal(ks[0], (B, H, W, DIM), dtype=jnp.float32), 'Wq': p(ks[1], (DIM, DIM)), 'bq': jnp.zeros((DIM,), jnp.float32), 'Wk': p(ks[2], (DIM, DIM)), 'bk': jnp.zeros((DIM,), jnp.float32), 'Wv': p(ks[3], (DIM, DIM)), 'bv': jnp.zeros((DIM,), jnp.float32), 'Wp': p(ks[4], (DIM, DIM)), 'bp': jnp.zeros((DIM,), jnp.float32), 'bias_table': p(ks[5], ((2 * WS + 2 * HS - 1) ** 2, NH)), 'shift_size': 0}
    _L0_conv_all = _L0_conv_setup()
    _L0_conv_in = {k: v for k, v in _L0_conv_all.items() if k in ('Wq', 'bq', 'Wk', 'bk', 'Wv', 'bv', 'Wp', 'bp', 'bias_table', )}
    del _L0_conv_all

    def _L1_conv_setup():
        import jax, jax.numpy as jnp
        import numpy as np
        LN_EPS = 1e-05

        def _layer_norm(h, g, b):
            mu = jnp.mean(h, axis=-1, keepdims=True)
            var = jnp.mean(jnp.square(h - mu), axis=-1, keepdims=True)
            return (h - mu) * jax.lax.rsqrt(var + LN_EPS) * g + b

        def _forward_fourier(x, w1, w2):
            xt = jnp.transpose(x, (0, 3, 1, 2))
            B, I, M, N = xt.shape
            nm = w1.shape[2]
            cw1 = w1[..., 0] + 1j * w1[..., 1]
            cw2 = w2[..., 0] + 1j * w2[..., 1]
            O = cw1.shape[1]
            fty = jnp.fft.rfft(xt, axis=-1, norm='ortho')
            f1 = jnp.einsum('bixy,ioy->boxy', fty[..., :nm], cw1)
            pad_y = jnp.zeros((B, O, M, N // 2 + 1 - nm), dtype=f1.dtype)
            xy = jnp.fft.irfft(jnp.concatenate([f1, pad_y], axis=-1), n=N, axis=-1, norm='ortho')
            ftx = jnp.fft.rfft(xt, axis=-2, norm='ortho')
            f2 = jnp.einsum('bixy,iox->boxy', ftx[:, :, :nm, :], cw2)
            pad_x = jnp.zeros((B, O, M // 2 + 1 - nm, N), dtype=f2.dtype)
            xx = jnp.fft.irfft(jnp.concatenate([f2, pad_x], axis=-2), n=M, axis=-2, norm='ortho')
            return jnp.transpose(xx + xy, (0, 2, 3, 1))
        key = jax.random.key(seed)
        ks = jax.random.split(key, 6)
        B, M, N, D = (16, 128, 128, 128)
        NM, H = (16, 512)
        xav = float(np.sqrt(2.0 / (D + D)))
        return {'x': jax.random.normal(ks[0], (B, M, N, D), jnp.float32), 'w1': jax.random.normal(ks[1], (D, D, NM, 2), jnp.float32) * xav, 'w2': jax.random.normal(ks[2], (D, D, NM, 2), jnp.float32) * xav, 'ff_w0': jax.random.normal(ks[3], (D, H), jnp.float32) * float(1.0 / np.sqrt(D)), 'ff_b0': jnp.zeros((H,), jnp.float32), 'ff_w1': jax.random.normal(ks[4], (H, D), jnp.float32) * float(1.0 / np.sqrt(H)), 'ff_b1': jnp.zeros((D,), jnp.float32), 'ln_g': jnp.ones((D,), jnp.float32), 'ln_b': jnp.zeros((D,), jnp.float32)}
    _L1_conv_all = _L1_conv_setup()
    _L1_conv_in = {k: v for k, v in _L1_conv_all.items() if k in ('w1', 'w2', 'ff_w0', 'ff_b0', 'ff_w1', 'ff_b1', 'ln_g', 'ln_b', )}
    del _L1_conv_all

    def _L2_conv_setup():
        import jax, jax.numpy as jnp
        import numpy as np
        B, H, W, C, K, T = (16, 128, 128, 64, 7, 16)
        C2 = 2 * C

        def _pad_and_fft(kr, ki, h, w, k):
            kern = kr + 1j * ki
            ph = (h - k) // 2
            pw = (w - k) // 2
            padded = jnp.pad(kern, ((0, 0), (ph, h - k - ph), (pw, w - k - pw)))
            return jnp.fft.fft2(padded, axes=(-2, -1))
        key = jax.random.key(seed)
        ks = jax.random.split(key, 12)
        d = {'x_ri': jax.random.normal(ks[0], (B, H, W, C2), jnp.float32), 'Wf': jax.random.normal(ks[1], (C2, C2), jnp.float32) * 0.05, 'bf': jnp.zeros((C2,), jnp.float32), 'Wi': jax.random.normal(ks[2], (C2, C2), jnp.float32) * 0.05, 'bi': jnp.zeros((C2,), jnp.float32), 'Wd': jax.random.normal(ks[3], (C2, C2), jnp.float32) * 0.05, 'bd': jnp.zeros((C2,), jnp.float32), 'A_real': jax.random.normal(ks[4], (C, K, K), jnp.float32) * 0.02, 'A_imag': jax.random.normal(ks[5], (C, K, K), jnp.float32) * 0.02, 'B_real': jax.random.normal(ks[6], (C, K, K), jnp.float32) * 0.02, 'B_imag': jax.random.normal(ks[7], (C, K, K), jnp.float32) * 0.02}
        return d
    _L2_conv_all = _L2_conv_setup()
    _L2_conv_in = {k: v for k, v in _L2_conv_all.items() if k in ('Wf', 'bf', 'Wi', 'bi', 'Wd', 'bd', 'A_real', 'A_imag', 'B_real', 'B_imag', )}
    del _L2_conv_all

    def _L3_conv_setup():
        import jax, jax.numpy as jnp
        import numpy as np
        import math
        D_MODEL = 128
        D_STATE = 16
        D_CONV = 3
        EXPAND = 2
        D_INNER = EXPAND * D_MODEL
        DT_RANK = math.ceil(D_MODEL / 16)
        B, H, W = (2, 64, 64)
        LN_EPS = 1e-05

        def _local_scan(x, Hh, Ww, w_h, w_w, flip=False, column_first=False):
            Bb, C = (x.shape[0], x.shape[1])
            Hg, Wg = (Hh // w_h, Ww // w_w)
            x = x.reshape(Bb, C, Hg, w_h, Wg, w_w)
            if column_first:
                x = x.transpose(0, 1, 4, 2, 5, 3)
            else:
                x = x.transpose(0, 1, 2, 4, 3, 5)
            x = x.reshape(Bb, C, -1)
            if flip:
                x = x[:, :, ::-1]
            return x

        def _selective_scan(u, delta, A, Bm, Cm, D, delta_bias):
            Bsz, Dch, L = u.shape
            K, N = (Bm.shape[1], A.shape[1])
            d = Dch // K
            delta = jax.nn.softplus(delta + delta_bias[None, :, None])
            A4 = A.reshape(K, d, N)
            u4 = u.reshape(Bsz, K, d, L)
            dt4 = delta.reshape(Bsz, K, d, L)

            def step(h, inp):
                ut, dt, bt, ct = inp
                dA = jnp.exp(dt[..., None] * A4)
                h = dA * h + (dt * ut)[..., None] * bt[:, :, None, :]
                y = jnp.einsum('bkdn,bkn->bkd', h, ct)
                return (h, y)
            xs_t = (u4.transpose(3, 0, 1, 2), dt4.transpose(3, 0, 1, 2), Bm.transpose(3, 0, 1, 2), Cm.transpose(3, 0, 1, 2))
            h0 = jnp.zeros((Bsz, K, d, N), u.dtype)
            _, ys = jax.lax.scan(step, h0, xs_t)
            y = ys.transpose(1, 2, 3, 0).reshape(Bsz, Dch, L)
            return y + u * D[None, :, None]
        key = jax.random.key(seed)
        ks = jax.random.split(key, 8)
        x = jax.random.normal(ks[0], (B, H, W, D_MODEL), jnp.float32)
        W_in = jax.random.normal(ks[1], (2 * D_INNER, D_MODEL), jnp.float32) * D_MODEL ** (-0.5)
        conv_w = jax.random.normal(ks[2], (D_INNER, 1, D_CONV, D_CONV), jnp.float32) * (1.0 / D_CONV)
        conv_b = jnp.zeros((D_INNER,), jnp.float32)
        x_proj_w = jax.random.normal(ks[3], (4, DT_RANK + 2 * D_STATE, D_INNER), jnp.float32) * D_INNER ** (-0.5)
        std = DT_RANK ** (-0.5)
        dt_proj_w = jax.random.uniform(ks[4], (4, D_INNER, DT_RANK), jnp.float32, -std, std)
        dt = jnp.exp(jax.random.uniform(ks[5], (4, D_INNER), jnp.float32) * (math.log(0.1) - math.log(0.001)) + math.log(0.001))
        dt = jnp.maximum(dt, 0.0001)
        dt_proj_b = dt + jnp.log(-jnp.expm1(-dt))
        A_logs = jnp.log(jnp.tile(jnp.arange(1, D_STATE + 1, dtype=jnp.float32)[None, :], (4 * D_INNER, 1)))
        Ds = jnp.ones((4 * D_INNER,), jnp.float32)
        ln_w = jnp.ones((D_INNER,), jnp.float32)
        ln_b = jnp.zeros((D_INNER,), jnp.float32)
        W_out = jax.random.normal(ks[6], (D_MODEL, D_INNER), jnp.float32) * D_INNER ** (-0.5)
        return dict(x=x, W_in=W_in, conv_w=conv_w, conv_b=conv_b, x_proj_w=x_proj_w, dt_proj_w=dt_proj_w, dt_proj_b=dt_proj_b, A_logs=A_logs, Ds=Ds, ln_w=ln_w, ln_b=ln_b, W_out=W_out)
    _L3_conv_all = _L3_conv_setup()
    _L3_conv_in = {k: v for k, v in _L3_conv_all.items() if k in ('W_in', 'conv_w', 'conv_b', 'x_proj_w', 'dt_proj_w', 'dt_proj_b', 'A_logs', 'Ds', 'ln_w', 'ln_b', 'W_out', )}
    del _L3_conv_all

    return {
        "x": x,
        "L0_conv_Wq": _L0_conv_in["Wq"],
        "L0_conv_bq": _L0_conv_in["bq"],
        "L0_conv_Wk": _L0_conv_in["Wk"],
        "L0_conv_bk": _L0_conv_in["bk"],
        "L0_conv_Wv": _L0_conv_in["Wv"],
        "L0_conv_bv": _L0_conv_in["bv"],
        "L0_conv_Wp": _L0_conv_in["Wp"],
        "L0_conv_bp": _L0_conv_in["bp"],
        "L0_conv_bias_table": _L0_conv_in["bias_table"],
        "L1_conv_w1": _L1_conv_in["w1"],
        "L1_conv_w2": _L1_conv_in["w2"],
        "L1_conv_ff_w0": _L1_conv_in["ff_w0"],
        "L1_conv_ff_b0": _L1_conv_in["ff_b0"],
        "L1_conv_ff_w1": _L1_conv_in["ff_w1"],
        "L1_conv_ff_b1": _L1_conv_in["ff_b1"],
        "L1_conv_ln_g": _L1_conv_in["ln_g"],
        "L1_conv_ln_b": _L1_conv_in["ln_b"],
        "L2_conv_Wf": _L2_conv_in["Wf"],
        "L2_conv_bf": _L2_conv_in["bf"],
        "L2_conv_Wi": _L2_conv_in["Wi"],
        "L2_conv_bi": _L2_conv_in["bi"],
        "L2_conv_Wd": _L2_conv_in["Wd"],
        "L2_conv_bd": _L2_conv_in["bd"],
        "L2_conv_A_real": _L2_conv_in["A_real"],
        "L2_conv_A_imag": _L2_conv_in["A_imag"],
        "L2_conv_B_real": _L2_conv_in["B_real"],
        "L2_conv_B_imag": _L2_conv_in["B_imag"],
        "L3_conv_W_in": _L3_conv_in["W_in"],
        "L3_conv_conv_w": _L3_conv_in["conv_w"],
        "L3_conv_conv_b": _L3_conv_in["conv_b"],
        "L3_conv_x_proj_w": _L3_conv_in["x_proj_w"],
        "L3_conv_dt_proj_w": _L3_conv_in["dt_proj_w"],
        "L3_conv_dt_proj_b": _L3_conv_in["dt_proj_b"],
        "L3_conv_A_logs": _L3_conv_in["A_logs"],
        "L3_conv_Ds": _L3_conv_in["Ds"],
        "L3_conv_ln_w": _L3_conv_in["ln_w"],
        "L3_conv_ln_b": _L3_conv_in["ln_b"],
        "L3_conv_W_out": _L3_conv_in["W_out"],
    }

def reference(x, L0_conv_Wq, L0_conv_bq, L0_conv_Wk, L0_conv_bk, L0_conv_Wv, L0_conv_bv, L0_conv_Wp, L0_conv_bp, L0_conv_bias_table, L1_conv_w1, L1_conv_w2, L1_conv_ff_w0, L1_conv_ff_b0, L1_conv_ff_w1, L1_conv_ff_b1, L1_conv_ln_g, L1_conv_ln_b, L2_conv_Wf, L2_conv_bf, L2_conv_Wi, L2_conv_bi, L2_conv_Wd, L2_conv_bd, L2_conv_A_real, L2_conv_A_imag, L2_conv_B_real, L2_conv_B_imag, L3_conv_W_in, L3_conv_conv_w, L3_conv_conv_b, L3_conv_x_proj_w, L3_conv_dt_proj_w, L3_conv_dt_proj_b, L3_conv_A_logs, L3_conv_Ds, L3_conv_ln_w, L3_conv_ln_b, L3_conv_W_out):
    import jax
    import jax.numpy as jnp
    def _L0_conv_ref(x, Wq, bq, Wk, bk, Wv, bv, Wp, bp, bias_table, shift_size):
        import jax, jax.numpy as jnp
        import numpy as np
        WS = 16
        HS = 8
        NH = 4
        DIM = 128
        WSH = WS + 2 * HS
        B, H, W = (2, 128, 128)

        def _rel_pos_index():
            r = np.arange(-HS, WS + HS)
            coords = np.stack(np.meshgrid(r, r, indexing='ij'))
            cf = coords.reshape(2, -1)
            rel = (cf[:, :, None] - cf[:, None, :]).transpose(1, 2, 0)
            rel = rel.copy()
            rel[..., 0] += WS + HS - 1
            rel[..., 1] += WS + HS - 1
            rel[..., 0] *= 2 * WS + 2 * HS - 1
            return rel.sum(-1)
        _RPI = _rel_pos_index()
        Bx, Hx, Wx, C = x.shape
        hd = C // NH
        scale = hd ** (-0.5)
        if shift_size > 0:
            x = jnp.roll(x, (-shift_size, -shift_size), axis=(1, 2))
        xp = jnp.pad(x, ((0, 0), (HS, HS), (HS, HS), (0, 0)), mode='reflect')
        nWh, nWw = (Hx // WS, Wx // WS)
        rows = (jnp.arange(nWh) * WS)[:, None] + jnp.arange(WSH)
        cols = (jnp.arange(nWw) * WS)[:, None] + jnp.arange(WSH)
        w = xp[:, rows]
        w = w[:, :, :, cols]
        w = w.transpose(0, 1, 3, 2, 4, 5).reshape(-1, WSH, WSH, C)
        center = w[:, HS:HS + WS, HS:HS + WS].reshape(-1, WS * WS, C)
        kv = w.reshape(-1, WSH * WSH, C)
        q = (center @ Wq.T + bq).reshape(-1, WS * WS, NH, hd).transpose(0, 2, 1, 3)
        k = (kv @ Wk.T + bk).reshape(-1, WSH * WSH, NH, hd).transpose(0, 2, 1, 3)
        v = (kv @ Wv.T + bv).reshape(-1, WSH * WSH, NH, hd).transpose(0, 2, 1, 3)
        attn = jnp.einsum('bhqd,bhkd->bhqk', q, k) * scale
        bias = bias_table[_RPI.reshape(-1)].reshape(WSH * WSH, WSH * WSH, NH)
        bias = bias.transpose(2, 0, 1)
        start = HS * 2 * WS
        attn = attn + bias[:, start:start + WS * WS, :][None]
        attn = jax.nn.softmax(attn, axis=-1)
        out = jnp.einsum('bhqk,bhkd->bhqd', attn, v)
        out = out.transpose(0, 2, 1, 3).reshape(-1, WS * WS, C)
        out = out @ Wp.T + bp
        out = out.reshape(Bx, nWh, nWw, WS, WS, C).transpose(0, 1, 3, 2, 4, 5)
        out = out.reshape(Bx, Hx, Wx, C)
        if shift_size > 0:
            out = jnp.roll(out, (shift_size, shift_size), axis=(1, 2))
        return out

    def _L1_conv_ref(x, w1, w2, ff_w0, ff_b0, ff_w1, ff_b1, ln_g, ln_b):
        import jax, jax.numpy as jnp
        import numpy as np
        LN_EPS = 1e-05

        def _layer_norm(h, g, b):
            mu = jnp.mean(h, axis=-1, keepdims=True)
            var = jnp.mean(jnp.square(h - mu), axis=-1, keepdims=True)
            return (h - mu) * jax.lax.rsqrt(var + LN_EPS) * g + b

        def _forward_fourier(x, w1, w2):
            xt = jnp.transpose(x, (0, 3, 1, 2))
            B, I, M, N = xt.shape
            nm = w1.shape[2]
            cw1 = w1[..., 0] + 1j * w1[..., 1]
            cw2 = w2[..., 0] + 1j * w2[..., 1]
            O = cw1.shape[1]
            fty = jnp.fft.rfft(xt, axis=-1, norm='ortho')
            f1 = jnp.einsum('bixy,ioy->boxy', fty[..., :nm], cw1)
            pad_y = jnp.zeros((B, O, M, N // 2 + 1 - nm), dtype=f1.dtype)
            xy = jnp.fft.irfft(jnp.concatenate([f1, pad_y], axis=-1), n=N, axis=-1, norm='ortho')
            ftx = jnp.fft.rfft(xt, axis=-2, norm='ortho')
            f2 = jnp.einsum('bixy,iox->boxy', ftx[:, :, :nm, :], cw2)
            pad_x = jnp.zeros((B, O, M // 2 + 1 - nm, N), dtype=f2.dtype)
            xx = jnp.fft.irfft(jnp.concatenate([f2, pad_x], axis=-2), n=M, axis=-2, norm='ortho')
            return jnp.transpose(xx + xy, (0, 2, 3, 1))
        h = _forward_fourier(x, w1, w2)
        h1 = jax.nn.relu(jnp.einsum('bmni,ih->bmnh', h, ff_w0) + ff_b0)
        h2 = jnp.einsum('bmnh,ho->bmno', h1, ff_w1) + ff_b1
        return _layer_norm(h2, ln_g, ln_b)

    def _L2_conv_ref(x_ri, Wf, bf, Wi, bi, Wd, bd, A_real, A_imag, B_real, B_imag):
        import jax, jax.numpy as jnp
        import numpy as np
        B, H, W, C, K, T = (16, 128, 128, 64, 7, 16)
        C2 = 2 * C

        def _pad_and_fft(kr, ki, h, w, k):
            kern = kr + 1j * ki
            ph = (h - k) // 2
            pw = (w - k) // 2
            padded = jnp.pad(kern, ((0, 0), (ph, h - k - ph), (pw, w - k - pw)))
            return jnp.fft.fft2(padded, axes=(-2, -1))
        b, h, w, c2 = x_ri.shape
        c = c2 // 2
        k = A_real.shape[-1]
        forget_gate = jax.nn.sigmoid(x_ri @ Wf + bf + 2.0)
        input_gate = jax.nn.sigmoid(x_ri @ Wi + bi)
        delta = jax.nn.softplus(x_ri @ Wd + bd) * 0.1
        A_f = _pad_and_fft(A_real, A_imag, h, w, k)
        B_f = _pad_and_fft(B_real, B_imag, h, w, k)
        A_ri = jnp.concatenate([A_f.real, A_f.imag], 0).transpose(1, 2, 0)[None]
        B_ri = jnp.concatenate([B_f.real, B_f.imag], 0).transpose(1, 2, 0)[None]
        Ar, Ai = (A_ri[..., :c], A_ri[..., c:])
        mag = jnp.sqrt(Ar ** 2 + Ai ** 2 + 1e-08)
        scale = 0.95 * jax.nn.sigmoid(mag) / (mag + 1e-08)
        Ar = Ar * scale
        Ai = Ai * scale
        Br, Bi_ = (B_ri[..., :c], B_ri[..., c:])
        x_r, x_i = (x_ri[..., :c], x_ri[..., c:])
        Bx_r = Br * x_r - Bi_ * x_i
        Bx_i = Br * x_i + Bi_ * x_r
        inp_r = delta[..., :c] * input_gate[..., :c] * Bx_r
        inp_i = delta[..., c:] * input_gate[..., c:] * Bx_i
        fg_r, fg_i = (forget_gate[..., :c], forget_gate[..., c:])

        def step(h_state, _):
            h_r, h_i = h_state
            Ah_r = Ar * h_r - Ai * h_i
            Ah_i = Ar * h_i + Ai * h_r
            return ((fg_r * Ah_r + inp_r, fg_i * Ah_i + inp_i), None)
        h0 = (jnp.zeros_like(x_r), jnp.zeros_like(x_i))
        (h_r, h_i), _ = jax.lax.scan(step, h0, None, length=T)
        return jnp.concatenate([h_r, h_i], axis=-1)

    def _L3_conv_ref(x, W_in, conv_w, conv_b, x_proj_w, dt_proj_w, dt_proj_b, A_logs, Ds, ln_w, ln_b, W_out):
        import jax, jax.numpy as jnp
        import numpy as np
        import math
        D_MODEL = 128
        D_STATE = 16
        D_CONV = 3
        EXPAND = 2
        D_INNER = EXPAND * D_MODEL
        DT_RANK = math.ceil(D_MODEL / 16)
        B, H, W = (2, 64, 64)
        LN_EPS = 1e-05

        def _local_scan(x, Hh, Ww, w_h, w_w, flip=False, column_first=False):
            Bb, C = (x.shape[0], x.shape[1])
            Hg, Wg = (Hh // w_h, Ww // w_w)
            x = x.reshape(Bb, C, Hg, w_h, Wg, w_w)
            if column_first:
                x = x.transpose(0, 1, 4, 2, 5, 3)
            else:
                x = x.transpose(0, 1, 2, 4, 3, 5)
            x = x.reshape(Bb, C, -1)
            if flip:
                x = x[:, :, ::-1]
            return x

        def _selective_scan(u, delta, A, Bm, Cm, D, delta_bias):
            Bsz, Dch, L = u.shape
            K, N = (Bm.shape[1], A.shape[1])
            d = Dch // K
            delta = jax.nn.softplus(delta + delta_bias[None, :, None])
            A4 = A.reshape(K, d, N)
            u4 = u.reshape(Bsz, K, d, L)
            dt4 = delta.reshape(Bsz, K, d, L)

            def step(h, inp):
                ut, dt, bt, ct = inp
                dA = jnp.exp(dt[..., None] * A4)
                h = dA * h + (dt * ut)[..., None] * bt[:, :, None, :]
                y = jnp.einsum('bkdn,bkn->bkd', h, ct)
                return (h, y)
            xs_t = (u4.transpose(3, 0, 1, 2), dt4.transpose(3, 0, 1, 2), Bm.transpose(3, 0, 1, 2), Cm.transpose(3, 0, 1, 2))
            h0 = jnp.zeros((Bsz, K, d, N), u.dtype)
            _, ys = jax.lax.scan(step, h0, xs_t)
            y = ys.transpose(1, 2, 3, 0).reshape(Bsz, Dch, L)
            return y + u * D[None, :, None]
        Bb, Hh, Ww, _ = x.shape
        L = Hh * Ww
        d_inner = conv_b.shape[0]
        dt_rank = dt_proj_w.shape[2]
        N = A_logs.shape[1]
        xz = x @ W_in.T
        xc, z = jnp.split(xz, 2, axis=-1)
        xc = xc.transpose(0, 3, 1, 2)
        xc = jax.lax.conv_general_dilated(xc, conv_w, (1, 1), ((1, 1), (1, 1)), dimension_numbers=('NCHW', 'OIHW', 'NCHW'), feature_group_count=d_inner) + conv_b[None, :, None, None]
        xc = jax.nn.silu(xc)
        w_h, w_w = (Hh // 4, Ww // 4)
        x1 = _local_scan(xc, Hh, Ww, w_h, w_w)
        x2 = _local_scan(xc, Hh, Ww, w_h, w_w, column_first=True)
        x3 = _local_scan(xc, Hh, Ww, w_h, w_w, flip=True)
        x4 = _local_scan(xc, Hh, Ww, w_h, w_w, column_first=True, flip=True)
        xs = jnp.stack([x1, x2, x3, x4], axis=1)
        x_dbl = jnp.einsum('bkdl,kcd->bkcl', xs, x_proj_w)
        dts, Bs, Cs = jnp.split(x_dbl, [dt_rank, dt_rank + N], axis=2)
        dts = jnp.einsum('bkrl,kdr->bkdl', dts, dt_proj_w)
        u = xs.reshape(Bb, -1, L)
        delta = dts.reshape(Bb, -1, L)
        As = -jnp.exp(A_logs)
        out_y = _selective_scan(u, delta, As, Bs, Cs, Ds, dt_proj_b.reshape(-1)).reshape(Bb, 4, -1, L)
        inv_y = out_y[:, 2:4, :, ::-1]
        wh_y = out_y[:, 1].reshape(Bb, -1, Ww, Hh).transpose(0, 1, 3, 2).reshape(Bb, -1, L)
        invwh_y = inv_y[:, 1].reshape(Bb, -1, Ww, Hh).transpose(0, 1, 3, 2).reshape(Bb, -1, L)
        y = out_y[:, 0] + inv_y[:, 0] + wh_y + invwh_y
        y = y.transpose(0, 2, 1).reshape(Bb, Hh, Ww, -1)
        mu = jnp.mean(y, axis=-1, keepdims=True)
        var = jnp.mean(jnp.square(y - mu), axis=-1, keepdims=True)
        y = (y - mu) * jax.lax.rsqrt(var + LN_EPS) * ln_w + ln_b
        y = y * jax.nn.silu(z)
        return y @ W_out.T

    def _gn(v, G=32, eps=1e-5):
        B_, H_, W_, C_ = v.shape
        g = v.reshape(B_, H_, W_, G, C_ // G)
        m = jnp.mean(g, axis=(1, 2, 4), keepdims=True)
        s = jnp.var(g, axis=(1, 2, 4), keepdims=True)
        return ((g - m) / jnp.sqrt(s + eps)).reshape(v.shape)

    def _ln_c(v, eps=1e-6):
        m = jnp.mean(v, axis=-1, keepdims=True)
        s = jnp.var(v, axis=-1, keepdims=True)
        return (v - m) / jnp.sqrt(s + eps)

    def _ln_t(v, eps=1e-5):
        m = jnp.mean(v, axis=-1, keepdims=True)
        s = jnp.var(v, axis=-1, keepdims=True)
        return (v - m) / jnp.sqrt(s + eps)

    def _to_tokens(v):
        B_, H_, W_, C_ = v.shape
        return v.reshape(B_, H_ * W_, C_)
    def _from_tokens(t, like):
        return t.reshape(like.shape)

    x = x + _L0_conv_ref(_gn(x), L0_conv_Wq, L0_conv_bq, L0_conv_Wk, L0_conv_bk, L0_conv_Wv, L0_conv_bv, L0_conv_Wp, L0_conv_bp, L0_conv_bias_table, 0)
    x = x + _L1_conv_ref(_gn(x), L1_conv_w1, L1_conv_w2, L1_conv_ff_w0, L1_conv_ff_b0, L1_conv_ff_w1, L1_conv_ff_b1, L1_conv_ln_g, L1_conv_ln_b)
    x = x + _L2_conv_ref(_gn(x), L2_conv_Wf, L2_conv_bf, L2_conv_Wi, L2_conv_bi, L2_conv_Wd, L2_conv_bd, L2_conv_A_real, L2_conv_A_imag, L2_conv_B_real, L2_conv_B_imag)
    x = x + _L3_conv_ref(_gn(x), L3_conv_W_in, L3_conv_conv_w, L3_conv_conv_b, L3_conv_x_proj_w, L3_conv_dt_proj_w, L3_conv_dt_proj_b, L3_conv_A_logs, L3_conv_Ds, L3_conv_ln_w, L3_conv_ln_b, L3_conv_W_out)
    return x


_drawn_inputs = setup_inputs


def setup_inputs(seed=0):
    import zlib

    import numpy as np

    out = dict(_drawn_inputs(seed))
    spreads = {'L0_conv_bq': (0.0, 0.8),
     'L0_conv_bk': (0.0, 2.0),
     'L0_conv_bv': (0.0, 0.273),
     'L0_conv_bp': (0.0, 0.1),
     'L1_conv_ff_b0': (0.0, 0.1),
     'L1_conv_ff_b1': (0.0, 0.1),
     'L1_conv_ln_g': (1.0, 0.2),
     'L1_conv_ln_b': (0.0, 0.1),
     'L2_conv_bf': (0.0, 0.8),
     'L2_conv_bi': (0.0, 0.8),
     'L2_conv_bd': (0.0, 0.8),
     'L3_conv_conv_b': (0.0, 0.1),
     'L3_conv_Ds': (1.0, 0.2),
     'L3_conv_ln_w': (1.0, 0.2),
     'L3_conv_ln_b': (0.0, 0.1)}
    factors = {'L0_conv_Wq': 8.0,
     'L0_conv_Wk': 8.0,
     'L0_conv_Wv': 8.0,
     'L0_conv_bias_table': 23.779,
     'L2_conv_Wf': 8.0,
     'L2_conv_Wi': 8.0,
     'L2_conv_Wd': 8.0,
     'L2_conv_A_real': 8.0,
     'L2_conv_A_imag': 8.0,
     'L2_conv_B_real': 8.0,
     'L2_conv_B_imag': 8.0,
     'L3_conv_dt_proj_w': 7.632,
     'L3_conv_dt_proj_b': 3.463,
     'L3_conv_A_logs': 2.723}
    for name, (base, spread) in spreads.items():
        noise = np.random.default_rng([zlib.crc32(name.encode()), seed]).standard_normal(out[name].shape)
        drawn = base * np.exp(spread * noise) if base else spread * noise
        out[name] = jnp.asarray(drawn.astype(out[name].dtype))
    for name, factor in factors.items():
        out[name] = (out[name] * factor).astype(out[name].dtype)
    return out
```

```python
from contextlib import ExitStack

import numpy as np
import concourse.bass as bass
from concourse import mybir

F32 = mybir.dt.float32
BF16 = mybir.dt.bfloat16
ALU = mybir.AluOpType
ACT = mybir.ActivationFunctionType
AXX = mybir.AxisListType.X

B, HW, C = 2, 128, 128
L = HW * HW
EPS = 1e-5


class Lane:

    def __init__(self, sem):
        self.sem, self.items, self.first = sem, [], []
        self.linked = False

    def do(self, fn, *args, after=(), **kw):
        if self.linked and self.items:
            after = [*after, (self, len(self.items) - 1)]
        self.items.append([fn, args, kw, [*self.first, *after], False])
        self.first = []
        return (self, len(self.items) - 1)

    def number(self):
        self.count, n = [], 0
        for it in self.items:
            n += it[4]
            self.count.append(n)

    def play(self, eng):
        seen = {}
        for fn, args, kw, after, marked in self.items:
            need = {}
            for src, at in after:
                v = src.count[at] if isinstance(src, Lane) else at
                if v > need.get(src, 0):
                    need[src] = v
            for src, v in need.items():
                if v > seen.get(src, 0):
                    eng.wait_ge(src.sem, v)
                    seen[src] = v
            if fn is None:
                continue
            ins = fn(*args, **kw)
            if marked:
                ins.then_inc(self.sem, 1)


class Chan:

    def __init__(self, sem):
        self.sem, self.n = sem, 0


class Ring:

    def __init__(self, bufs):
        self.bufs, self.n = bufs, 0
        self.held = [[] for _ in bufs]

    def take(self):
        i = self.n % len(self.bufs)
        self.n += 1
        w, self.held[i] = self.held[i], []
        return i, self.bufs[i], w


class Core:
    def __init__(self, nc, ctx):
        self.nc, self.ctx = nc, ctx
        self.lanes = {}
        for n in ("pe", "act", "dve", "pool", "sp"):
            self.lanes[n] = Lane(ctx.enter_context(nc.semaphore(f"s_{n}")))
        self.chans = []
        self.words = 51600
        self.mem = ctx.enter_context(nc.sbuf_tensor("mem", [128, self.words], F32))
        self.ps = ctx.enter_context(nc.psum_tensor("ps", [128, 8, 512], F32))
        self.low = self.top = 0
        self.nchan = 0

    def chan(self):
        self.nchan += 1
        c = Chan(self.ctx.enter_context(self.nc.semaphore(f"d{self.nchan}")))
        self.chans.append(c)
        return c

    def buf(self, *shape, dt=F32, parts=128):
        n = int(np.prod(shape))
        words = n if dt == F32 else (n + 1) // 2
        assert self.top + words <= self.words, (self.top, words)
        a = self.mem[0:parts, self.top:self.top + words]
        self.top += words
        if dt != F32:
            a = a.bitcast(dt)
        if len(shape) == 2:
            a = a.rearrange("p (a b) -> p a b", a=shape[0])
        elif len(shape) == 3:
            a = a.rearrange("p (a b c) -> p a b c", a=shape[0], b=shape[1])
        return a

    def dma(self, chan, out, in_, after=(), lane="sp"):
        ln = self.lanes[lane]
        eng = {"sp": self.nc.sync, "pool": self.nc.gpsimd, "act": self.nc.scalar}[lane]
        chan.n += 16
        ln.do(lambda o=out, i=in_, s=chan.sem, e=eng: e.dma_start(o, i).then_inc(s, 16), after=after)
        return (chan, chan.n)

    def phase(self):
        ends = [(ln, len(ln.items) - 1) for ln in self.lanes.values()
                if ln.items and ln is not self.lanes["sp"]]
        ends += [(c, c.n) for c in self.chans if c.n]
        for ln in self.lanes.values():
            ln.first = list(ends)
        self.top = self.low

    def play(self):
        for ln in self.lanes.values():
            for it in ln.items:
                for src, at in it[3]:
                    if isinstance(src, Lane):
                        src.items[at][4] = True
        ends = [(c, c.n) for c in self.chans if c.n]
        self.lanes["sp"].do(None, after=ends)
        for ln in self.lanes.values():
            ln.number()
        with self.nc.Block() as block:
            @block.tensor
            def _(e):
                self.lanes["pe"].play(e)

            @block.scalar
            def _(e):
                self.lanes["act"].play(e)

            @block.vector
            def _(e):
                self.lanes["dve"].play(e)

            @block.gpsimd
            def _(e):
                self.lanes["pool"].play(e)

            @block.sync
            def _(e):
                self.lanes["sp"].play(e)


def norm_params(k, d, stats, ready, aggregate=True):
    nc, V, S, T = k.nc, k.lanes["dve"], k.lanes["act"], k.lanes["pe"]
    mv, sm = d["mv"], d["sm"]
    t = ready[0]
    for b in range(B) if aggregate else ():
        t = V.do(nc.vector.bn_aggr, mv[:, b, :], stats[:, b, :], after=ready)
    p = k.ps[:, 0, 0:2]
    t = T.do(nc.tensor.matmul, p, d["grp"], mv[:, :, 0], start=True, stop=True, after=[t, d["t_const"]])
    t = V.do(nc.vector.tensor_copy, sm[:, 0:2], p, after=[t])
    t = V.do(nc.vector.tensor_tensor, sm[:, 2:4], mv[:, :, 0], sm[:, 0:2], ALU.subtract, after=[t])
    t = V.do(nc.vector.tensor_tensor, sm[:, 4:6], sm[:, 2:4], sm[:, 2:4], ALU.mult, after=[t])
    t = V.do(nc.vector.tensor_tensor, sm[:, 6:8], sm[:, 4:6], mv[:, :, 1], ALU.add, after=[t])
    t = T.do(nc.tensor.matmul, p, d["grp"], sm[:, 6:8], start=True, stop=True, after=[t])
    t = V.do(nc.vector.tensor_scalar, sm[:, 2:4], p, EPS, None, ALU.add, after=[t])
    t = S.do(nc.scalar.activation, sm[:, 4:6], sm[:, 2:4], ACT.Sqrt, after=[t])
    t = V.do(nc.vector.reciprocal, d["rs"], sm[:, 4:6], after=[t])
    t = V.do(nc.vector.scalar_tensor_tensor, out=d["nb"], in0=sm[:, 0:2], scalar=-1.0, in1=d["rs"],
             op0=ALU.mult, op1=ALU.mult, after=[t])
    return t


def first_stats(k, d, xin):
    nc, V = k.nc, k.lanes["dve"]
    ring = Ring([k.buf(4096) for _ in range(4)])
    ch = [k.chan() for _ in range(4)]
    t = None
    for b in range(B):
        for n in range(4):
            i, x, w = ring.take()
            ld = k.dma(ch[i], x, xin[:, b, n * 4096:(n + 1) * 4096], after=w)
            for j in range(8):
                t = V.do(nc.vector.bn_stats, d["stats"][:, b, (n * 8 + j) * 6:(n * 8 + j) * 6 + 6],
                         x[:, j * 512:(j + 1) * 512], after=[ld])
            ring.held[i] = [t]
    return t


def layer0(k, d, I, xin, xout):
    nc = k.nc
    V, S, T = k.lanes["dve"], k.lanes["act"], k.lanes["pe"]
    ps = k.ps
    c0 = k.chan()
    wq, wk, wv, wp = [k.buf(128) for _ in range(4)]
    rel = k.buf(2, 4, 1024)
    for t_, n in ((wq, "wq"), (wk, "wk"), (wv, "wv"), (wp, "wp")):
        k.dma(c0, t_, I[n])
    bv4 = k.buf(5)
    tw = k.dma(c0, bv4[:, 0:4], I["b0"])
    tb = k.dma(k.chan(), rel, I["rel"].rearrange("p (a b c) -> p a b c", a=2, b=4))
    tq = S.do(nc.scalar.mul, bv4[:, 4:5], bv4[:, 0:1], 32 ** -0.5, after=[tw])
    scale = 32 ** -0.5
    stats = d["stats2"]

    NO = 6
    raw = [k.buf(8, 128) for _ in range(NO)]
    Kb = [k.buf(9 * 128) for _ in range(NO)]
    Vb = [k.buf(9, 128) for _ in range(NO)]
    Qb = [k.buf(8, 128) for _ in range(NO)]
    xnr = Ring([k.buf(9, 8, 16) for _ in range(2)])
    chr_ = [k.chan() for _ in range(NO)]
    held = [[] for _ in range(NO)]
    Tr = Ring([k.buf(1024) for _ in range(2)])
    Pr = Ring([k.buf(1024) for _ in range(3)])
    PTr = Ring([k.buf(1024) for _ in range(2)])
    mx = k.buf(4, 4)
    outr = Ring([k.buf(16, 128) for _ in range(2)])
    cho = [k.chan() for _ in range(2)]
    Osb = Ring([k.buf(128) for _ in range(2)])
    OT = Ring([k.buf(256) for _ in range(2)])
    rsum = Ring([k.buf(4) for _ in range(4)])
    rinv = Ring([k.buf(4) for _ in range(4)])
    Sp = Ring([ps[:, 0:2, :].rearrange("p a b -> p (a b)"), ps[:, 2:4, :].rearrange("p a b -> p (a b)")])
    PTp = Ring([ps[:, 4:6, :].rearrange("p a b -> p (a b)")])
    misc = Ring([ps[:, 6, :], ps[:, 7, :]])
    octs = {}
    loads = {}

    def load_oct(b, o):
        i = (b * 18 + o) % NO
        r0 = 1 if o == 0 else 119 if o == 17 else 8 * o - 8
        w, held[i] = held[i], []
        loads[b, o] = k.dma(chr_[i], raw[i].rearrange("p a b -> p (a b)"),
                            xin[:, b, r0 * 128:(r0 + 8) * 128], after=w)

    def make_oct(b, o):
        i = (b * 18 + o) % NO
        ld = loads.pop((b, o))
        j, xn, w = xnr.take()
        src = raw[i][:, ::-1, :] if o in (0, 17) else raw[i]
        cen = src.rearrange("p r (a c) -> p r a c", c=8)
        x4 = xn.rearrange("p cb r (h c) -> p r cb h c", h=2)
        rs, nb = d["rs"][:, b:b + 1], d["nb"][:, b:b + 1]
        ts = []
        for r in range(2):
            dst = x4[:, :, 1:9, 0, :] if r == 0 else x4[:, :, 0:8, 1, :]
            sr = cen[:, :, 1::2, :] if r == 0 else cen[:, :, 0::2, :]
            ts.append(S.do(nc.scalar.activation, dst, sr, ACT.Identity, bias=nb, scale=rs,
                           after=[ld, *w]))
        ts.append(S.do(nc.scalar.activation, x4[:, :, 0, 0, :], src[:, :, 8:0:-1], ACT.Identity,
                       bias=nb, scale=rs))
        ts.append(S.do(nc.scalar.activation, x4[:, :, 8, 1, :], src[:, :, 126:118:-1], ACT.Identity,
                       bias=nb, scale=rs))
        tk = []
        xf = xn.rearrange("p a r c -> p a (r c)")
        for c3 in range(3):
            m, p, w = Sp.take()
            t = T.do(nc.tensor.matmul, p[:, 0:384], wk, xf[:, 3 * c3:3 * c3 + 3, :].rearrange("p a b -> p (a b)"),
                     start=True, stop=True, after=[*w, ts[-1], tw])
            t = S.do(nc.scalar.activation, Kb[i][:, 384 * c3:384 * c3 + 384], p[:, 0:384], ACT.Identity,
                     bias=bv4[:, 1:2], after=[t])
            Sp.held[m] = [t]
            tk.append(t)
        for c3 in range(3):
            m, p, w = Sp.take()
            for a in range(3):
                t = T.do(nc.tensor.matmul, p[:, a * 128:(a + 1) * 128], xf[:, 3 * c3 + a, :], wv,
                         start=True, stop=True, after=w)
            t = V.do(nc.vector.tensor_copy, Vb[i][:, 3 * c3:3 * c3 + 3, :].rearrange("p a b -> p (a b)"), p[:, 0:384],
                     after=[t])
            Sp.held[m] = [t]
            tk.append(t)
        if 1 <= o <= 16:
            xo = k.nc
            for c4 in range(2):
                m, p, w = Sp.take()
                for a in range(4):
                    wj = 4 * c4 + a
                    for hh in range(2):
                        dst = p[:, a * 128:(a + 1) * 128].rearrange("p (r c) -> p r c", r=8)[:, :, 8 * hh:8 * hh + 8]
                        sr = xn[:, wj, :, 8:16] if hh == 0 else xn[:, wj + 1, :, 0:8]
                        t = T.do(nc.tensor.matmul, dst, wq, sr, start=True, stop=True, after=w)
                t = S.do(nc.scalar.activation, Qb[i][:, 4 * c4:4 * c4 + 4, :].rearrange("p a b -> p (a b)"), p[:, 0:512],
                         ACT.Identity, bias=bv4[:, 4:5], scale=scale, after=[t, tq])
                Sp.held[m] = [t]
                tk.append(t)
        xnr.held[j] = [t for t in tk]
        octs[b, o] = (i, tk)

    units = [(b, wi, wj, t, h) for b in range(B) for wi in range(8) for wj in range(8)
             for t in range(2) for h in range(4)]
    st = {}
    win = {}
    rows = {}

    def stage_a(n):
        b, wi, wj, t, h = units[n]
        if wj == 0 and t == 0 and h == 0:
            if wi == 0:
                for o in range(4):
                    load_oct(b, o)
                for o in range(4):
                    make_oct(b, o)
            else:
                for o in (2 * wi + 2, 2 * wi + 3):
                    make_oct(b, o)
        if wi < 7 and t == 0 and h == 0 and wj == 2:
            for o in (2 * wi + 4, 2 * wi + 5):
                load_oct(b, o)
        i, s, w = Sp.take()
        qi, qt = octs[b, 2 * wi + 1 + t]
        for o in range(4):
            ki, kt = octs[b, 2 * wi + o]
            tt = T.do(nc.tensor.matmul, s[:, o * 256:(o + 1) * 256], Qb[qi][32 * h:32 * h + 32, wj, :],
                      Kb[ki][32 * h:32 * h + 32, wj * 128:wj * 128 + 256], start=True, stop=True,
                      after=[*w, *qt, *kt])
        j, tl, w = Tr.take()
        m = n % 4
        mxc = mx[:, m, :]
        wm = st[n - 4]["exp"] if n >= 4 else None
        tm = V.do(nc.vector.tensor_tensor_reduce, tl, s, rel[:, t, h, :], 1.0, -3.0e38, ALU.add, ALU.max,
                  mxc[:, 0:1], after=[tt, tb, *w, *([wm] if wm else [])])
        Sp.held[i] = [tm]
        tn = V.do(nc.vector.tensor_scalar, mxc[:, 1:2], mxc[:, 0:1], -1.0, None, ALU.mult, after=[tm])
        st[n] = {"tn": tn, "T": (j, tl), "m": mxc}
        if h == 0:
            ri, r, w = rsum.take()
            win[b, wi, wj, t] = {"rs": (ri, r), "rw": w}
        st[n]["win"] = win[b, wi, wj, t]

    def stage_b(n):
        b, wi, wj, t, h = units[n]
        u = st[n]
        j, tl = u["T"]
        pi, p, w = Pr.take()
        ri, r = u["win"]["rs"]
        te = S.do(nc.scalar.activation, p, tl, ACT.Exp, bias=u["m"][:, 1:2], scale=1.0,
                  accum_out=r[:, h:h + 1], after=[u["tn"], *w, *u["win"]["rw"]])
        Tr.held[j] = [te]
        u["exp"], u["P"] = te, (pi, p)

    def stage_c(n):
        u = st[n]
        pi, p = u["P"]
        i, q, w = PTp.take()
        j, pt, w2 = PTr.take()
        for g in range(8):
            tt = T.do(nc.tensor.transpose, q[:, g * 128:(g + 1) * 128], p[:, g * 128:(g + 1) * 128],
                      d["ident"], after=[u["exp"], *w, d["t_const"]])
            if g == 3:
                t1 = V.do(nc.vector.tensor_copy, pt[:, 0:512], q[:, 0:512], after=[tt, *w2])
        t2 = S.do(nc.scalar.copy, pt[:, 512:1024], q[:, 512:1024], after=[tt, *w2])
        Pr.held[pi] = [tt]
        PTp.held[i] = [t1, t2]
        u["PT"] = (j, pt, [t1, t2])

    def stage_d(n):
        b, wi, wj, t, h = units[n]
        u = st[n]
        j, pt, ready = u["PT"]
        wn = u["win"]
        if h == 0:
            wn["O"] = misc.take()
        m, o_, w = wn["O"]
        for g in range(8):
            ki, kt = octs[b, 2 * wi + g // 2]
            tt = T.do(nc.tensor.matmul, o_[:, 32 * h:32 * h + 32], pt[:, g * 128:(g + 1) * 128],
                      Vb[ki][:, wj + g % 2, 32 * h:32 * h + 32], start=(g == 0), stop=(g == 7),
                      after=[*ready, *w, *kt])
        PTr.held[j] = [tt]
        if h == 3:
            ri, r = wn["rs"]
            vi, rv, w = rinv.take()
            t1 = V.do(nc.vector.reciprocal, rv, r, after=[u["exp"], *w])
            rsum.held[ri] = [t1]
            oi, ob, w = Osb.take()
            t2 = V.do(nc.vector.tensor_tensor, ob.rearrange("p (h x) -> p h x", h=4),
                      o_[:, 0:128].rearrange("p (h x) -> p h x", h=4),
                      rv.unsqueeze(2).broadcast_to([128, 4, 32]), ALU.mult, after=[t1, tt, *w])
            rinv.held[vi] = [t2]
            wn["fin"] = (m, o_, oi, ob, t2)
        if h == 3 and wj == 7 and t == 1:
            for o in (2 * wi, 2 * wi + 1) if wi < 7 else range(14, 18):
                held[octs[b, o][0]].append(tt)

    def stage_e(n):
        b, wi, wj, t, h = units[n]
        if h != 3:
            return
        wn = st[n]["win"]
        m, o_, oi, ob, t2 = wn["fin"]
        tt = T.do(nc.tensor.transpose, o_[:, 128:256], ob, d["ident"], after=[t2])
        Osb.held[oi] = [tt]
        if t == 0:
            win[b, wi, wj] = OT.take()
        ti, ot, w = win[b, wi, wj]
        t3 = S.do(nc.scalar.activation, ot[:, 128 * t:128 * t + 128], o_[:, 128:256], ACT.Identity,
                  bias=bv4[:, 2:3], after=[tt, *w])
        misc.held[m] = [t3]
        if t == 1:
            m, p, w = misc.take()
            tt = T.do(nc.tensor.matmul, p[:, 0:256], wp, ot, start=True, stop=True, after=[*w, t3])
            OT.held[ti] = [tt]
            if wj == 0:
                rows[b, wi] = outr.take()
            oi, ob, w = rows[b, wi]
            for tt_ in range(2):
                ri = octs[b, 2 * wi + 1 + tt_][0]
                t4 = V.do(nc.vector.scalar_tensor_tensor, out=ob[:, 8 * tt_:8 * tt_ + 8, 16 * wj:16 * wj + 16],
                          in0=p[:, 128 * tt_:128 * tt_ + 128].rearrange("p (r c) -> p r c", r=8), scalar=bv4[:, 3:4],
                          in1=raw[ri][:, :, 16 * wj:16 * wj + 16], op0=ALU.add, op1=ALU.add, after=[tt, *w])
            misc.held[m] = [t4]
            if wj == 7:
                of = ob.rearrange("p a b -> p (a b)")
                for q in range(4):
                    at = (wi * 4 + q) * 6
                    t5 = V.do(nc.vector.bn_stats, stats[:, b, at:at + 6], of[:, q * 512:(q + 1) * 512], after=[t4])
                ds = k.dma(cho[oi], xout[:, b, wi * 2048:(wi + 1) * 2048], of, after=[t4])
                outr.held[oi] = [t5, ds]
                d["t_stats"] = t5
                for o in (2 * wi, 2 * wi + 1) if wi < 7 else range(14, 18):
                    held[octs[b, o][0]].append(t4)

    N = len(units) // B
    for b in range(B):
        for s in range(N + 3):
            for lag, f in ((0, stage_a), (0, stage_b), (1, stage_c), (3, stage_e), (2, stage_d)):
                if 0 <= s - lag < N:
                    f(b * N + s - lag)
    return d["t_stats"]


def layer1(k, d, I, xin, xout):
    nc = k.nc
    V, S, T, G_ = k.lanes["dve"], k.lanes["act"], k.lanes["pe"], k.lanes["pool"]
    ps = k.ps
    stats = d["stats2"]
    xn = k.buf(128, 128)
    hs = k.buf(128, 128)
    W = k.buf(16, 2, 128)
    F = k.buf(16, 3, 128)
    Gm = k.buf(128, 16, 2)
    XT = Ring([k.buf(4, 128) for _ in range(2)])
    gT = Ring([k.buf(4, 128, parts=32) for _ in range(2)])
    dft = k.buf(48)
    idft = k.buf(128, parts=32)
    sm = k.buf(8)
    c0, cw = k.chan(), k.chan()
    k.dma(c0, dft, I["dft"])
    k.dma(c0, sm[:, 0:7], I["b1"])
    t_c = k.dma(c0, idft, I["idft"])
    Ff = F.rearrange("p a b c -> p (a b) c")
    xf = xn.rearrange("p a b -> p (a b)")
    hf = hs.rearrange("p a b -> p (a b)")
    at = [0]

    def over(n):
        at[0] += n
        return xf[:, at[0] - n:at[0]]

    w0 = over(512)
    w1 = over(512).rearrange("p (a b) -> p a b", a=4)
    h1r = Ring([over(2048).rearrange("p (a b) -> p a b", a=4) for _ in range(2)])
    h2r = Ring([over(512) for _ in range(2)])
    ddr = Ring([over(512) for _ in range(4)])
    sqr = Ring([over(512) for _ in range(2)])
    sdr = Ring([over(512) for _ in range(2)])
    yr = Ring([over(512) for _ in range(2)])
    xr = Ring([over(512) for _ in range(4)])
    outr = Ring([over(512) for _ in range(3)])
    cx = [k.chan() for _ in range(4)]
    cin = [k.chan() for _ in range(4)]
    cxr = [k.chan() for _ in range(4)]
    co = [k.chan() for _ in range(3)]
    cf = k.chan()
    w_free, x_free = [], []
    t_stat = None
    bank = [ps[:, i, :] for i in range(8)]
    XTp = op = Ring(bank[0:2])
    Fp, Gp, gp = Ring(bank[2:4]), Ring(bank[4:6]), Ring(bank[6:8])

    for b in range(B):
        rs, nb = d["rs"][:, b:b + 1], d["nb"][:, b:b + 1]
        tx = []
        for q in range(4):
            ld = k.dma(cin[q], xf[:, q * 4096:(q + 1) * 4096], xin[:, b, q * 4096:(q + 1) * 4096], after=x_free)
            for e, (ln, eng) in enumerate(((S, "a"), (V, "v"))):
                part = xf[:, q * 4096 + e * 2048:q * 4096 + (e + 1) * 2048]
                if eng == "a":
                    tx.append(S.do(nc.scalar.activation, part, part, ACT.Identity, bias=nb, scale=rs, after=[ld]))
                else:
                    tx.append(V.do(nc.vector.tensor_scalar, part, part, rs, nb, ALU.mult, ALU.add, after=[ld]))
        t_hs = []
        for dr in range(2):
            tw = k.dma(cw, W.rearrange("p a b c -> p (a b c)"), I["wf"][dr], after=w_free)
            tF = []
            pend = []
            slot = [None]

            def dft_mms(g, xi, xt, t_ev):
                if g % 2 == 0:
                    slot[0] = Fp.take()
                i, p, w = slot[0]
                for j in range(4):
                    c = (g % 2) * 4 + j
                    tt = T.do(nc.tensor.matmul, p[:, c * 48:(c + 1) * 48], xt[:, j, :], dft,
                              start=True, stop=True, after=[*w, t_ev, t_c])
                XT.held[xi] = [tt]
                if g % 2 == 1:
                    ev = V.do(nc.vector.tensor_copy, Ff[:, :, 4 * g - 4:4 * g + 4],
                              p[:, 0:384].rearrange("p (l k) -> p k l", l=8), after=[tt, *t_hs])
                    Fp.held[i] = [ev]
                    tF.append(ev)

            for g in range(32):
                i, p, w = XTp.take()
                for j in range(4):
                    ln_ = 4 * g + j
                    src = xn[:, ln_, :] if dr == 0 else xn[:, :, ln_]
                    tt = T.do(nc.tensor.transpose, p[:, j * 128:(j + 1) * 128], src, d["ident"],
                              after=[*w, *(tx if dr else tx[0:2 * (g // 8) + 2])])
                xi, xt, w2 = XT.take()
                ev = S.do(nc.scalar.copy, xt.rearrange("p a b -> p (a b)"), p, after=[tt, *w2])
                XTp.held[i] = [ev]
                pend.append((g, xi, xt, ev))
                if len(pend) > 1:
                    dft_mms(*pend.pop(0))
            dft_mms(*pend.pop(0))
            x_last = tt
            tG = []
            for ky in range(16):
                i, p, w = Gp.take()
                o_ = p[:, 0:256]
                T.do(nc.tensor.matmul, o_, W[:, ky, 0, :], F[:, ky, 1:3, :].rearrange("p a b -> p (a b)"),
                     start=True, stop=False, after=[*w, tw, tF[-1]])
                tt = T.do(nc.tensor.matmul, o_, W[:, ky, 1, :], F[:, ky, 0:2, :].rearrange("p a b -> p (a b)"),
                          start=False, stop=True)
                src = o_.rearrange("p (r l) -> p l r", r=2)
                if ky % 2:
                    ev = V.do(nc.vector.tensor_copy, Gm[:, :, ky, :], src, after=[tt])
                else:
                    ev = S.do(nc.scalar.copy, Gm[:, :, ky, :], src, after=[tt])
                Gp.held[i] = [ev]
                tG.append(ev)
            w_free = [tt]
            pend = []

            def inverse(g, gi, gt, t_ev):
                i, p, w = op.take()
                for j in range(4):
                    tt = T.do(nc.tensor.matmul, p[:, j * 128:(j + 1) * 128], gt[:, j, :], idft,
                              start=True, stop=True, after=[*w, t_ev])
                gT.held[gi] = [tt]
                if dr == 0:
                    ev = V.do(nc.vector.tensor_copy, hf[:, g * 512:(g + 1) * 512], p, after=[tt, *hs_free])
                else:
                    o_ = hs[:, :, 4 * g:4 * g + 4]
                    ev = V.do(nc.vector.tensor_tensor, o_, p.rearrange("p (w h) -> p h w", w=4), o_, ALU.add,
                              after=[tt, *t_hs])
                op.held[i] = [ev]
                last[0] = ev

            hs_free = x_free
            last = [None]
            for g in range(32):
                i, p, w = gp.take()
                for j in range(4):
                    tt = T.do(nc.tensor.transpose, p[0:32, j * 128:(j + 1) * 128],
                              Gm[:, 4 * g + j, :, :].rearrange("p a b -> p (a b)"), d["ident"],
                              after=[*w, tG[-1], tG[-2]])
                gi, gt, w2 = gT.take()
                ev = S.do(nc.scalar.copy, gt.rearrange("p a b -> p (a b)"), p[0:32, :], after=[tt, *w2])
                gp.held[i] = [ev]
                pend.append((g, gi, gt, ev))
                if len(pend) > 1:
                    inverse(*pend.pop(0))
            inverse(*pend.pop(0))
            t_hs = [last[0], tt]

        k.dma(cf, w0, I["ff0"], after=[x_last])
        tf = k.dma(cf, w1.rearrange("p a b -> p (a b)"), I["ff1"], after=[x_last])
        h1p, h2p, mp = Ring(bank[0:3]), Ring(bank[3:5]), Ring(bank[5:8])
        u = {n: {} for n in range(32)}
        start = [*op.held[0], *op.held[1], *gp.held[0], *gp.held[1], x_last, t_hs[0]]

        def f0(n):
            i, x, w = xr.take()
            u[n]["x"] = (i, x, k.dma(cxr[i], x, xin[:, b, n * 512:(n + 1) * 512], after=[*w, x_last]))

        def f1(n):
            hi, h1, w1_ = h1r.take()
            for m in range(4):
                i, p, w = h1p.take()
                tt = T.do(nc.tensor.matmul, p, w0[:, m * 128:(m + 1) * 128], hf[:, n * 512:(n + 1) * 512],
                          start=True, stop=True, after=[*w, tf, *start])
                if m < 3:
                    ev = S.do(nc.scalar.activation, h1[:, m, :], p, ACT.Relu, bias=sm[:, m:m + 1],
                              after=[tt, *w1_, t_c])
                else:
                    ev = V.do(nc.vector.tensor_scalar, h1[:, m, :], p, sm[:, m:m + 1], 0.0, ALU.add, ALU.max,
                              after=[tt, *w1_, t_c])
                h1p.held[i] = [ev]
                u[n][f"part{m}"] = ev
            u[n]["h1"] = (hi, h1)
            u[n]["rhs"] = tt

        def f2(n):
            hi, h1 = u[n]["h1"]
            i, p, w = h2p.take()
            for m in range(4):
                tt = T.do(nc.tensor.matmul, p, w1[:, m, :], h1[:, m, :], start=(m == 0), stop=(m == 3),
                          after=[*w, u[n][f"part{m}"]])
            h1r.held[hi] = [tt]
            j, h2, w2 = h2r.take()
            ev = S.do(nc.scalar.activation, h2, p, ACT.Identity, bias=sm[:, 4:5], after=[tt, *w2])
            h2p.held[i] = [ev]
            u[n]["h2"] = (j, h2, ev)

        def f3(n):
            j, h2, ev = u[n]["h2"]
            i, p, w = mp.take()
            tt = T.do(nc.tensor.matmul, p, d["avg"], h2, start=True, stop=True, after=[*w, ev])
            di, dd, w2 = ddr.take()
            t1 = V.do(nc.vector.tensor_tensor, dd, h2, p, ALU.subtract, after=[tt, ev, *w2])
            mp.held[i] = [t1]
            h2r.held[j] = [t1]
            qi, sq, w3 = sqr.take()
            t2 = S.do(nc.scalar.activation, sq, dd, ACT.Square, after=[t1, *w3])
            u[n]["dd"] = (di, dd, t1)
            u[n]["sq"] = (qi, sq, t2)

        def f4(n):
            qi, sq, t2 = u[n]["sq"]
            i, p, w = mp.take()
            tt = T.do(nc.tensor.matmul, p, d["avg"], sq, start=True, stop=True, after=[*w, t2])
            sqr.held[qi] = [tt]
            si, sd, w2 = sdr.take()
            t1 = V.do(nc.vector.tensor_scalar, sd, p, EPS, None, ALU.add, after=[tt, *w2])
            mp.held[i] = [t1]
            t2 = S.do(nc.scalar.activation, sd, sd, ACT.Sqrt, after=[t1])
            u[n]["sd"] = (si, sd, t2)

        def f5(n):
            si, sd, t2 = u[n]["sd"]
            di, dd, t1 = u[n]["dd"]
            yi, y, w = yr.take()
            t3 = V.do(nc.vector.reciprocal, sd, sd, after=[t2])
            t4 = V.do(nc.vector.tensor_tensor, y, dd, sd, ALU.mult, after=[t3, *w])
            sdr.held[si] = [t4]
            ddr.held[di] = [t4]
            t5 = V.do(nc.vector.tensor_scalar, y, y, sm[:, 5:6], sm[:, 6:7], ALU.mult, ALU.add, after=[t4])
            xi, x, tl = u[n]["x"]
            oi, o_, w = outr.take()
            t6 = G_.do(nc.gpsimd.tensor_tensor, o_, y, x, ALU.add, after=[t5, tl, *w])
            yr.held[yi] = [t6]
            xr.held[xi] = [t6]
            t7 = V.do(nc.vector.bn_stats, stats[:, b, n * 6:n * 6 + 6], o_, after=[t6])
            ds = k.dma(co[oi], xout[:, b, n * 512:(n + 1) * 512], o_, after=[t6])
            outr.held[oi] = [t7, ds]
            u[n]["end"] = [t6, t7, ds]

        for s in range(32 + 5):
            for lag, f in ((3, f0), (1, f1), (2, f2), (3, f3), (4, f4), (5, f5)):
                if 0 <= s - lag < 32:
                    f(s - lag)
        x_free = [c for n in (29, 30, 31) for c in u[n]["end"]] + [u[31]["rhs"]]
        t_stat = u[31]["end"][1]
    return t_stat


def layer2(k, d, I, xin, xout):
    nc = k.nc
    V, S, T, P = k.lanes["dve"], k.lanes["act"], k.lanes["pe"], k.lanes["pool"]
    stats = d["stats2"]
    N = 512
    WG = k.buf(3, 128)
    bg = k.buf(6)
    pk = k.buf(4)
    kern = k.buf(4, 128)
    nk = k.buf(2, 128)
    c0 = k.chan()
    k.dma(c0, WG.rearrange("p a b -> p (a b)"), I["wg"])
    k.dma(c0, bg, I["bg"])
    tc = k.dma(c0, kern.rearrange("p a b -> p (a b)"), I["kern"])
    t_k = V.do(nc.vector.tensor_copy, nk[0:64, :, :], kern[0:64, 2:4, :], after=[tc])
    t_k = V.do(nc.vector.tensor_scalar, nk[64:128, :, :], kern[64:128, 2:4, :], -1.0, None, ALU.mult, after=[tc])
    bank = [k.ps[:, i, :] for i in range(8)]
    V.linked = P.linked = True
    for b in range(B):
        for h in range(2):
            for j, s_ in enumerate((d["rs"], d["nb"])):
                t = T.do(nc.tensor.matmul, bank[0][64 * b:64 * b + 64, 2 * h + j:2 * h + j + 1],
                         d["ident"][:, 64 * h:64 * h + 64], s_[:, b:b + 1], start=True, stop=True, after=[tc])
    t_pk = V.do(nc.vector.tensor_copy, pk, bank[0][:, 0:4], after=[t])
    t_bg = V.do(nc.vector.tensor_scalar, bg[:, 0:2], bg[:, 0:2], 2.0, None, ALU.add, after=[tc])

    sets = []
    names2 = ("xp", "q2", "A", "f", "g", "e", "sp", "w2", "res")
    names1 = ("m2", "sg", "m11", "p12", "m21", "m22", "tau", "del", "u1", "u2", "u3", "u4", "u5",
              "a1", "b1", "a2", "b2", "p1", "p2")
    for _ in range(2):
        s = {n: k.buf(2, N) for n in names2}
        s.update({n: k.buf(N) for n in names1})
        s["xc"] = k.buf(2, N)
        s["bas"] = k.buf(N)
        s["ch"] = [k.chan() for _ in range(4)]
        sets.append(s)
    outs = Ring([k.buf(2, N) for _ in range(2)])
    couts = [k.chan() for _ in range(2)]
    done = [[], []]
    sr4, pr = bank[0:4], Ring(bank[4:8])
    sr_held = [[] for _ in range(4)]
    NC = L // N
    loads = {}

    def load(n):
        s, fr = sets[n % 2], done[n % 2]
        sl = slice(n * N, (n + 1) * N)
        c = s["ch"]
        t0 = k.dma(c[0], s["bas"], I["basis"][:, sl], after=fr)
        t1 = k.dma(c[1], s["xc"], xin[:, :, sl], after=fr)
        for b in range(B):
            for h in range(2):
                t2 = k.dma(c[2], s["xp"][64 * b:64 * b + 64, h, :], xin[64 * h:64 * h + 64, b, sl], after=fr)
        for b in range(B):
            for h in range(2):
                t3 = k.dma(c[3], s["res"][64 * b:64 * b + 64, h, :], xin[64 * h:64 * h + 64, b, sl], after=fr)
        loads[n] = (t0, t1, t2, t3)

    load(0)
    for n in range(NC):
        s, fr = sets[n % 2], done[n % 2]
        t_bas, t_xc, t_xp, tr = loads.pop(n)
        t = {}
        for ln in (V, S, T, P):
            ln.first = ln.first + list(fr)
        sp = {}
        for i, (nm, w) in enumerate((("Ar", kern[:, 0, :]), ("Ai", nk[:, 0, :]), ("Br", kern[:, 1, :]),
                                     ("Bi", nk[:, 1, :]))):
            p, wt = sr4[i], sr_held[i]
            sp[nm] = (i, p)
            t[nm] = T.do(nc.tensor.matmul, p, w, s["bas"], start=True, stop=True, after=[*wt, t_bas, t_k, t_pk])
        for b in range(B):
            t["xc"] = S.do(nc.scalar.activation, s["xc"][:, b, :], s["xc"][:, b, :], ACT.Identity,
                           bias=d["nb"][:, b:b + 1], scale=d["rs"][:, b:b + 1], after=[t_xc])
        S.do(nc.scalar.activation, s["q2"][:, 0, :], sp["Ar"][1], ACT.Square, after=[t["Ar"]])
        t["q2"] = S.do(nc.scalar.activation, s["q2"][:, 1, :], sp["Ai"][1], ACT.Square, after=[t["Ai"]])
        t["m2"] = V.do(nc.vector.scalar_tensor_tensor, out=s["m2"], in0=s["q2"][:, 0, :], scalar=1e-8,
                       in1=s["q2"][:, 1, :], op0=ALU.add, op1=ALU.add, after=[t["q2"]])
        t["mag"] = S.do(nc.scalar.activation, s["m2"], s["m2"], ACT.Sqrt, after=[t["m2"]])
        gates = {}
        for gi, gn in enumerate(("f", "g", "e")):
            for h in range(2):
                i, p, wt = pr.take()
                for b in range(B):
                    tt = T.do(nc.tensor.matmul, p[64 * b:64 * b + 64, :], WG[:, gi, 64 * h:64 * h + 64],
                              s["xc"][:, b, :], start=True, stop=True, after=[*wt, t["xc"]])
                if gn == "e":
                    ev = S.do(nc.scalar.activation, s["e"][:, h, :], p, ACT.Abs, bias=bg[:, 4 + h:5 + h], after=[tt])
                    ev2 = V.do(nc.vector.tensor_scalar, s["sp"][:, h, :], p, bg[:, 4 + h:5 + h], 0.0, ALU.add,
                               ALU.max, after=[tt, ev])
                    pr.held[i] = [ev, ev2]
                    t["relu"], t["abs"] = ev2, ev
                else:
                    ev = S.do(nc.scalar.activation, s[gn][:, h, :], p, ACT.Sigmoid,
                              bias=bg[:, 2 * gi + h:2 * gi + h + 1], after=[tt, t_bg])
                    pr.held[i] = [ev]
                    t[gn] = ev
        t["sg"] = S.do(nc.scalar.activation, s["sg"], s["m2"], ACT.Sigmoid, after=[t["mag"]])
        t["ex"] = S.do(nc.scalar.activation, s["e"], s["e"], ACT.Exp, scale=-1.0, after=[t["abs"]])
        t["ln"] = S.do(nc.scalar.activation, s["e"], s["e"], ACT.Ln, bias=1.0, after=[t["ex"]])
        for h in range(2):
            t["xp"] = S.do(nc.scalar.activation, s["xp"][:, h, :], s["xp"][:, h, :], ACT.Identity,
                           bias=pk[:, 2 * h + 1:2 * h + 2], scale=pk[:, 2 * h:2 * h + 1], after=[t_xp, t_pk])
        t["u1"] = V.do(nc.vector.tensor_scalar, s["u1"], s["m2"], 1e-8, None, ALU.add, after=[t["mag"], t["sg"]])
        t["u2"] = V.do(nc.vector.reciprocal, s["u2"], s["u1"], after=[t["u1"]])
        t["u3"] = V.do(nc.vector.scalar_tensor_tensor, out=s["u3"], in0=s["sg"], scalar=0.95, in1=s["u2"],
                       op0=ALU.mult, op1=ALU.mult, after=[t["u2"], t["sg"]])
        for h, nm in enumerate(("Ar", "Ai")):
            t["A"] = V.do(nc.vector.tensor_tensor, s["A"][:, h, :], s["u3"], sp[nm][1], ALU.mult, after=[t["u3"]])
            sr_held[sp[nm][0]] = [t["A"], t["q2"]]
        xr_, xi_ = s["xp"][:, 0, :], s["xp"][:, 1, :]
        V.do(nc.vector.tensor_tensor, s["p1"], xr_, sp["Br"][1], ALU.mult, after=[t["Br"], t["xp"]])
        t["p2"] = V.do(nc.vector.tensor_tensor, s["p2"], xi_, sp["Bi"][1], ALU.mult, after=[t["Bi"]])
        t["q0"] = V.do(nc.vector.tensor_tensor, s["q2"][:, 0, :], s["p1"], s["p2"], ALU.subtract, after=[t["p2"]])
        t["a1"] = V.do(nc.vector.tensor_tensor, s["a1"], xi_, sp["Br"][1], ALU.mult)
        t["b1"] = V.do(nc.vector.tensor_tensor, s["b1"], xr_, sp["Bi"][1], ALU.mult)
        sr_held[sp["Br"][0]] = [t["a1"]]
        sr_held[sp["Bi"][0]] = [t["b1"]]
        t["Bx"] = V.do(nc.vector.tensor_tensor, s["q2"][:, 1, :], s["a1"], s["b1"], ALU.add, after=[t["b1"]])
        t["sp"] = P.do(nc.gpsimd.tensor_tensor, s["sp"], s["sp"], s["e"], ALU.add, after=[t["relu"], t["ln"]])
        t["sg2"] = P.do(nc.gpsimd.tensor_tensor, s["sp"], s["sp"], s["g"], ALU.mult, after=[t["sp"], t["g"]])
        t["inp"] = V.do(nc.vector.scalar_tensor_tensor, out=s["sp"], in0=s["sp"], scalar=0.1, in1=s["q2"],
                        op0=ALU.mult, op1=ALU.mult, after=[t["sg2"], t["Bx"], t["q0"]])
        Ar, Ai, fr_, fi_ = s["A"][:, 0, :], s["A"][:, 1, :], s["f"][:, 0, :], s["f"][:, 1, :]

        def v(o, a, op, b_, *after):
            t[o] = V.do(nc.vector.tensor_tensor, s[o], s[a], s[b_], op, after=[t[x] for x in after])

        def g(o, a, op, b_, *after):
            t[o] = P.do(nc.gpsimd.tensor_tensor, s[o], s[a], s[b_], op, after=[t[x] for x in after])

        t["m11"] = V.do(nc.vector.tensor_tensor, s["m11"], fr_, Ar, ALU.mult, after=[t["A"], t["f"]])
        t["m22"] = V.do(nc.vector.tensor_tensor, s["m22"], fi_, Ar, ALU.mult, after=[t["A"], t["f"]])
        t["p12"] = P.do(nc.gpsimd.tensor_tensor, s["p12"], fr_, Ai, ALU.mult, after=[t["A"], t["f"]])
        t["m21"] = P.do(nc.gpsimd.tensor_tensor, s["m21"], fi_, Ai, ALU.mult, after=[t["A"], t["f"]])
        g("p1", "m11", ALU.mult, "m22", "m11", "m22", "q0")
        v("tau", "m11", ALU.add, "m22", "m11", "m22")
        g("p2", "p12", ALU.mult, "m21", "p12", "m21", "q0")
        g("del", "p1", ALU.add, "p2", "p1", "p2")
        ir, ii = s["sp"][:, 0, :], s["sp"][:, 1, :]
        P.do(nc.gpsimd.tensor_tensor, s["e"][:, 0, :], s["m11"], ir, ALU.mult, after=[t["inp"]])
        P.do(nc.gpsimd.tensor_tensor, s["e"][:, 1, :], s["m21"], ir, ALU.mult)
        P.do(nc.gpsimd.tensor_tensor, s["w2"][:, 0, :], s["p12"], ii, ALU.mult)
        t["w2"] = P.do(nc.gpsimd.tensor_tensor, s["w2"][:, 1, :], s["m22"], ii, ALU.mult)
        P.do(nc.gpsimd.tensor_tensor, s["w2"][:, 0, :], s["e"][:, 0, :], s["w2"][:, 0, :], ALU.subtract,
             after=[t["w2"]])
        t["Mv"] = P.do(nc.gpsimd.tensor_tensor, s["w2"][:, 1, :], s["e"][:, 1, :], s["w2"][:, 1, :], ALU.add)
        v("u1", "tau", ALU.mult, "tau", "tau")
        v("u2", "tau", ALU.mult, "del", "tau", "del")
        t["u3"] = V.do(nc.vector.tensor_scalar, s["u3"], s["del"], -1.0, 1.0, ALU.mult, ALU.add, after=[t["del"]])
        v("b1", "u3", ALU.subtract, "u2", "u3", "u2")
        v("a1", "u1", ALU.add, "tau", "u1")
        v("a1", "a1", ALU.add, "u3", "a1")
        t["u1"] = V.do(nc.vector.scalar_tensor_tensor, out=s["u1"], in0=s["del"], scalar=-2.0, in1=s["u1"],
                       op0=ALU.mult, op1=ALU.add, after=[t["u1"]])
        v("u2", "del", ALU.mult, "del", "del")
        v("u4", "u1", ALU.mult, "u1", "u1")
        t["u4"] = V.do(nc.vector.scalar_tensor_tensor, out=s["u4"], in0=s["u2"], scalar=-2.0, in1=s["u4"],
                       op0=ALU.mult, op1=ALU.add, after=[t["u4"], t["u2"]])
        v("u5", "u2", ALU.mult, "u2", "u2")
        v("m2", "u1", ALU.mult, "del", "u1")
        v("m2", "m2", ALU.add, "u2", "m2", "u2")
        v("u3", "u1", ALU.mult, "tau", "u1")
        v("a2", "u4", ALU.mult, "u4", "u4")
        v("a2", "a2", ALU.add, "u4", "a2")
        t["u2"] = V.do(nc.vector.tensor_scalar, s["u2"], s["u5"], -1.0, 1.0, ALU.mult, ALU.add, after=[t["u5"]])
        v("a2", "a2", ALU.add, "u2", "a2", "u2")
        v("b2", "u4", ALU.mult, "u5", "u5")
        v("b2", "u2", ALU.subtract, "b2", "b2", "u2")
        v("u1", "a2", ALU.mult, "u3", "a2", "u3")
        v("u2", "a2", ALU.mult, "m2", "a2", "m2")
        v("u2", "b2", ALU.subtract, "u2", "u2", "b2")
        v("u3", "a1", ALU.mult, "u1", "a1", "u1")
        v("u4", "u3", ALU.mult, "tau", "u3")
        v("u5", "a1", ALU.mult, "u2", "u2")
        v("m2", "b1", ALU.mult, "u1", "b1")
        v("u4", "u4", ALU.add, "u5", "u4", "u5")
        v("u4", "u4", ALU.add, "m2", "u4", "m2")
        v("b2", "b1", ALU.mult, "u2", "u2")
        v("u3", "u3", ALU.mult, "del", "u3")
        v("b2", "b2", ALU.subtract, "u3", "b2", "u3")
        al = s["u4"].unsqueeze(1).broadcast_to([128, 2, N])
        be = s["b2"].unsqueeze(1).broadcast_to([128, 2, N])
        t["r1"] = V.do(nc.vector.tensor_tensor, s["w2"], s["w2"], al, ALU.mult, after=[t["Mv"], t["u4"]])
        t["r2"] = P.do(nc.gpsimd.tensor_tensor, s["sp"], s["sp"], be, ALU.mult, after=[t["b2"], t["Mv"]])
        if n + 1 < NC:
            load(n + 1)
        t["r3"] = P.do(nc.gpsimd.tensor_tensor, s["w2"], s["w2"], s["sp"], ALU.add, after=[t["r1"], t["r2"]])
        oi, o_, w = outs.take()
        t["o"] = P.do(nc.gpsimd.tensor_tensor, o_, s["w2"], s["res"], ALU.add, after=[t["r3"], tr, *w])
        for h in range(2):
            t["st"] = V.do(nc.vector.bn_stats, d["statp"][:, h, n * 6:n * 6 + 6], o_[:, h, :], after=[t["o"]])
        for b in range(B):
            for h in range(2):
                td = k.dma(couts[oi], xout[64 * h:64 * h + 64, b, n * N:(n + 1) * N],
                           o_[64 * b:64 * b + 64, h, :], after=[t["o"]])
        outs.held[oi] = [t["st"], td]
        done[n % 2] = [t["st"], t["o"], t["xp"], tt]
    V.linked = P.linked = False
    mvp = k.buf(2, 2)
    for h in range(2):
        ta = V.do(nc.vector.bn_aggr, mvp[:, h, :], d["statp"][:, h, :], after=[t["st"]])
    for b in range(B):
        for h in range(2):
            tt = T.do(nc.tensor.matmul, bank[4][64 * h:64 * h + 64, 2 * b:2 * b + 2],
                      d["ident"][:, 64 * b:64 * b + 64], mvp[:, h, :], start=True, stop=True,
                      after=[ta, *pr.held[0]])
    return V.do(nc.vector.tensor_copy, d["mv"].rearrange("p a b -> p (a b)"), bank[4][:, 0:4], after=[tt])


def layer3(k, d, I, xin, xout):
    nc = k.nc
    V, S, T, P = k.lanes["dve"], k.lanes["act"], k.lanes["pe"], k.lanes["pool"]
    ps = k.ps
    U, Y = d["U"], d["Y"]
    win = k.buf(256)
    cwb = k.buf(9, 256)
    cb = k.buf(2)
    c0 = k.chan()
    k.dma(c0, win, I["winx"])
    k.dma(c0, cb, I["convb"])
    t_w = k.dma(c0, cwb.rearrange("p a b -> p (a b)"), I["convw"].partition_broadcast(128))
    for tap in range(9):
        t_cw = V.do(nc.vector.tensor_tensor, cwb[:, tap, :], cwb[:, tap, :], win, ALU.mult, after=[t_w])
    strips = Ring([k.buf(34, 130) for _ in range(2)])
    raws = Ring([k.buf(34, 128) for _ in range(2)])
    for st in strips.bufs:
        t_z = V.do(nc.vector.memset, st, 0.0)
    craw = [k.chan() for _ in range(2)]
    u1 = Ring([k.buf(4, 32, 32) for _ in range(2)])
    u2 = Ring([k.buf(4, 32, 32) for _ in range(2)])
    cu1 = [k.chan() for _ in range(2)]
    cu2 = [k.chan() for _ in range(2)]
    pr = Ring([ps[:, i, :] for i in range(8)])
    rl = {}
    order = [(b, g) for b in range(B) for g in range(4)]

    def load1(n):
        b, g = order[n]
        i, rw, w = raws.take()
        r0, r1 = max(32 * g - 1, 0), min(32 * g + 33, 128)
        o = r0 - (32 * g - 1)
        rl[n] = (i, rw, o, r1 - r0, k.dma(craw[i], rw[:, o:o + r1 - r0, :].rearrange("p a b -> p (a b)"),
                                          xin[:, b, r0 * 128:r1 * 128], after=w))

    load1(0)
    for n, (b, g) in enumerate(order):
        i, rw, o, nr, ld = rl.pop(n)
        j, st, w = strips.take()
        if g in (0, 3) and n > 1:
            t_z = V.do(nc.vector.memset, st[:, 0 if g == 0 else 33, :], 0.0, after=w)
        tn = S.do(nc.scalar.activation, st[:, o:o + nr, 1:129], rw[:, o:o + nr, :], ACT.Identity,
                  bias=d["nb"][:, b:b + 1], scale=d["rs"][:, b:b + 1], after=[ld, *w, t_z])
        raws.held[i] = [tn]
        if n + 1 < len(order):
            load1(n + 1)
        for h in range(2):
            a1, o1, w1 = u1.take()
            a2, o2, w2 = u2.take()
            for r4 in range(8):
                pi, p, wp_ = pr.take()
                for tap in range(9):
                    dy, dx = tap // 3, tap % 3
                    tt = T.do(nc.tensor.matmul, p.rearrange("p (r c) -> p r c", r=4),
                              cwb[:, tap, h * 128:(h + 1) * 128],
                              st[:, 4 * r4 + dy:4 * r4 + dy + 4, dx:dx + 128],
                              start=(tap == 0), stop=(tap == 8), after=[*wp_, tn, t_cw, t_z])
                ev = S.do(nc.scalar.activation, o1[:, :, 4 * r4:4 * r4 + 4, :],
                          p.rearrange("p (r a c) -> p a r c", r=4, a=4), ACT.Silu,
                          bias=cb[:, h:h + 1], after=[tt, *w1])
                pr.held[pi] = [ev]
            for a in range(4):
                ln, eng = (V, nc.vector) if a % 2 else (P, nc.gpsimd)
                t_c = ln.do(eng.tensor_copy, o2[:, a, :, :], o1[:, a, :, :].rearrange("p r c -> p c r"),
                            after=[ev, *w2])
                if a == 2:
                    t_c2 = t_c
            d1 = k.dma(cu1[a1], U[0, b, h, :, g * 4096:(g + 1) * 4096], o1.rearrange("p a r c -> p (a r c)"),
                       after=[ev])
            d2 = k.dma(cu2[a2], U[1, b, h].rearrange("p (a q l) -> p a q l", a=4, q=4)[:, :, g, :],
                       o2.rearrange("p a r c -> p a (r c)"), after=[t_c, t_c2])
            u1.held[a1] = [t_c, t_c2, d1]
            u2.held[a2] = [d2]
        strips.held[j] = [tt]
    k.phase()

    TL = 1024
    NCH = L // TL
    selw = k.buf(32, 128, dt=BF16)
    c0 = k.chan()
    t_sel = k.dma(c0, selw.rearrange("p a b -> p (a b)"), I["sel"])
    par = Ring([(k.buf(2, 104), k.buf(256), k.buf(2, 18), k.buf(2, 16)) for _ in range(2)])
    cpar = [k.chan() for _ in range(2)]
    ur = Ring([k.buf(2, TL) for _ in range(2)])
    cu = [k.chan() for _ in range(2)]
    X = k.buf(TL)
    R1 = k.buf(TL)
    Mb = k.buf(TL, dt=BF16)
    S3r = Ring([k.buf(TL, dt=BF16) for _ in range(2)])
    dl = Ring([k.buf(2, TL) for _ in range(2)])
    du = Ring([k.buf(2, TL) for _ in range(2)])
    tmp = k.buf(2, TL)
    Bb = Ring([k.buf(TL) for _ in range(2)])
    Cb = Ring([k.buf(TL) for _ in range(3)])
    dA = Ring([k.buf(2, TL) for _ in range(2)])
    dBu = Ring([k.buf(2, TL) for _ in range(2)])
    hr = Ring([k.buf(2, TL) for _ in range(2)])
    hcr = Ring([k.buf(2, TL) for _ in range(2)])
    yo = Ring([k.buf(2, TL) for _ in range(1)])
    yp = Ring([k.buf(2, TL) for _ in range(1)])
    state = k.buf(2, 16)
    cy, cyp = [k.chan() for _ in range(1)], [k.chan() for _ in range(1)]
    pp = Ring([ps[:, 0:2, :].rearrange("p a b -> p (a b)"), ps[:, 2:4, :].rearrange("p a b -> p (a b)")])
    yps = ps[:, 4:8, :].rearrange("p (h a) b -> p h (a b)", h=2)
    chunks = []
    for b in range(B):
        for kk in (0, 2, 1, 3):
            cs = range(NCH) if kk < 2 else range(NCH - 1, -1, -1)
            chunks += [(b, kk, c, n == 0) for n, c in enumerate(cs)]
    C_ = {}
    held_X, held_M, held_tmp = [], [], []
    parn = {}
    y_free = [[]]
    y_done = {}

    def fetch(n):
        b, kk, c, first = chunks[n]
        e = C_[n] = {}
        if first:
            i, bufs, w = par.take()
            k.dma(cpar[i], bufs[0].rearrange("p a b -> p (a b)"), I["xproj"][kk], after=w)
            k.dma(cpar[i], bufs[1][96:104, :], I["dtw"][kk], after=w)
            tp = k.dma(cpar[i], bufs[2].rearrange("p a b -> p (a b)"), I["par"][kk], after=w)
            ta = S.do(nc.scalar.activation, bufs[3], bufs[2][:, :, 0:16], ACT.Exp, after=[tp, *w])
            ta = V.do(nc.vector.tensor_scalar, bufs[3], bufs[3], -1.0, None, ALU.mult, after=[ta])
            parn[b, kk] = (i, bufs, tp, ta)
        e["par"] = parn[b, kk]
        i, u, w = ur.take()
        for h in range(2):
            t = k.dma(cu[i], u[:, h, :], U[kk % 2, b, h, :, c * TL:(c + 1) * TL], after=w)
        e["u"] = (i, u, t)

    def prep(n):
        e = C_[n]
        pi, (xp, dtw, pc, A), tp, ta = e["par"]
        ui, u, tu = e["u"]
        i, p, w = pp.take()
        for q in range(2):
            for h in range(2):
                tt = T.do(nc.tensor.matmul, p[0:104, q * 512:(q + 1) * 512], xp[:, h, :],
                          u[:, h, q * 512:(q + 1) * 512], start=(h == 0), stop=(h == 1), after=[*w, tu, tp])
        tX = S.do(nc.scalar.copy, X[0:104, :], p[0:104, :], after=[tt, *held_X])
        pp.held[i] = [tX]
        si, S3, w3 = S3r.take()
        t1 = S.do(nc.scalar.copy, S3[0:96, :], X[0:96, :], after=[tX, *w3])
        t2 = P.do(nc.gpsimd.tensor_tensor, R1[0:96, :], X[0:96, :], S3[0:96, :], ALU.subtract, after=[t1, *held_M])
        t3 = S.do(nc.scalar.copy, Mb[0:96, :], R1[0:96, :], after=[t2, *held_M])
        t4 = P.do(nc.gpsimd.tensor_tensor, R1[64:96, :], R1[64:96, :], Mb[64:96, :], ALU.subtract, after=[t3])
        t5 = S.do(nc.scalar.copy, S3[32:64, :], Mb[32:64, :], after=[t3, t2])
        t6 = S.do(nc.scalar.copy, S3[64:96, :], R1[64:96, :], after=[t4])
        e["S3"] = (si, S3, [t5, t6])
        held_M[:] = [t5, t6]
        di, de, wd = dl.take()
        qi, dq, wq_ = du.take()
        for h in range(2):
            i, p, w = pp.take()
            for q in range(2):
                tt = T.do(nc.tensor.matmul, p[:, q * 512:(q + 1) * 512], dtw[96:104, h * 128:(h + 1) * 128],
                          X[96:104, q * 512:(q + 1) * 512], start=True, stop=True, after=[*w, tX])
            bias = pc[:, h, 16:17]
            t7 = S.do(nc.scalar.activation, tmp[:, h, :], p, ACT.Abs, bias=bias, after=[tt, *held_tmp])
            t8 = S.do(nc.scalar.activation, de[:, h, :], p, ACT.Relu, bias=bias, after=[tt, *wd])
            pp.held[i] = [t8]
        held_X[:] = [tt, t2]
        t9 = S.do(nc.scalar.activation, tmp, tmp, ACT.Exp, scale=-1.0, after=[t7])
        t10 = S.do(nc.scalar.activation, tmp, tmp, ACT.Ln, bias=1.0, after=[t9])
        t11 = P.do(nc.gpsimd.tensor_tensor, de, de, tmp, ALU.add, after=[t10, t8])
        t12 = P.do(nc.gpsimd.tensor_tensor, dq, de, u, ALU.mult, after=[t11, tu, *wq_])
        held_tmp[:] = [t11]
        e["dl"], e["du"] = (di, de, t11), (qi, dq, t12)

    iters = [(n, m) for n in range(len(chunks)) for m in range(16)]
    E = {}

    def bc(it):
        n, m = iters[it]
        e = C_[n]
        si, S3, ts = e["S3"]
        r = E[it] = {}
        for nm, ring, row in (("B", Bb, m), ("C", Cb, 16 + m)):
            i, p, w = pp.take()
            for q in range(2):
                tt = T.do(nc.tensor.matmul, p[:, q * 512:(q + 1) * 512], selw[0:96, row, :],
                          S3[0:96, q * 512:(q + 1) * 512], start=True, stop=True, after=[*w, *ts, t_sel])
            j, o_, w2 = ring.take()
            ev = S.do(nc.scalar.copy, o_, p, after=[tt, *w2])
            pp.held[i] = [ev]
            r[nm] = (j, o_, ev)
        if m == 15:
            S3r.held[si] = [tt]

    def ex(it):
        n, m = iters[it]
        e, r = C_[n], E[it]
        _, (xp, dtw, pc, A), tp, ta = e["par"]
        di, de, td = e["dl"]
        j, a, w = dA.take()
        for h in range(2):
            t = S.do(nc.scalar.activation, a[:, h, :], de[:, h, :], ACT.Exp, scale=A[:, h, m:m + 1],
                     after=[td, ta, *w])
        r["dA"] = (j, a, t)
        qi, dq, tq = e["du"]
        bj, bb, tb = r["B"]
        j, q, w = dBu.take()
        t2 = P.do(nc.gpsimd.tensor_tensor, q, dq, bb.unsqueeze(1).broadcast_to([128, 2, TL]), ALU.mult,
                  after=[tq, tb, *w])
        Bb.held[bj] = [t2]
        r["dBu"] = (j, q, t2)
        if m == 15:
            dl.held[di] = [t]
            du.held[qi] = [t2]

    def scan(it):
        n, m = iters[it]
        b, kk, c, first = chunks[n]
        r = E[it]
        j, a, ta = r["dA"]
        i, q, tq = r["dBu"]
        hj, hb, w = hr.take()
        step = 1 if kk < 2 else -1
        for h in range(2):
            t = V.do(nc.vector.tensor_tensor_scan, hb[:, h, ::step], a[:, h, ::step], q[:, h, ::step],
                     0.0 if first else state[:, h, m:m + 1], ALU.mult, ALU.add, after=[ta, tq, *w, *st_t.get(m, [])])
        dA.held[j] = [t]
        dBu.held[i] = [t]
        end = TL - 1 if kk < 2 else 0
        r["h"] = (hj, hb, t)
        r["end"] = end

    st_t = {}

    def outp(it):
        n, m = iters[it]
        r = E[it]
        hj, hb, t = r["h"]
        end = r["end"]
        ts = V.do(nc.vector.tensor_copy, state[:, :, m:m + 1], hb[:, :, end:end + 1], after=[t])
        st_t[m] = [ts]
        cj, cc, tc_ = r["C"]
        gj, hc, w = hcr.take()
        ln, eng = (P, nc.gpsimd) if m in POOLC else (V, nc.vector)
        t2 = ln.do(eng.tensor_tensor, hc, hb, cc.unsqueeze(1).broadcast_to([128, 2, TL]), ALU.mult,
                   after=[t, tc_, *w])
        Cb.held[cj] = [t2]
        hr.held[hj] = [t2, ts]
        r["hc"] = (gj, hc, t2)

    POOLC = (3, 7, 11, 15)

    def acc(it):
        n, m = iters[it]
        b, kk, c, first = chunks[n]
        r, e = E.pop(it), C_[n]
        gj, hc, t2 = r["hc"]
        for h in range(2):
            for q in range(2):
                tt = T.do(nc.tensor.matmul, yps[:, h, q * 512:(q + 1) * 512], d["ident"],
                          hc[:, h, q * 512:(q + 1) * 512], start=(m == 0), stop=(m == 15),
                          after=[t2, *y_free[0]])
        hcr.held[gj] = [tt]
        if m == 15:
            pi, (xp, dtw, pc, A), tp, ta = e["par"]
            ui, u, tu = e["u"]
            oi, o_, w = yo.take()
            for h in range(2):
                t3 = V.do(nc.vector.scalar_tensor_tensor, out=o_[:, h, :], in0=u[:, h, :],
                          scalar=pc[:, h, 17:18], in1=yps[:, h, :], op0=ALU.mult, op1=ALU.add,
                          after=[tt, *w])
            y_free[0] = [t3]
            ur.held[ui] = [t3]
            par.held[pi] = [t3, tt, r["dA"][2]]
            dst = Y[kk % 2, b]
            if kk >= 2:
                qi, prev, w = yp.take()
                for h in range(2):
                    tl = k.dma(cyp[qi], prev[:, h, :], dst[h, :, c * TL:(c + 1) * TL],
                               after=[*w, y_done[b, kk - 2, c]])
                t3 = P.do(nc.gpsimd.tensor_tensor, o_, o_, prev, ALU.add, after=[t3, tl])
                yp.held[qi] = [t3]
            for h in range(2):
                td = k.dma(cy[oi], dst[h, :, c * TL:(c + 1) * TL], o_[:, h, :], after=[t3])
            y_done[b, kk, c] = td
            yo.held[oi] = [td]

    NI = len(iters)
    fetch(0)
    prep(0)
    fetch(1)
    for s in range(NI + 4):
        if 0 <= s - 3 < NI:
            acc(s - 3)
        if s < NI:
            n, m = iters[s]
            if m == 8 and n + 1 < len(chunks):
                prep(n + 1)
            bc(s)
        if 0 <= s - 1 < NI:
            ex(s - 1)
        if 0 <= s - 2 < NI:
            scan(s - 2)
            outp(s - 2)
        if 0 <= s - 3 < NI:
            n, m = iters[s - 3]
            if m == 15 and n + 2 < len(chunks):
                fetch(n + 2)
    k.phase()

    wz = k.buf(256)
    wo = k.buf(2, 128)
    lnp = k.buf(2, 2)
    c0 = k.chan()
    k.dma(c0, wz, I["winz"])
    k.dma(c0, wo.rearrange("p a b -> p (a b)"), I["wout"])
    t_c = k.dma(c0, lnp.rearrange("p a b -> p (a b)"), I["lnp"])
    Y1 = [k.buf(128, 128) for _ in range(2)]
    cY1 = [k.chan() for _ in range(2)]
    N = 512
    xr = Ring([k.buf(N) for _ in range(4)])
    xnr = Ring([k.buf(N) for _ in range(2)])
    yr = Ring([k.buf(2, N) for _ in range(4)])
    sqr = Ring([k.buf(2, N) for _ in range(2)])
    zr = Ring([k.buf(2, N) for _ in range(3)])
    sdr = Ring([k.buf(N) for _ in range(2)])
    outr = Ring([k.buf(N) for _ in range(2)])
    cx, cyr, co = [k.chan() for _ in range(4)], [k.chan() for _ in range(4)], [k.chan() for _ in range(2)]
    bk = [ps[:, i, :] for i in range(8)]
    mp, zp, op = Ring(bk[0:3]), Ring(bk[3:6]), Ring(bk[6:8])
    y_last = []
    for b in range(B):
        for h in range(2):
            tY = k.dma(cY1[h], Y1[h].rearrange("p a b -> p (a b)"), Y[1, b, h], after=y_last)
            y_last2 = tY
            if h == 0:
                tY0 = tY
        u = {}

        def g0(n):
            i, x, w = xr.take()
            tx = k.dma(cx[i], x, xin[:, b, n * N:(n + 1) * N], after=w)
            j, y, w = yr.take()
            for h in range(2):
                ty = k.dma(cyr[j], y[:, h, :], Y[0, b, h, :, n * N:(n + 1) * N], after=w)
            u[n] = {"x": (i, x, tx), "y": (j, y, ty)}

        def g1(n):
            i, x, tx = u[n]["x"]
            j, y, ty = u[n]["y"]
            for h in range(2):
                yv = y[:, h, :].rearrange("p (r w) -> p r w", r=4)
                t1 = V.do(nc.vector.tensor_tensor, yv, yv,
                          Y1[h][:, :, 4 * n:4 * n + 4].rearrange("p w r -> p r w"), ALU.add, after=[ty, tY0, tY])
            u[n]["y1"] = t1
            q, xn, w = xnr.take()
            t2 = S.do(nc.scalar.activation, xn, x, ACT.Identity, bias=d["nb"][:, b:b + 1],
                      scale=d["rs"][:, b:b + 1], after=[tx, *w])
            zi, z, w = zr.take()
            for h in range(2):
                m, p, w2 = zp.take()
                tt = T.do(nc.tensor.matmul, p, wz[:, h * 128:(h + 1) * 128], xn, start=True, stop=True,
                          after=[t2, *w2, t_c])
                t3 = S.do(nc.scalar.activation, z[:, h, :], p, ACT.Silu, after=[tt, *w])
                zp.held[m] = [t3]
            xnr.held[q] = [tt]
            u[n]["z"] = (zi, z, t3)

        def g2(n):
            j, y, ty = u[n]["y"]
            m, p, w = mp.take()
            for h in range(2):
                tt = T.do(nc.tensor.matmul, p, d["avg"], y[:, h, :], start=(h == 0), stop=(h == 1),
                          after=[u[n]["y1"], *w])
            for h in range(2):
                t1 = V.do(nc.vector.scalar_tensor_tensor, out=y[:, h, :], in0=p, scalar=-0.5, in1=y[:, h, :],
                          op0=ALU.mult, op1=ALU.add, after=[tt])
            mp.held[m] = [t1]
            qi, sq, w = sqr.take()
            t2 = S.do(nc.scalar.activation, sq, y, ACT.Square, after=[t1, *w])
            u[n]["sq"] = (qi, sq, t2)
            u[n]["yd"] = t1

        def g3(n):
            qi, sq, t2 = u[n]["sq"]
            m, p, w = mp.take()
            for h in range(2):
                tt = T.do(nc.tensor.matmul, p, d["avg"], sq[:, h, :], start=(h == 0), stop=(h == 1), after=[t2, *w])
            sqr.held[qi] = [tt]
            si, sd, w = sdr.take()
            t1 = V.do(nc.vector.tensor_scalar, sd, p, 0.5, EPS, ALU.mult, ALU.add, after=[tt, *w])
            mp.held[m] = [t1]
            t2 = S.do(nc.scalar.activation, sd, sd, ACT.Sqrt, after=[t1])
            t3 = V.do(nc.vector.reciprocal, sd, sd, after=[t2])
            j, y, ty = u[n]["y"]
            zi, z, tz = u[n]["z"]
            t4 = P.do(nc.gpsimd.tensor_tensor, y, y, sd.unsqueeze(1).broadcast_to([128, 2, N]), ALU.mult,
                      after=[t3, u[n]["yd"], t2])
            sdr.held[si] = [t4]
            for h in range(2):
                t5 = V.do(nc.vector.tensor_scalar, y[:, h, :], y[:, h, :], lnp[:, h, 0:1], lnp[:, h, 1:2],
                          ALU.mult, ALU.add, after=[t4, t_c])
            t6 = V.do(nc.vector.tensor_tensor, z, z, y, ALU.mult, after=[t5, tz])
            yr.held[j] = [t6]
            m, p, w = op.take()
            for h in range(2):
                tt = T.do(nc.tensor.matmul, p, wo[:, h, :], z[:, h, :], start=(h == 0), stop=(h == 1),
                          after=[t6, *w])
            zr.held[zi] = [tt]
            oi, o_, w = outr.take()
            xi, x, tx = u[n]["x"]
            t7 = V.do(nc.vector.tensor_tensor, o_, x, p, ALU.add, after=[tt, *w])
            op.held[m] = [t7]
            xr.held[xi] = [t7]
            td = k.dma(co[oi], xout[:, b, n * N:(n + 1) * N], o_, after=[t7])
            outr.held[oi] = [td]
            u[n]["end"] = t7

        for s in range(32 + 3):
            for lag, f in ((0, g0), (1, g1), (2, g2), (3, g3)):
                if 0 <= s - lag < 32:
                    f(s - lag)
        y_last = [u[31]["y1"]]
    return None


LAYERS = {0: layer0, 1: layer1, 2: layer2, 3: layer3}

def program(nc, I, xin, scratch, out, layers=(0, 1, 2, 3)):
    with ExitStack() as ctx:
        k = Core(nc, ctx)
        d = {}
        d["grp"] = k.buf(128)
        d["ident"] = k.buf(128)
        d["avg"] = k.buf(128)
        d["rs"] = k.buf(2)
        d["nb"] = k.buf(2)
        d["mv"] = k.buf(2, 2)
        d["sm"] = k.buf(8)
        d["stats"] = k.buf(2, 192)
        d["stats2"] = d["stats"]
        d["statp"] = d["stats"]
        d["U"] = nc.dram_tensor("U", (2, B, 2, 128, L), F32).ap()
        d["Y"] = nc.dram_tensor("Y", (2, B, 2, 128, L), F32).ap()
        cc = k.chan()
        k.dma(cc, d["grp"], I["grp"])
        k.dma(cc, d["ident"], I["ident"])
        d["t_const"] = k.dma(cc, d["avg"], I["avg"])
        k.low = k.top
        t = first_stats(k, d, xin)
        t = norm_params(k, d, d["stats"], [t])
        x = xin
        fns = LAYERS
        for n, lay in enumerate(layers):
            k.phase()
            y = out if n == len(layers) - 1 else scratch[n % 2]
            t = fns[lay](k, d, I, x, y)
            if n < len(layers) - 1:
                k.phase()
                norm_params(k, d, d["stats"], [t], aggregate=lay != 2)
            x = y
        k.play()


def _rel_index():
    q = np.arange(256)
    o, cb, r, c = np.meshgrid(np.arange(4), np.arange(2), np.arange(8), np.arange(16), indexing="ij")
    rk, ck = (8 * o + r).ravel(), (16 * cb + c).ravel()
    rq, cq = 8 + q // 32, q % 32
    return (47 * (rq[:, None] - rk + 23) + cq[:, None] - ck + 23) % (47 * 47)


def _lay(inputs):
    g = {n: np.asarray(a) for n, a in inputs.items()}
    f = np.float32
    I = {"x": np.ascontiguousarray(g["x"].transpose(3, 0, 1, 2).reshape(128, B, L))}
    for n in "qkvp":
        I["w" + n] = np.ascontiguousarray(g[f"L0_conv_W{n}"].T)
    I["b0"] = np.stack([g[f"L0_conv_b{n}"] for n in "qkvp"], 1)
    t = g["L0_conv_bias_table"].T[:, _rel_index()]
    I["rel"] = np.ascontiguousarray(t.reshape(4, 2, 128, 1024).transpose(2, 1, 0, 3).reshape(128, 8192))
    a = np.arange(128)
    I["grp"] = (a[:, None] // 4 == a // 4).astype(f) / 4
    I["ident"] = np.eye(128, dtype=f)
    I["avg"] = np.full((128, 128), 1 / 128, f)
    I["wf"] = np.ascontiguousarray(np.stack([g[f"L1_conv_w{n}"].transpose(0, 2, 3, 1) for n in (1, 2)])
                                   .reshape(2, 128, 4096))
    y, m = np.arange(128), np.arange(16)
    th = 2 * np.pi * ((y[:, None] * m) % 128) / 128
    n_ = 128 ** -0.5
    I["dft"] = (np.stack([np.sin(th), np.cos(th), -np.sin(th)], 2).reshape(128, 48) * n_).astype(f)
    w = np.where(m == 0, 1.0, 2.0) * n_
    I["idft"] = np.stack([w * np.cos(th), -w * np.sin(th)], 2).reshape(128, 32).T.astype(f)
    I["ff0"] = g["L1_conv_ff_w0"]
    I["ff1"] = g["L1_conv_ff_w1"].reshape(4, 128, 128).transpose(1, 0, 2).reshape(128, 512)
    I["b1"] = np.concatenate([g["L1_conv_ff_b0"].reshape(4, 128).T] +
                             [g["L1_conv_" + n][:, None] for n in ("ff_b1", "ln_g", "ln_b")], 1)
    I["wg"] = np.concatenate([g[f"L2_conv_W{n}"] for n in "fid"], 1)
    bg = [g[f"L2_conv_b{n}"][64 * h:64 * h + 64] for n in "fid" for h in range(2)]
    I["bg"] = np.stack([np.concatenate([v, v]) for v in bg], 1)
    kern = np.zeros((128, 4, 2, 64), f)
    for i, n in enumerate("AB"):
        re, im = (g[f"L2_conv_{n}_{p}"].reshape(64, 49).T[:, None, :] for p in ("real", "imag"))
        kern[0:49, i], kern[64:113, i] = re, im
        kern[0:49, 2 + i], kern[64:113, 2 + i] = im, re
    I["kern"] = kern.reshape(128, 512)
    p, q = np.arange(49) // 7, np.arange(49) % 7
    u = np.arange(128)
    ph = (u[None, :, None] * (60 + p)[:, None, None] + u[None, None, :] * (60 + q)[:, None, None]) % 128
    ph = (2 * np.pi * ph / 128).reshape(49, L)
    basis = np.zeros((128, L), f)
    basis[0:49], basis[64:113] = np.cos(ph), np.sin(ph)
    I["basis"] = basis
    win = g["L3_conv_W_in"].T
    I["winx"], I["winz"] = win[:, 0:256], win[:, 256:512]
    I["convw"] = g["L3_conv_conv_w"].reshape(256, 9).T.reshape(2304)
    half = lambda v: v.reshape(2, 128, *v.shape[1:])
    I["convb"] = half(g["L3_conv_conv_b"]).T
    xp = g["L3_conv_x_proj_w"].transpose(0, 2, 1)
    xp = np.concatenate([xp[:, :, 8:40]] * 3 + [xp[:, :, 0:8]], 2)
    I["xproj"] = xp.reshape(4, 2, 128, 104).transpose(0, 2, 1, 3).reshape(4, 128, 208)
    I["dtw"] = g["L3_conv_dt_proj_w"].transpose(0, 2, 1)
    par = np.concatenate([g["L3_conv_A_logs"].reshape(4, 256, 16), g["L3_conv_dt_proj_b"].reshape(4, 256, 1),
                          g["L3_conv_Ds"].reshape(4, 256, 1)], 2)
    I["par"] = par.reshape(4, 2, 128, 18).transpose(0, 2, 1, 3).reshape(4, 128, 36)
    sel = np.zeros((128, 32, 128), mybir.dt.np(BF16))
    for r in range(32):
        sel[[r, 32 + r, 64 + r], r, :] = 1
    I["sel"] = sel.reshape(128, 4096)
    I["lnp"] = np.stack([half(g["L3_conv_ln_w"]), half(g["L3_conv_ln_b"])], 2).transpose(1, 0, 2).reshape(128, 4)
    I["wout"] = g["L3_conv_W_out"].T.reshape(2, 128, 128).transpose(1, 0, 2).reshape(128, 256)
    return I


def _build(nc, arrays, layers=(0, 1, 2, 3)):
    I = {n[3:]: nc.dram_tensor(n, a.shape, mybir.dt.from_np(a.dtype), kind="ExternalInput").ap()
         for n, a in arrays.items()}
    out = nc.dram_tensor("out_dram", (128, B, L), F32, kind="ExternalOutput").ap()
    scratch = [nc.dram_tensor(f"scr{i}", (128, B, L), F32).ap() for i in range(2)]
    program(nc, I, I["x"], scratch, out, layers)


def kernel(**inputs):
    import concourse.bacc as _bacc
    from concourse.bass_utils import run_bass_kernel_spmd as _run

    arrays = {f"in_{n}": np.ascontiguousarray(a) for n, a in _lay(inputs).items()}
    nc = _bacc.Bacc("TRN2", target_bir_lowering=False, num_devices=1)
    _build(nc, arrays)
    r = _run(nc, [arrays], core_ids=[0])
    return np.ascontiguousarray(r.results[0]["out_dram"].reshape(128, B, HW, HW).transpose(1, 2, 3, 0))
```

```python
from contextlib import ExitStack

import numpy as np
import concourse.bass as bass
from concourse import mybir

F32 = mybir.dt.float32
BF16 = mybir.dt.bfloat16
ALU = mybir.AluOpType
ACT = mybir.ActivationFunctionType
AXX = mybir.AxisListType.X

B, HW, C = 2, 128, 128
L = HW * HW
EPS = 1e-5


class Lane:

    def __init__(self, sem):
        self.sem, self.items, self.first = sem, [], []
        self.linked = False

    def do(self, fn, *args, after=(), **kw):
        if self.linked and self.items:
            after = [*after, (self, len(self.items) - 1)]
        self.items.append([fn, args, kw, [*self.first, *after], False])
        self.first = []
        return (self, len(self.items) - 1)

    def number(self):
        self.count, n = [], 0
        for it in self.items:
            n += it[4]
            self.count.append(n)

    def play(self, eng):
        seen = {}
        for fn, args, kw, after, marked in self.items:
            need = {}
            for src, at in after:
                v = src.count[at] if isinstance(src, Lane) else at
                if v > need.get(src, 0):
                    need[src] = v
            for src, v in need.items():
                if v > seen.get(src, 0):
                    eng.wait_ge(src.sem, v)
                    seen[src] = v
            if fn is None:
                continue
            ins = fn(*args, **kw)
            if marked:
                ins.then_inc(self.sem, 1)


class Chan:

    def __init__(self, sem):
        self.sem, self.n = sem, 0


class Ring:

    def __init__(self, bufs):
        self.bufs, self.n = bufs, 0
        self.held = [[] for _ in bufs]

    def take(self):
        i = self.n % len(self.bufs)
        self.n += 1
        w, self.held[i] = self.held[i], []
        return i, self.bufs[i], w


class Core:
    def __init__(self, nc, ctx):
        self.nc, self.ctx = nc, ctx
        self.lanes = {}
        for n in ("pe", "act", "dve", "pool", "sp"):
            self.lanes[n] = Lane(ctx.enter_context(nc.semaphore(f"s_{n}")))
        self.chans = []
        self.words = 51600
        self.mem = ctx.enter_context(nc.sbuf_tensor("mem", [128, self.words], F32))
        self.ps = ctx.enter_context(nc.psum_tensor("ps", [128, 8, 512], F32))
        self.low = self.top = 0
        self.nchan = 0

    def chan(self):
        self.nchan += 1
        c = Chan(self.ctx.enter_context(self.nc.semaphore(f"d{self.nchan}")))
        self.chans.append(c)
        return c

    def buf(self, *shape, dt=F32, parts=128):
        n = int(np.prod(shape))
        words = n if dt == F32 else (n + 1) // 2
        assert self.top + words <= self.words, (self.top, words)
        a = self.mem[0:parts, self.top:self.top + words]
        self.top += words
        if dt != F32:
            a = a.bitcast(dt)
        if len(shape) == 2:
            a = a.rearrange("p (a b) -> p a b", a=shape[0])
        elif len(shape) == 3:
            a = a.rearrange("p (a b c) -> p a b c", a=shape[0], b=shape[1])
        return a

    def dma(self, chan, out, in_, after=(), lane="sp"):
        ln = self.lanes[lane]
        eng = {"sp": self.nc.sync, "pool": self.nc.gpsimd, "act": self.nc.scalar}[lane]
        chan.n += 16
        ln.do(lambda o=out, i=in_, s=chan.sem, e=eng: e.dma_start(o, i).then_inc(s, 16), after=after)
        return (chan, chan.n)

    def phase(self):
        ends = [(ln, len(ln.items) - 1) for ln in self.lanes.values()
                if ln.items and ln is not self.lanes["sp"]]
        ends += [(c, c.n) for c in self.chans if c.n]
        for ln in self.lanes.values():
            ln.first = list(ends)
        self.top = self.low

    def play(self):
        for ln in self.lanes.values():
            for it in ln.items:
                for src, at in it[3]:
                    if isinstance(src, Lane):
                        src.items[at][4] = True
        ends = [(c, c.n) for c in self.chans if c.n]
        self.lanes["sp"].do(None, after=ends)
        for ln in self.lanes.values():
            ln.number()
        with self.nc.Block() as block:
            @block.tensor
            def _(e):
                self.lanes["pe"].play(e)

            @block.scalar
            def _(e):
                self.lanes["act"].play(e)

            @block.vector
            def _(e):
                self.lanes["dve"].play(e)

            @block.gpsimd
            def _(e):
                self.lanes["pool"].play(e)

            @block.sync
            def _(e):
                self.lanes["sp"].play(e)


def norm_params(k, d, stats, ready, aggregate=True):
    nc, V, S, T = k.nc, k.lanes["dve"], k.lanes["act"], k.lanes["pe"]
    mv, sm = d["mv"], d["sm"]
    t = ready[0]
    for b in range(B) if aggregate else ():
        t = V.do(nc.vector.bn_aggr, mv[:, b, :], stats[:, b, :], after=ready)
    p = k.ps[:, 0, 0:2]
    t = T.do(nc.tensor.matmul, p, d["grp"], mv[:, :, 0], start=True, stop=True, after=[t, d["t_const"]])
    t = V.do(nc.vector.tensor_copy, sm[:, 0:2], p, after=[t])
    t = V.do(nc.vector.tensor_tensor, sm[:, 2:4], mv[:, :, 0], sm[:, 0:2], ALU.subtract, after=[t])
    t = V.do(nc.vector.tensor_tensor, sm[:, 4:6], sm[:, 2:4], sm[:, 2:4], ALU.mult, after=[t])
    t = V.do(nc.vector.tensor_tensor, sm[:, 6:8], sm[:, 4:6], mv[:, :, 1], ALU.add, after=[t])
    t = T.do(nc.tensor.matmul, p, d["grp"], sm[:, 6:8], start=True, stop=True, after=[t])
    t = V.do(nc.vector.tensor_scalar, sm[:, 2:4], p, EPS, None, ALU.add, after=[t])
    t = S.do(nc.scalar.activation, sm[:, 4:6], sm[:, 2:4], ACT.Sqrt, after=[t])
    t = V.do(nc.vector.reciprocal, d["rs"], sm[:, 4:6], after=[t])
    t = V.do(nc.vector.scalar_tensor_tensor, out=d["nb"], in0=sm[:, 0:2], scalar=-1.0, in1=d["rs"],
             op0=ALU.mult, op1=ALU.mult, after=[t])
    return t


def first_stats(k, d, xin):
    nc, V = k.nc, k.lanes["dve"]
    ring = Ring([k.buf(4096) for _ in range(4)])
    ch = [k.chan() for _ in range(4)]
    t = None
    for b in range(B):
        for n in range(4):
            i, x, w = ring.take()
            ld = k.dma(ch[i], x, xin[:, b, n * 4096:(n + 1) * 4096], after=w)
            for j in range(8):
                t = V.do(nc.vector.bn_stats, d["stats"][:, b, (n * 8 + j) * 6:(n * 8 + j) * 6 + 6],
                         x[:, j * 512:(j + 1) * 512], after=[ld])
            ring.held[i] = [t]
    return t


def layer0(k, d, I, xin, xout):
    nc = k.nc
    V, S, T = k.lanes["dve"], k.lanes["act"], k.lanes["pe"]
    ps = k.ps
    c0 = k.chan()
    wq, wk, wv, wp = [k.buf(128) for _ in range(4)]
    rel = k.buf(2, 4, 1024)
    for t_, n in ((wq, "wq"), (wk, "wk"), (wv, "wv"), (wp, "wp")):
        k.dma(c0, t_, I[n])
    bv4 = k.buf(5)
    tw = k.dma(c0, bv4[:, 0:4], I["b0"])
    tb = k.dma(k.chan(), rel, I["rel"].rearrange("p (a b c) -> p a b c", a=2, b=4))
    tq = S.do(nc.scalar.mul, bv4[:, 4:5], bv4[:, 0:1], 32 ** -0.5, after=[tw])
    scale = 32 ** -0.5
    stats = d["stats2"]

    NO = 6
    raw = [k.buf(8, 128) for _ in range(NO)]
    Kb = [k.buf(9 * 128) for _ in range(NO)]
    Vb = [k.buf(9, 128) for _ in range(NO)]
    Qb = [k.buf(8, 128) for _ in range(NO)]
    xnr = Ring([k.buf(9, 8, 16) for _ in range(2)])
    chr_ = [k.chan() for _ in range(NO)]
    held = [[] for _ in range(NO)]
    Tr = Ring([k.buf(1024) for _ in range(2)])
    Pr = Ring([k.buf(1024) for _ in range(3)])
    PTr = Ring([k.buf(1024) for _ in range(2)])
    mx = k.buf(4, 4)
    outr = Ring([k.buf(16, 128) for _ in range(2)])
    cho = [k.chan() for _ in range(2)]
    Osb = Ring([k.buf(128) for _ in range(2)])
    OT = Ring([k.buf(256) for _ in range(2)])
    rsum = Ring([k.buf(4) for _ in range(4)])
    rinv = Ring([k.buf(4) for _ in range(4)])
    Sp = Ring([ps[:, 0:2, :].rearrange("p a b -> p (a b)"), ps[:, 2:4, :].rearrange("p a b -> p (a b)")])
    PTp = Ring([ps[:, 4:6, :].rearrange("p a b -> p (a b)")])
    misc = Ring([ps[:, 6, :], ps[:, 7, :]])
    octs = {}
    loads = {}

    def load_oct(b, o):
        i = (b * 18 + o) % NO
        r0 = 1 if o == 0 else 119 if o == 17 else 8 * o - 8
        w, held[i] = held[i], []
        loads[b, o] = k.dma(chr_[i], raw[i].rearrange("p a b -> p (a b)"),
                            xin[:, b, r0 * 128:(r0 + 8) * 128], after=w)

    def make_oct(b, o):
        i = (b * 18 + o) % NO
        ld = loads.pop((b, o))
        j, xn, w = xnr.take()
        src = raw[i][:, ::-1, :] if o in (0, 17) else raw[i]
        cen = src.rearrange("p r (a c) -> p r a c", c=8)
        x4 = xn.rearrange("p cb r (h c) -> p r cb h c", h=2)
        rs, nb = d["rs"][:, b:b + 1], d["nb"][:, b:b + 1]
        ts = []
        for r in range(2):
            dst = x4[:, :, 1:9, 0, :] if r == 0 else x4[:, :, 0:8, 1, :]
            sr = cen[:, :, 1::2, :] if r == 0 else cen[:, :, 0::2, :]
            ts.append(S.do(nc.scalar.activation, dst, sr, ACT.Identity, bias=nb, scale=rs,
                           after=[ld, *w]))
        ts.append(S.do(nc.scalar.activation, x4[:, :, 0, 0, :], src[:, :, 8:0:-1], ACT.Identity,
                       bias=nb, scale=rs))
        ts.append(S.do(nc.scalar.activation, x4[:, :, 8, 1, :], src[:, :, 126:118:-1], ACT.Identity,
                       bias=nb, scale=rs))
        tk = []
        xf = xn.rearrange("p a r c -> p a (r c)")
        for c3 in range(3):
            m, p, w = Sp.take()
            t = T.do(nc.tensor.matmul, p[:, 0:384], wk, xf[:, 3 * c3:3 * c3 + 3, :].rearrange("p a b -> p (a b)"),
                     start=True, stop=True, after=[*w, ts[-1], tw])
            t = S.do(nc.scalar.activation, Kb[i][:, 384 * c3:384 * c3 + 384], p[:, 0:384], ACT.Identity,
                     bias=bv4[:, 1:2], after=[t])
            Sp.held[m] = [t]
            tk.append(t)
        for c3 in range(3):
            m, p, w = Sp.take()
            for a in range(3):
                t = T.do(nc.tensor.matmul, p[:, a * 128:(a + 1) * 128], xf[:, 3 * c3 + a, :], wv,
                         start=True, stop=True, after=w)
            t = V.do(nc.vector.tensor_copy, Vb[i][:, 3 * c3:3 * c3 + 3, :].rearrange("p a b -> p (a b)"), p[:, 0:384],
                     after=[t])
            Sp.held[m] = [t]
            tk.append(t)
        if 1 <= o <= 16:
            xo = k.nc
            for c4 in range(2):
                m, p, w = Sp.take()
                for a in range(4):
                    wj = 4 * c4 + a
                    for hh in range(2):
                        dst = p[:, a * 128:(a + 1) * 128].rearrange("p (r c) -> p r c", r=8)[:, :, 8 * hh:8 * hh + 8]
                        sr = xn[:, wj, :, 8:16] if hh == 0 else xn[:, wj + 1, :, 0:8]
                        t = T.do(nc.tensor.matmul, dst, wq, sr, start=True, stop=True, after=w)
                t = S.do(nc.scalar.activation, Qb[i][:, 4 * c4:4 * c4 + 4, :].rearrange("p a b -> p (a b)"), p[:, 0:512],
                         ACT.Identity, bias=bv4[:, 4:5], scale=scale, after=[t, tq])
                Sp.held[m] = [t]
                tk.append(t)
        xnr.held[j] = [t for t in tk]
        octs[b, o] = (i, tk)

    units = [(b, wi, wj, t, h) for b in range(B) for wi in range(8) for wj in range(8)
             for t in range(2) for h in range(4)]
    st = {}
    win = {}
    rows = {}

    def stage_a(n):
        b, wi, wj, t, h = units[n]
        if wj == 0 and t == 0 and h == 0:
            if wi == 0:
                for o in range(4):
                    load_oct(b, o)
                for o in range(4):
                    make_oct(b, o)
            else:
                for o in (2 * wi + 2, 2 * wi + 3):
                    make_oct(b, o)
        if wi < 7 and t == 0 and h == 0 and wj == 2:
            for o in (2 * wi + 4, 2 * wi + 5):
                load_oct(b, o)
        i, s, w = Sp.take()
        qi, qt = octs[b, 2 * wi + 1 + t]
        for o in range(4):
            ki, kt = octs[b, 2 * wi + o]
            tt = T.do(nc.tensor.matmul, s[:, o * 256:(o + 1) * 256], Qb[qi][32 * h:32 * h + 32, wj, :],
                      Kb[ki][32 * h:32 * h + 32, wj * 128:wj * 128 + 256], start=True, stop=True,
                      after=[*w, *qt, *kt])
        j, tl, w = Tr.take()
        m = n % 4
        mxc = mx[:, m, :]
        wm = st[n - 4]["exp"] if n >= 4 else None
        tm = V.do(nc.vector.tensor_tensor_reduce, tl, s, rel[:, t, h, :], 1.0, -3.0e38, ALU.add, ALU.max,
                  mxc[:, 0:1], after=[tt, tb, *w, *([wm] if wm else [])])
        Sp.held[i] = [tm]
        tn = V.do(nc.vector.tensor_scalar, mxc[:, 1:2], mxc[:, 0:1], -1.0, None, ALU.mult, after=[tm])
        st[n] = {"tn": tn, "T": (j, tl), "m": mxc}
        if h == 0:
            ri, r, w = rsum.take()
            win[b, wi, wj, t] = {"rs": (ri, r), "rw": w}
        st[n]["win"] = win[b, wi, wj, t]

    def stage_b(n):
        b, wi, wj, t, h = units[n]
        u = st[n]
        j, tl = u["T"]
        pi, p, w = Pr.take()
        ri, r = u["win"]["rs"]
        te = S.do(nc.scalar.activation, p, tl, ACT.Exp, bias=u["m"][:, 1:2], scale=1.0,
                  accum_out=r[:, h:h + 1], after=[u["tn"], *w, *u["win"]["rw"]])
        Tr.held[j] = [te]
        u["exp"], u["P"] = te, (pi, p)

    def stage_c(n):
        u = st[n]
        pi, p = u["P"]
        i, q, w = PTp.take()
        j, pt, w2 = PTr.take()
        for g in range(8):
            tt = T.do(nc.tensor.transpose, q[:, g * 128:(g + 1) * 128], p[:, g * 128:(g + 1) * 128],
                      d["ident"], after=[u["exp"], *w, d["t_const"]])
            if g == 3:
                t1 = V.do(nc.vector.tensor_copy, pt[:, 0:512], q[:, 0:512], after=[tt, *w2])
        t2 = S.do(nc.scalar.copy, pt[:, 512:1024], q[:, 512:1024], after=[tt, *w2])
        Pr.held[pi] = [tt]
        PTp.held[i] = [t1, t2]
        u["PT"] = (j, pt, [t1, t2])

    def stage_d(n):
        b, wi, wj, t, h = units[n]
        u = st[n]
        j, pt, ready = u["PT"]
        wn = u["win"]
        if h == 0:
            wn["O"] = misc.take()
        m, o_, w = wn["O"]
        for g in range(8):
            ki, kt = octs[b, 2 * wi + g // 2]
            tt = T.do(nc.tensor.matmul, o_[:, 32 * h:32 * h + 32], pt[:, g * 128:(g + 1) * 128],
                      Vb[ki][:, wj + g % 2, 32 * h:32 * h + 32], start=(g == 0), stop=(g == 7),
                      after=[*ready, *w, *kt])
        PTr.held[j] = [tt]
        if h == 3:
            ri, r = wn["rs"]
            vi, rv, w = rinv.take()
            t1 = V.do(nc.vector.reciprocal, rv, r, after=[u["exp"], *w])
            rsum.held[ri] = [t1]
            oi, ob, w = Osb.take()
            t2 = V.do(nc.vector.tensor_tensor, ob.rearrange("p (h x) -> p h x", h=4),
                      o_[:, 0:128].rearrange("p (h x) -> p h x", h=4),
                      rv.unsqueeze(2).broadcast_to([128, 4, 32]), ALU.mult, after=[t1, tt, *w])
            rinv.held[vi] = [t2]
            wn["fin"] = (m, o_, oi, ob, t2)
        if h == 3 and wj == 7 and t == 1:
            for o in (2 * wi, 2 * wi + 1) if wi < 7 else range(14, 18):
                held[octs[b, o][0]].append(tt)

    def stage_e(n):
        b, wi, wj, t, h = units[n]
        if h != 3:
            return
        wn = st[n]["win"]
        m, o_, oi, ob, t2 = wn["fin"]
        tt = T.do(nc.tensor.transpose, o_[:, 128:256], ob, d["ident"], after=[t2])
        Osb.held[oi] = [tt]
        if t == 0:
            win[b, wi, wj] = OT.take()
        ti, ot, w = win[b, wi, wj]
        t3 = S.do(nc.scalar.activation, ot[:, 128 * t:128 * t + 128], o_[:, 128:256], ACT.Identity,
                  bias=bv4[:, 2:3], after=[tt, *w])
        misc.held[m] = [t3]
        if t == 1:
            m, p, w = misc.take()
            tt = T.do(nc.tensor.matmul, p[:, 0:256], wp, ot, start=True, stop=True, after=[*w, t3])
            OT.held[ti] = [tt]
            if wj == 0:
                rows[b, wi] = outr.take()
            oi, ob, w = rows[b, wi]
            for tt_ in range(2):
                ri = octs[b, 2 * wi + 1 + tt_][0]
                t4 = V.do(nc.vector.scalar_tensor_tensor, out=ob[:, 8 * tt_:8 * tt_ + 8, 16 * wj:16 * wj + 16],
                          in0=p[:, 128 * tt_:128 * tt_ + 128].rearrange("p (r c) -> p r c", r=8), scalar=bv4[:, 3:4],
                          in1=raw[ri][:, :, 16 * wj:16 * wj + 16], op0=ALU.add, op1=ALU.add, after=[tt, *w])
            misc.held[m] = [t4]
            if wj == 7:
                of = ob.rearrange("p a b -> p (a b)")
                for q in range(4):
                    at = (wi * 4 + q) * 6
                    t5 = V.do(nc.vector.bn_stats, stats[:, b, at:at + 6], of[:, q * 512:(q + 1) * 512], after=[t4])
                ds = k.dma(cho[oi], xout[:, b, wi * 2048:(wi + 1) * 2048], of, after=[t4])
                outr.held[oi] = [t5, ds]
                d["t_stats"] = t5
                for o in (2 * wi, 2 * wi + 1) if wi < 7 else range(14, 18):
                    held[octs[b, o][0]].append(t4)

    N = len(units) // B
    for b in range(B):
        for s in range(N + 3):
            for lag, f in ((0, stage_a), (0, stage_b), (1, stage_c), (3, stage_e), (2, stage_d)):
                if 0 <= s - lag < N:
                    f(b * N + s - lag)
    return d["t_stats"]


def layer1(k, d, I, xin, xout):
    nc = k.nc
    V, S, T, G_ = k.lanes["dve"], k.lanes["act"], k.lanes["pe"], k.lanes["pool"]
    ps = k.ps
    stats = d["stats2"]
    xn = k.buf(128, 128)
    hs = k.buf(128, 128)
    W = k.buf(16, 2, 128)
    F = k.buf(16, 3, 128)
    Gm = k.buf(128, 16, 2)
    XT = Ring([k.buf(4, 128) for _ in range(2)])
    gT = Ring([k.buf(4, 128, parts=32) for _ in range(2)])
    dft = k.buf(48)
    idft = k.buf(128, parts=32)
    sm = k.buf(8)
    c0, cw = k.chan(), k.chan()
    k.dma(c0, dft, I["dft"])
    k.dma(c0, sm[:, 0:7], I["b1"])
    t_c = k.dma(c0, idft, I["idft"])
    Ff = F.rearrange("p a b c -> p (a b) c")
    xf = xn.rearrange("p a b -> p (a b)")
    hf = hs.rearrange("p a b -> p (a b)")
    at = [0]

    def over(n):
        at[0] += n
        return xf[:, at[0] - n:at[0]]

    w0 = over(512)
    w1 = over(512).rearrange("p (a b) -> p a b", a=4)
    h1r = Ring([over(2048).rearrange("p (a b) -> p a b", a=4) for _ in range(2)])
    h2r = Ring([over(512) for _ in range(2)])
    ddr = Ring([over(512) for _ in range(4)])
    sqr = Ring([over(512) for _ in range(2)])
    sdr = Ring([over(512) for _ in range(2)])
    yr = Ring([over(512) for _ in range(2)])
    xr = Ring([over(512) for _ in range(4)])
    outr = Ring([over(512) for _ in range(3)])
    cx = [k.chan() for _ in range(4)]
    cin = [k.chan() for _ in range(4)]
    cxr = [k.chan() for _ in range(4)]
    co = [k.chan() for _ in range(3)]
    cf = k.chan()
    w_free, x_free = [], []
    t_stat = None
    bank = [ps[:, i, :] for i in range(8)]
    XTp = op = Ring(bank[0:2])
    Fp, Gp, gp = Ring(bank[2:4]), Ring(bank[4:6]), Ring(bank[6:8])

    for b in range(B):
        rs, nb = d["rs"][:, b:b + 1], d["nb"][:, b:b + 1]
        tx = []
        for q in range(4):
            ld = k.dma(cin[q], xf[:, q * 4096:(q + 1) * 4096], xin[:, b, q * 4096:(q + 1) * 4096], after=x_free)
            for e, (ln, eng) in enumerate(((S, "a"), (V, "v"))):
                part = xf[:, q * 4096 + e * 2048:q * 4096 + (e + 1) * 2048]
                if eng == "a":
                    tx.append(S.do(nc.scalar.activation, part, part, ACT.Identity, bias=nb, scale=rs, after=[ld]))
                else:
                    tx.append(V.do(nc.vector.tensor_scalar, part, part, rs, nb, ALU.mult, ALU.add, after=[ld]))
        t_hs = []
        for dr in range(2):
            tw = k.dma(cw, W.rearrange("p a b c -> p (a b c)"), I["wf"][dr], after=w_free)
            tF = []
            pend = []
            slot = [None]

            def dft_mms(g, xi, xt, t_ev):
                if g % 2 == 0:
                    slot[0] = Fp.take()
                i, p, w = slot[0]
                for j in range(4):
                    c = (g % 2) * 4 + j
                    tt = T.do(nc.tensor.matmul, p[:, c * 48:(c + 1) * 48], xt[:, j, :], dft,
                              start=True, stop=True, after=[*w, t_ev, t_c])
                XT.held[xi] = [tt]
                if g % 2 == 1:
                    ev = V.do(nc.vector.tensor_copy, Ff[:, :, 4 * g - 4:4 * g + 4],
                              p[:, 0:384].rearrange("p (l k) -> p k l", l=8), after=[tt, *t_hs])
                    Fp.held[i] = [ev]
                    tF.append(ev)

            for g in range(32):
                i, p, w = XTp.take()
                for j in range(4):
                    ln_ = 4 * g + j
                    src = xn[:, ln_, :] if dr == 0 else xn[:, :, ln_]
                    tt = T.do(nc.tensor.transpose, p[:, j * 128:(j + 1) * 128], src, d["ident"],
                              after=[*w, *(tx if dr else tx[0:2 * (g // 8) + 2])])
                xi, xt, w2 = XT.take()
                ev = S.do(nc.scalar.copy, xt.rearrange("p a b -> p (a b)"), p, after=[tt, *w2])
                XTp.held[i] = [ev]
                pend.append((g, xi, xt, ev))
                if len(pend) > 1:
                    dft_mms(*pend.pop(0))
            dft_mms(*pend.pop(0))
            x_last = tt
            tG = []
            for ky in range(16):
                i, p, w = Gp.take()
                o_ = p[:, 0:256]
                T.do(nc.tensor.matmul, o_, W[:, ky, 0, :], F[:, ky, 1:3, :].rearrange("p a b -> p (a b)"),
                     start=True, stop=False, after=[*w, tw, tF[-1]])
                tt = T.do(nc.tensor.matmul, o_, W[:, ky, 1, :], F[:, ky, 0:2, :].rearrange("p a b -> p (a b)"),
                          start=False, stop=True)
                src = o_.rearrange("p (r l) -> p l r", r=2)
                if ky % 2:
                    ev = V.do(nc.vector.tensor_copy, Gm[:, :, ky, :], src, after=[tt])
                else:
                    ev = S.do(nc.scalar.copy, Gm[:, :, ky, :], src, after=[tt])
                Gp.held[i] = [ev]
                tG.append(ev)
            w_free = [tt]
            pend = []

            def inverse(g, gi, gt, t_ev):
                i, p, w = op.take()
                for j in range(4):
                    tt = T.do(nc.tensor.matmul, p[:, j * 128:(j + 1) * 128], gt[:, j, :], idft,
                              start=True, stop=True, after=[*w, t_ev])
                gT.held[gi] = [tt]
                if dr == 0:
                    ev = V.do(nc.vector.tensor_copy, hf[:, g * 512:(g + 1) * 512], p, after=[tt, *hs_free])
                else:
                    o_ = hs[:, :, 4 * g:4 * g + 4]
                    ev = V.do(nc.vector.tensor_tensor, o_, p.rearrange("p (w h) -> p h w", w=4), o_, ALU.add,
                              after=[tt, *t_hs])
                op.held[i] = [ev]
                last[0] = ev

            hs_free = x_free
            last = [None]
            for g in range(32):
                i, p, w = gp.take()
                for j in range(4):
                    tt = T.do(nc.tensor.transpose, p[0:32, j * 128:(j + 1) * 128],
                              Gm[:, 4 * g + j, :, :].rearrange("p a b -> p (a b)"), d["ident"],
                              after=[*w, tG[-1], tG[-2]])
                gi, gt, w2 = gT.take()
                ev = S.do(nc.scalar.copy, gt.rearrange("p a b -> p (a b)"), p[0:32, :], after=[tt, *w2])
                gp.held[i] = [ev]
                pend.append((g, gi, gt, ev))
                if len(pend) > 1:
                    inverse(*pend.pop(0))
            inverse(*pend.pop(0))
            t_hs = [last[0], tt]

        k.dma(cf, w0, I["ff0"], after=[x_last])
        tf = k.dma(cf, w1.rearrange("p a b -> p (a b)"), I["ff1"], after=[x_last])
        h1p, h2p, mp = Ring(bank[0:3]), Ring(bank[3:5]), Ring(bank[5:8])
        u = {n: {} for n in range(32)}
        start = [*op.held[0], *op.held[1], *gp.held[0], *gp.held[1], x_last, t_hs[0]]

        def f0(n):
            i, x, w = xr.take()
            u[n]["x"] = (i, x, k.dma(cxr[i], x, xin[:, b, n * 512:(n + 1) * 512], after=[*w, x_last]))

        def f1(n):
            hi, h1, w1_ = h1r.take()
            for m in range(4):
                i, p, w = h1p.take()
                tt = T.do(nc.tensor.matmul, p, w0[:, m * 128:(m + 1) * 128], hf[:, n * 512:(n + 1) * 512],
                          start=True, stop=True, after=[*w, tf, *start])
                if m < 3:
                    ev = S.do(nc.scalar.activation, h1[:, m, :], p, ACT.Relu, bias=sm[:, m:m + 1],
                              after=[tt, *w1_, t_c])
                else:
                    ev = V.do(nc.vector.tensor_scalar, h1[:, m, :], p, sm[:, m:m + 1], 0.0, ALU.add, ALU.max,
                              after=[tt, *w1_, t_c])
                h1p.held[i] = [ev]
                u[n][f"part{m}"] = ev
            u[n]["h1"] = (hi, h1)
            u[n]["rhs"] = tt

        def f2(n):
            hi, h1 = u[n]["h1"]
            i, p, w = h2p.take()
            for m in range(4):
                tt = T.do(nc.tensor.matmul, p, w1[:, m, :], h1[:, m, :], start=(m == 0), stop=(m == 3),
                          after=[*w, u[n][f"part{m}"]])
            h1r.held[hi] = [tt]
            j, h2, w2 = h2r.take()
            ev = S.do(nc.scalar.activation, h2, p, ACT.Identity, bias=sm[:, 4:5], after=[tt, *w2])
            h2p.held[i] = [ev]
            u[n]["h2"] = (j, h2, ev)

        def f3(n):
            j, h2, ev = u[n]["h2"]
            i, p, w = mp.take()
            tt = T.do(nc.tensor.matmul, p, d["avg"], h2, start=True, stop=True, after=[*w, ev])
            di, dd, w2 = ddr.take()
            t1 = V.do(nc.vector.tensor_tensor, dd, h2, p, ALU.subtract, after=[tt, ev, *w2])
            mp.held[i] = [t1]
            h2r.held[j] = [t1]
            qi, sq, w3 = sqr.take()
            t2 = S.do(nc.scalar.activation, sq, dd, ACT.Square, after=[t1, *w3])
            u[n]["dd"] = (di, dd, t1)
            u[n]["sq"] = (qi, sq, t2)

        def f4(n):
            qi, sq, t2 = u[n]["sq"]
            i, p, w = mp.take()
            tt = T.do(nc.tensor.matmul, p, d["avg"], sq, start=True, stop=True, after=[*w, t2])
            sqr.held[qi] = [tt]
            si, sd, w2 = sdr.take()
            t1 = V.do(nc.vector.tensor_scalar, sd, p, EPS, None, ALU.add, after=[tt, *w2])
            mp.held[i] = [t1]
            t2 = S.do(nc.scalar.activation, sd, sd, ACT.Sqrt, after=[t1])
            u[n]["sd"] = (si, sd, t2)

        def f5(n):
            si, sd, t2 = u[n]["sd"]
            di, dd, t1 = u[n]["dd"]
            yi, y, w = yr.take()
            t3 = V.do(nc.vector.reciprocal, sd, sd, after=[t2])
            t4 = V.do(nc.vector.tensor_tensor, y, dd, sd, ALU.mult, after=[t3, *w])
            sdr.held[si] = [t4]
            ddr.held[di] = [t4]
            t5 = V.do(nc.vector.tensor_scalar, y, y, sm[:, 5:6], sm[:, 6:7], ALU.mult, ALU.add, after=[t4])
            xi, x, tl = u[n]["x"]
            oi, o_, w = outr.take()
            t6 = G_.do(nc.gpsimd.tensor_tensor, o_, y, x, ALU.add, after=[t5, tl, *w])
            yr.held[yi] = [t6]
            xr.held[xi] = [t6]
            t7 = V.do(nc.vector.bn_stats, stats[:, b, n * 6:n * 6 + 6], o_, after=[t6])
            ds = k.dma(co[oi], xout[:, b, n * 512:(n + 1) * 512], o_, after=[t6])
            outr.held[oi] = [t7, ds]
            u[n]["end"] = [t6, t7, ds]

        for s in range(32 + 5):
            for lag, f in ((3, f0), (1, f1), (2, f2), (3, f3), (4, f4), (5, f5)):
                if 0 <= s - lag < 32:
                    f(s - lag)
        x_free = [c for n in (29, 30, 31) for c in u[n]["end"]] + [u[31]["rhs"]]
        t_stat = u[31]["end"][1]
    return t_stat


def layer2(k, d, I, xin, xout):
    nc = k.nc
    V, S, T, P = k.lanes["dve"], k.lanes["act"], k.lanes["pe"], k.lanes["pool"]
    stats = d["stats2"]
    N = 512
    WG = k.buf(3, 128)
    bg = k.buf(6)
    pk = k.buf(4)
    kern = k.buf(4, 128)
    nk = k.buf(2, 128)
    c0 = k.chan()
    k.dma(c0, WG.rearrange("p a b -> p (a b)"), I["wg"])
    k.dma(c0, bg, I["bg"])
    tc = k.dma(c0, kern.rearrange("p a b -> p (a b)"), I["kern"])
    t_k = V.do(nc.vector.tensor_copy, nk[0:64, :, :], kern[0:64, 2:4, :], after=[tc])
    t_k = V.do(nc.vector.tensor_scalar, nk[64:128, :, :], kern[64:128, 2:4, :], -1.0, None, ALU.mult, after=[tc])
    bank = [k.ps[:, i, :] for i in range(8)]
    V.linked = P.linked = True
    for b in range(B):
        for h in range(2):
            for j, s_ in enumerate((d["rs"], d["nb"])):
                t = T.do(nc.tensor.matmul, bank[0][64 * b:64 * b + 64, 2 * h + j:2 * h + j + 1],
                         d["ident"][:, 64 * h:64 * h + 64], s_[:, b:b + 1], start=True, stop=True, after=[tc])
    t_pk = V.do(nc.vector.tensor_copy, pk, bank[0][:, 0:4], after=[t])
    t_bg = V.do(nc.vector.tensor_scalar, bg[:, 0:2], bg[:, 0:2], 2.0, None, ALU.add, after=[tc])

    sets = []
    names2 = ("xp", "q2", "A", "f", "g", "e", "sp", "w2", "res")
    names1 = ("m2", "sg", "m11", "p12", "m21", "m22", "tau", "del", "u1", "u2", "u3", "u4", "u5",
              "a1", "b1", "a2", "b2", "p1", "p2")
    for _ in range(2):
        s = {n: k.buf(2, N) for n in names2}
        s.update({n: k.buf(N) for n in names1})
        s["xc"] = k.buf(2, N)
        s["bas"] = k.buf(N)
        s["ch"] = [k.chan() for _ in range(4)]
        sets.append(s)
    outs = Ring([k.buf(2, N) for _ in range(2)])
    couts = [k.chan() for _ in range(2)]
    done = [[], []]
    sr4, pr = bank[0:4], Ring(bank[4:8])
    sr_held = [[] for _ in range(4)]
    NC = L // N
    loads = {}

    def load(n):
        s, fr = sets[n % 2], done[n % 2]
        sl = slice(n * N, (n + 1) * N)
        c = s["ch"]
        t0 = k.dma(c[0], s["bas"], I["basis"][:, sl], after=fr)
        t1 = k.dma(c[1], s["xc"], xin[:, :, sl], after=fr)
        for b in range(B):
            for h in range(2):
                t2 = k.dma(c[2], s["xp"][64 * b:64 * b + 64, h, :], xin[64 * h:64 * h + 64, b, sl], after=fr)
        for b in range(B):
            for h in range(2):
                t3 = k.dma(c[3], s["res"][64 * b:64 * b + 64, h, :], xin[64 * h:64 * h + 64, b, sl], after=fr)
        loads[n] = (t0, t1, t2, t3)

    load(0)
    for n in range(NC):
        s, fr = sets[n % 2], done[n % 2]
        t_bas, t_xc, t_xp, tr = loads.pop(n)
        t = {}
        for ln in (V, S, T, P):
            ln.first = ln.first + list(fr)
        sp = {}
        for i, (nm, w) in enumerate((("Ar", kern[:, 0, :]), ("Ai", nk[:, 0, :]), ("Br", kern[:, 1, :]),
                                     ("Bi", nk[:, 1, :]))):
            p, wt = sr4[i], sr_held[i]
            sp[nm] = (i, p)
            t[nm] = T.do(nc.tensor.matmul, p, w, s["bas"], start=True, stop=True, after=[*wt, t_bas, t_k, t_pk])
        for b in range(B):
            t["xc"] = S.do(nc.scalar.activation, s["xc"][:, b, :], s["xc"][:, b, :], ACT.Identity,
                           bias=d["nb"][:, b:b + 1], scale=d["rs"][:, b:b + 1], after=[t_xc])
        S.do(nc.scalar.activation, s["q2"][:, 0, :], sp["Ar"][1], ACT.Square, after=[t["Ar"]])
        t["q2"] = S.do(nc.scalar.activation, s["q2"][:, 1, :], sp["Ai"][1], ACT.Square, after=[t["Ai"]])
        t["m2"] = V.do(nc.vector.scalar_tensor_tensor, out=s["m2"], in0=s["q2"][:, 0, :], scalar=1e-8,
                       in1=s["q2"][:, 1, :], op0=ALU.add, op1=ALU.add, after=[t["q2"]])
        t["mag"] = S.do(nc.scalar.activation, s["m2"], s["m2"], ACT.Sqrt, after=[t["m2"]])
        gates = {}
        for gi, gn in enumerate(("f", "g", "e")):
            for h in range(2):
                i, p, wt = pr.take()
                for b in range(B):
                    tt = T.do(nc.tensor.matmul, p[64 * b:64 * b + 64, :], WG[:, gi, 64 * h:64 * h + 64],
                              s["xc"][:, b, :], start=True, stop=True, after=[*wt, t["xc"]])
                if gn == "e":
                    ev = S.do(nc.scalar.activation, s["e"][:, h, :], p, ACT.Abs, bias=bg[:, 4 + h:5 + h], after=[tt])
                    ev2 = V.do(nc.vector.tensor_scalar, s["sp"][:, h, :], p, bg[:, 4 + h:5 + h], 0.0, ALU.add,
                               ALU.max, after=[tt, ev])
                    pr.held[i] = [ev, ev2]
                    t["relu"], t["abs"] = ev2, ev
                else:
                    ev = S.do(nc.scalar.activation, s[gn][:, h, :], p, ACT.Sigmoid,
                              bias=bg[:, 2 * gi + h:2 * gi + h + 1], after=[tt, t_bg])
                    pr.held[i] = [ev]
                    t[gn] = ev
        t["sg"] = S.do(nc.scalar.activation, s["sg"], s["m2"], ACT.Sigmoid, after=[t["mag"]])
        t["ex"] = S.do(nc.scalar.activation, s["e"], s["e"], ACT.Exp, scale=-1.0, after=[t["abs"]])
        t["ln"] = S.do(nc.scalar.activation, s["e"], s["e"], ACT.Ln, bias=1.0, after=[t["ex"]])
        for h in range(2):
            t["xp"] = S.do(nc.scalar.activation, s["xp"][:, h, :], s["xp"][:, h, :], ACT.Identity,
                           bias=pk[:, 2 * h + 1:2 * h + 2], scale=pk[:, 2 * h:2 * h + 1], after=[t_xp, t_pk])
        t["u1"] = V.do(nc.vector.tensor_scalar, s["u1"], s["m2"], 1e-8, None, ALU.add, after=[t["mag"], t["sg"]])
        t["u2"] = V.do(nc.vector.reciprocal, s["u2"], s["u1"], after=[t["u1"]])
        t["u3"] = V.do(nc.vector.scalar_tensor_tensor, out=s["u3"], in0=s["sg"], scalar=0.95, in1=s["u2"],
                       op0=ALU.mult, op1=ALU.mult, after=[t["u2"], t["sg"]])
        for h, nm in enumerate(("Ar", "Ai")):
            t["A"] = V.do(nc.vector.tensor_tensor, s["A"][:, h, :], s["u3"], sp[nm][1], ALU.mult, after=[t["u3"]])
            sr_held[sp[nm][0]] = [t["A"], t["q2"]]
        xr_, xi_ = s["xp"][:, 0, :], s["xp"][:, 1, :]
        V.do(nc.vector.tensor_tensor, s["p1"], xr_, sp["Br"][1], ALU.mult, after=[t["Br"], t["xp"]])
        t["p2"] = V.do(nc.vector.tensor_tensor, s["p2"], xi_, sp["Bi"][1], ALU.mult, after=[t["Bi"]])
        t["q0"] = V.do(nc.vector.tensor_tensor, s["q2"][:, 0, :], s["p1"], s["p2"], ALU.subtract, after=[t["p2"]])
        t["a1"] = V.do(nc.vector.tensor_tensor, s["a1"], xi_, sp["Br"][1], ALU.mult)
        t["b1"] = V.do(nc.vector.tensor_tensor, s["b1"], xr_, sp["Bi"][1], ALU.mult)
        sr_held[sp["Br"][0]] = [t["a1"]]
        sr_held[sp["Bi"][0]] = [t["b1"]]
        t["Bx"] = V.do(nc.vector.tensor_tensor, s["q2"][:, 1, :], s["a1"], s["b1"], ALU.add, after=[t["b1"]])
        t["sp"] = P.do(nc.gpsimd.tensor_tensor, s["sp"], s["sp"], s["e"], ALU.add, after=[t["relu"], t["ln"]])
        t["sg2"] = P.do(nc.gpsimd.tensor_tensor, s["sp"], s["sp"], s["g"], ALU.mult, after=[t["sp"], t["g"]])
        t["inp"] = V.do(nc.vector.scalar_tensor_tensor, out=s["sp"], in0=s["sp"], scalar=0.1, in1=s["q2"],
                        op0=ALU.mult, op1=ALU.mult, after=[t["sg2"], t["Bx"], t["q0"]])
        Ar, Ai, fr_, fi_ = s["A"][:, 0, :], s["A"][:, 1, :], s["f"][:, 0, :], s["f"][:, 1, :]

        def v(o, a, op, b_, *after):
            t[o] = V.do(nc.vector.tensor_tensor, s[o], s[a], s[b_], op, after=[t[x] for x in after])

        def g(o, a, op, b_, *after):
            t[o] = P.do(nc.gpsimd.tensor_tensor, s[o], s[a], s[b_], op, after=[t[x] for x in after])

        t["m11"] = V.do(nc.vector.tensor_tensor, s["m11"], fr_, Ar, ALU.mult, after=[t["A"], t["f"]])
        t["m22"] = V.do(nc.vector.tensor_tensor, s["m22"], fi_, Ar, ALU.mult, after=[t["A"], t["f"]])
        t["p12"] = P.do(nc.gpsimd.tensor_tensor, s["p12"], fr_, Ai, ALU.mult, after=[t["A"], t["f"]])
        t["m21"] = P.do(nc.gpsimd.tensor_tensor, s["m21"], fi_, Ai, ALU.mult, after=[t["A"], t["f"]])
        g("p1", "m11", ALU.mult, "m22", "m11", "m22", "q0")
        v("tau", "m11", ALU.add, "m22", "m11", "m22")
        g("p2", "p12", ALU.mult, "m21", "p12", "m21", "q0")
        g("del", "p1", ALU.add, "p2", "p1", "p2")
        ir, ii = s["sp"][:, 0, :], s["sp"][:, 1, :]
        P.do(nc.gpsimd.tensor_tensor, s["e"][:, 0, :], s["m11"], ir, ALU.mult, after=[t["inp"]])
        P.do(nc.gpsimd.tensor_tensor, s["e"][:, 1, :], s["m21"], ir, ALU.mult)
        P.do(nc.gpsimd.tensor_tensor, s["w2"][:, 0, :], s["p12"], ii, ALU.mult)
        t["w2"] = P.do(nc.gpsimd.tensor_tensor, s["w2"][:, 1, :], s["m22"], ii, ALU.mult)
        P.do(nc.gpsimd.tensor_tensor, s["w2"][:, 0, :], s["e"][:, 0, :], s["w2"][:, 0, :], ALU.subtract,
             after=[t["w2"]])
        t["Mv"] = P.do(nc.gpsimd.tensor_tensor, s["w2"][:, 1, :], s["e"][:, 1, :], s["w2"][:, 1, :], ALU.add)
        v("u1", "tau", ALU.mult, "tau", "tau")
        v("u2", "tau", ALU.mult, "del", "tau", "del")
        t["u3"] = V.do(nc.vector.tensor_scalar, s["u3"], s["del"], -1.0, 1.0, ALU.mult, ALU.add, after=[t["del"]])
        v("b1", "u3", ALU.subtract, "u2", "u3", "u2")
        v("a1", "u1", ALU.add, "tau", "u1")
        v("a1", "a1", ALU.add, "u3", "a1")
        t["u1"] = V.do(nc.vector.scalar_tensor_tensor, out=s["u1"], in0=s["del"], scalar=-2.0, in1=s["u1"],
                       op0=ALU.mult, op1=ALU.add, after=[t["u1"]])
        v("u2", "del", ALU.mult, "del", "del")
        v("u4", "u1", ALU.mult, "u1", "u1")
        t["u4"] = V.do(nc.vector.scalar_tensor_tensor, out=s["u4"], in0=s["u2"], scalar=-2.0, in1=s["u4"],
                       op0=ALU.mult, op1=ALU.add, after=[t["u4"], t["u2"]])
        v("u5", "u2", ALU.mult, "u2", "u2")
        v("m2", "u1", ALU.mult, "del", "u1")
        v("m2", "m2", ALU.add, "u2", "m2", "u2")
        v("u3", "u1", ALU.mult, "tau", "u1")
        v("a2", "u4", ALU.mult, "u4", "u4")
        v("a2", "a2", ALU.add, "u4", "a2")
        t["u2"] = V.do(nc.vector.tensor_scalar, s["u2"], s["u5"], -1.0, 1.0, ALU.mult, ALU.add, after=[t["u5"]])
        v("a2", "a2", ALU.add, "u2", "a2", "u2")
        v("b2", "u4", ALU.mult, "u5", "u5")
        v("b2", "u2", ALU.subtract, "b2", "b2", "u2")
        v("u1", "a2", ALU.mult, "u3", "a2", "u3")
        v("u2", "a2", ALU.mult, "m2", "a2", "m2")
        v("u2", "b2", ALU.subtract, "u2", "u2", "b2")
        v("u3", "a1", ALU.mult, "u1", "a1", "u1")
        v("u4", "u3", ALU.mult, "tau", "u3")
        v("u5", "a1", ALU.mult, "u2", "u2")
        v("m2", "b1", ALU.mult, "u1", "b1")
        v("u4", "u4", ALU.add, "u5", "u4", "u5")
        v("u4", "u4", ALU.add, "m2", "u4", "m2")
        v("b2", "b1", ALU.mult, "u2", "u2")
        v("u3", "u3", ALU.mult, "del", "u3")
        v("b2", "b2", ALU.subtract, "u3", "b2", "u3")
        al = s["u4"].unsqueeze(1).broadcast_to([128, 2, N])
        be = s["b2"].unsqueeze(1).broadcast_to([128, 2, N])
        t["r1"] = V.do(nc.vector.tensor_tensor, s["w2"], s["w2"], al, ALU.mult, after=[t["Mv"], t["u4"]])
        t["r2"] = P.do(nc.gpsimd.tensor_tensor, s["sp"], s["sp"], be, ALU.mult, after=[t["b2"], t["Mv"]])
        if n + 1 < NC:
            load(n + 1)
        t["r3"] = P.do(nc.gpsimd.tensor_tensor, s["w2"], s["w2"], s["sp"], ALU.add, after=[t["r1"], t["r2"]])
        oi, o_, w = outs.take()
        t["o"] = P.do(nc.gpsimd.tensor_tensor, o_, s["w2"], s["res"], ALU.add, after=[t["r3"], tr, *w])
        for h in range(2):
            t["st"] = V.do(nc.vector.bn_stats, d["statp"][:, h, n * 6:n * 6 + 6], o_[:, h, :], after=[t["o"]])
        for b in range(B):
            for h in range(2):
                td = k.dma(couts[oi], xout[64 * h:64 * h + 64, b, n * N:(n + 1) * N],
                           o_[64 * b:64 * b + 64, h, :], after=[t["o"]])
        outs.held[oi] = [t["st"], td]
        done[n % 2] = [t["st"], t["o"], t["xp"], tt]
    V.linked = P.linked = False
    mvp = k.buf(2, 2)
    for h in range(2):
        ta = V.do(nc.vector.bn_aggr, mvp[:, h, :], d["statp"][:, h, :], after=[t["st"]])
    for b in range(B):
        for h in range(2):
            tt = T.do(nc.tensor.matmul, bank[4][64 * h:64 * h + 64, 2 * b:2 * b + 2],
                      d["ident"][:, 64 * b:64 * b + 64], mvp[:, h, :], start=True, stop=True,
                      after=[ta, *pr.held[0]])
    return V.do(nc.vector.tensor_copy, d["mv"].rearrange("p a b -> p (a b)"), bank[4][:, 0:4], after=[tt])


def layer3(k, d, I, xin, xout):
    nc = k.nc
    V, S, T, P = k.lanes["dve"], k.lanes["act"], k.lanes["pe"], k.lanes["pool"]
    ps = k.ps
    U, Y = d["U"], d["Y"]
    win = k.buf(256)
    cwb = k.buf(9, 256)
    cb = k.buf(2)
    c0 = k.chan()
    k.dma(c0, win, I["winx"])
    k.dma(c0, cb, I["convb"])
    t_w = k.dma(c0, cwb.rearrange("p a b -> p (a b)"), I["convw"].partition_broadcast(128))
    for tap in range(9):
        t_cw = V.do(nc.vector.tensor_tensor, cwb[:, tap, :], cwb[:, tap, :], win, ALU.mult, after=[t_w])
    strips = Ring([k.buf(34, 130) for _ in range(2)])
    raws = Ring([k.buf(34, 128) for _ in range(2)])
    for st in strips.bufs:
        t_z = V.do(nc.vector.memset, st, 0.0)
    craw = [k.chan() for _ in range(2)]
    u1 = Ring([k.buf(4, 32, 32) for _ in range(2)])
    u2 = Ring([k.buf(4, 32, 32) for _ in range(2)])
    cu1 = [k.chan() for _ in range(2)]
    cu2 = [k.chan() for _ in range(2)]
    pr = Ring([ps[:, i, :] for i in range(8)])
    rl = {}
    order = [(b, g) for b in range(B) for g in range(4)]

    def load1(n):
        b, g = order[n]
        i, rw, w = raws.take()
        r0, r1 = max(32 * g - 1, 0), min(32 * g + 33, 128)
        o = r0 - (32 * g - 1)
        rl[n] = (i, rw, o, r1 - r0, k.dma(craw[i], rw[:, o:o + r1 - r0, :].rearrange("p a b -> p (a b)"),
                                          xin[:, b, r0 * 128:r1 * 128], after=w))

    load1(0)
    for n, (b, g) in enumerate(order):
        i, rw, o, nr, ld = rl.pop(n)
        j, st, w = strips.take()
        if g in (0, 3) and n > 1:
            t_z = V.do(nc.vector.memset, st[:, 0 if g == 0 else 33, :], 0.0, after=w)
        tn = S.do(nc.scalar.activation, st[:, o:o + nr, 1:129], rw[:, o:o + nr, :], ACT.Identity,
                  bias=d["nb"][:, b:b + 1], scale=d["rs"][:, b:b + 1], after=[ld, *w, t_z])
        raws.held[i] = [tn]
        if n + 1 < len(order):
            load1(n + 1)
        for h in range(2):
            a1, o1, w1 = u1.take()
            a2, o2, w2 = u2.take()
            for r4 in range(8):
                pi, p, wp_ = pr.take()
                for tap in range(9):
                    dy, dx = tap // 3, tap % 3
                    tt = T.do(nc.tensor.matmul, p.rearrange("p (r c) -> p r c", r=4),
                              cwb[:, tap, h * 128:(h + 1) * 128],
                              st[:, 4 * r4 + dy:4 * r4 + dy + 4, dx:dx + 128],
                              start=(tap == 0), stop=(tap == 8), after=[*wp_, tn, t_cw, t_z])
                ev = S.do(nc.scalar.activation, o1[:, :, 4 * r4:4 * r4 + 4, :],
                          p.rearrange("p (r a c) -> p a r c", r=4, a=4), ACT.Silu,
                          bias=cb[:, h:h + 1], after=[tt, *w1])
                pr.held[pi] = [ev]
            for a in range(4):
                ln, eng = (V, nc.vector) if a % 2 else (P, nc.gpsimd)
                t_c = ln.do(eng.tensor_copy, o2[:, a, :, :], o1[:, a, :, :].rearrange("p r c -> p c r"),
                            after=[ev, *w2])
                if a == 2:
                    t_c2 = t_c
            d1 = k.dma(cu1[a1], U[0, b, h, :, g * 4096:(g + 1) * 4096], o1.rearrange("p a r c -> p (a r c)"),
                       after=[ev])
            d2 = k.dma(cu2[a2], U[1, b, h].rearrange("p (a q l) -> p a q l", a=4, q=4)[:, :, g, :],
                       o2.rearrange("p a r c -> p a (r c)"), after=[t_c, t_c2])
            u1.held[a1] = [t_c, t_c2, d1]
            u2.held[a2] = [d2]
        strips.held[j] = [tt]
    k.phase()

    TL = 1024
    NCH, NB = L // TL, TL // 128
    selw = k.buf(16, 128, dt=BF16)
    c0 = k.chan()
    t_sel = k.dma(c0, selw.rearrange("p a b -> p (a b)"), I["sel"])
    par = Ring([(k.buf(2, 120), k.buf(256), k.buf(2, 18), k.buf(2, 16)) for _ in range(2)])
    cpar = [k.chan() for _ in range(2)]
    dsum = k.buf(2, 4)
    cds = k.chan()
    t_ds = k.dma(cds, dsum.rearrange("p a b -> p (a b)"), I["ds"])
    ur = Ring([k.buf(2, TL) for _ in range(2)])
    cu = [k.chan() for _ in range(2)]
    X = k.buf(TL)
    R1 = k.buf(TL)
    Mb = k.buf(TL, dt=BF16)
    S3r = Ring([k.buf(TL, dt=BF16) for _ in range(2)])
    dl = Ring([k.buf(2, TL) for _ in range(2)])
    du = Ring([k.buf(2, TL) for _ in range(2)])
    tmp = k.buf(2, TL)
    CT = Ring([k.buf(NB, 24) for _ in range(2)])
    Bb = Ring([k.buf(TL) for _ in range(3)])
    dA = Ring([k.buf(2, TL) for _ in range(3)])
    dBu = Ring([k.buf(2, TL) for _ in range(3)])
    hr = Ring([k.buf(2, TL) for _ in range(3)])
    accr = Ring([k.buf(NB, 256) for _ in range(2)])
    cacc, cy = [k.chan() for _ in range(2)], [k.chan() for _ in range(2)]
    state = k.buf(2, 16)
    pp = Ring([ps[:, 0:2, :].rearrange("p a b -> p (a b)"), ps[:, 2:4, :].rearrange("p a b -> p (a b)")])
    hT = Ring([ps[:, 4 + i, :].rearrange("p (j c) -> p j c", j=2) for i in range(4)])
    chunks = []
    for b in range(B):
        for kk in range(4):
            cs = range(NCH) if kk < 2 else range(NCH - 1, -1, -1)
            chunks += [(b, kk, c, n == 0) for n, c in enumerate(cs)]
    C_ = {}
    held_X, held_M, held_tmp = [], [], []
    parn = {}
    y_done = {}
    for o in range(2):
        t_D = V.do(nc.vector.tensor_tensor, dsum[:, :, o:o + 1], dsum[:, :, o:o + 1], dsum[:, :, o + 2:o + 3],
                   ALU.add, after=[t_ds])

    def fetch(n):
        b, kk, c, first = chunks[n]
        e = C_[n] = {}
        if first:
            i, bufs, w = par.take()
            k.dma(cpar[i], bufs[0].rearrange("p a b -> p (a b)"), I["xproj"][kk], after=w)
            k.dma(cpar[i], bufs[1][96:104, :], I["dtw"][kk], after=w)
            tp = k.dma(cpar[i], bufs[2].rearrange("p a b -> p (a b)"), I["par"][kk], after=w)
            ta = S.do(nc.scalar.activation, bufs[3], bufs[2][:, :, 0:16], ACT.Exp, after=[tp, *w])
            ta = V.do(nc.vector.tensor_scalar, bufs[3], bufs[3], -1.0, None, ALU.mult, after=[ta])
            parn[b, kk] = (i, bufs, tp, ta)
        e["par"] = parn[b, kk]
        i, u, w = ur.take()
        for h in range(2):
            t = k.dma(cu[i], u[:, h, :], U[kk % 2, b, h, :, c * TL:(c + 1) * TL], after=w)
        e["u"] = (i, u, t)

    def y_rows(b, kk, c):
        return Y[kk % 2, b, c * TL:(c + 1) * TL, :].rearrange("(j p) d -> p j d", p=128)

    def prep(n):
        b, kk, c, first = chunks[n]
        e = C_[n]
        pi, (xp, dtw, pc, A), tp, ta = e["par"]
        ui, u, tu = e["u"]
        ai, acc, w_acc = accr.take()
        if kk >= 2:
            t_acc = k.dma(cacc[ai], acc, y_rows(b, kk, c), after=[*w_acc, y_done[b, kk - 2, c]])
        i, p, w = pp.take()
        for q in range(2):
            for h in range(2):
                tt = T.do(nc.tensor.matmul, p[0:120, q * 512:(q + 1) * 512], xp[:, h, :],
                          u[:, h, q * 512:(q + 1) * 512], start=(h == 0), stop=(h == 1), after=[*w, tu, tp])
        tX = S.do(nc.scalar.copy, X[0:120, :], p[0:120, :], after=[tt, *held_X])
        si, S3, w3 = S3r.take()
        t1 = S.do(nc.scalar.copy, S3[0:96, :], p[0:96, :], after=[*w3])
        pp.held[i] = [t1]
        yield
        t2 = V.do(nc.vector.tensor_tensor, R1[64:96, :], X[64:96, :], S3[64:96, :], ALU.subtract,
                  after=[t1, tX, *held_M])
        t3 = S.do(nc.scalar.copy, Mb[64:96, :], R1[64:96, :], after=[t2, *held_M])
        t4 = V.do(nc.vector.tensor_tensor, S3[32:64, :], X[32:64, :], S3[32:64, :], ALU.subtract, after=[t1, tX])
        yield
        t5 = V.do(nc.vector.tensor_tensor, S3[64:96, :], R1[64:96, :], Mb[64:96, :], ALU.subtract,
                  after=[t3, t2])
        e["S3"] = (si, S3, [t1, t4, t5])
        held_M[:] = [t5]
        yield
        i, p, w = pp.take()
        for j in range(NB):
            tt = T.do(nc.tensor.transpose, p[:, 24 * j:24 * j + 24], X[96:120, j * 128:(j + 1) * 128],
                      d["ident"][96:120, 96:120], after=[*w, tX])
        ci, ct, w = CT.take()
        t6 = S.do(nc.scalar.copy, ct.rearrange("p a b -> p (a b)"), p[:, 0:24 * NB], after=[tt, *w])
        pp.held[i] = [t6]
        e["CT"] = (ci, ct, t6)
        t_ct = tt
        yield
        di, de, wd = dl.take()
        for h in range(2):
            i, p, w = pp.take()
            for q in range(2):
                tt = T.do(nc.tensor.matmul, p[:, q * 512:(q + 1) * 512], dtw[96:104, h * 128:(h + 1) * 128],
                          X[96:104, q * 512:(q + 1) * 512], start=True, stop=True, after=[*w, tX])
            bias = pc[:, h, 16:17]
            t7 = S.do(nc.scalar.activation, tmp[:, h, :], p, ACT.Abs, bias=bias, after=[tt, *held_tmp])
            t8 = V.do(nc.vector.tensor_scalar, de[:, h, :], p, bias, 0.0, ALU.add, ALU.max, after=[tt, t7, *wd])
            pp.held[i] = [t8]
            yield
        held_X[:] = [tt, t2, t4, t_ct]
        t9 = S.do(nc.scalar.activation, tmp, tmp, ACT.Exp, scale=-1.0, after=[t7])
        t10 = S.do(nc.scalar.activation, tmp, tmp, ACT.Ln, bias=1.0, after=[t9])
        yield
        t11 = P.do(nc.gpsimd.tensor_tensor, de, de, tmp, ALU.add, after=[t10, t8])
        held_tmp[:] = [t11]
        yield
        qi, dq, wq_ = du.take()
        t12 = P.do(nc.gpsimd.tensor_tensor, dq, de, u, ALU.mult, after=[t11, tu, *wq_])
        e["dl"], e["du"] = (di, de, t11), (qi, dq, t12)
        last_u = [t12, tt]
        yield
        if kk < 2:
            for h in range(2):
                t13 = S.do(nc.scalar.mul, tmp[:, h, :], u[:, h, :], dsum[:, h, kk:kk + 1], after=[t11, t_D, tu])
            for g in range(2):
                yield
                i, p, w = pp.take()
                for j in range(4):
                    for h in range(2):
                        tt = T.do(nc.tensor.transpose, p[:, j * 256 + h * 128:j * 256 + h * 128 + 128],
                                  tmp[:, h, (4 * g + j) * 128:(4 * g + j + 1) * 128], d["ident"], after=[*w, t13])
                t_acc = S.do(nc.scalar.copy, acc[:, 4 * g:4 * g + 4, :].rearrange("p a b -> p (a b)"), p,
                             after=[tt, *w_acc])
                pp.held[i] = [t_acc]
            held_tmp[:] = [t11, tt]
            last_u.append(t13)
        ur.held[ui] = last_u
        e["acc"] = (ai, acc, t_acc)
        e["acc_t"] = [t_acc] * NB

    iters = [(n, m) for n in range(len(chunks)) for m in range(16)]
    E = {}

    def bc(it):
        n, m = iters[it]
        si, S3, ts = C_[n]["S3"]
        i, p, w = pp.take()
        for q in range(2):
            tt = T.do(nc.tensor.matmul, p[:, q * 512:(q + 1) * 512], selw[0:96, m, :],
                      S3[0:96, q * 512:(q + 1) * 512], start=True, stop=True, after=[*w, *ts, t_sel])
        j, o_, w2 = Bb.take()
        ev = S.do(nc.scalar.copy, o_, p, after=[tt, *w2])
        pp.held[i] = [ev]
        E[it] = {"B": (j, o_, ev)}
        if m == 15:
            S3r.held[si] = [tt]

    def ex(it):
        n, m = iters[it]
        e, r = C_[n], E[it]
        pi, (xp, dtw, pc, A), tp, ta = e["par"]
        di, de, td = e["dl"]
        j, a, w = dA.take()
        for h in range(2):
            t = S.do(nc.scalar.activation, a[:, h, :], de[:, h, :], ACT.Exp, scale=A[:, h, m:m + 1],
                     after=[td, ta, *w])
        r["dA"] = (j, a, t)
        qi, dq, tq = e["du"]
        bj, bb, tb = r["B"]
        j, q, w = dBu.take()
        t2 = P.do(nc.gpsimd.tensor_tensor, q, dq, bb.unsqueeze(1).broadcast_to([128, 2, TL]), ALU.mult,
                  after=[tq, tb, *w])
        Bb.held[bj] = [t2]
        r["dBu"] = (j, q, t2)
        if m == 15:
            dl.held[di] = [t]
            du.held[qi] = [t2]
            par.held[pi] = [t]

    st_t = {}

    def scan(it):
        n, m = iters[it]
        b, kk, c, first = chunks[n]
        r = E[it]
        j, a, ta = r["dA"]
        i, q, tq = r["dBu"]
        hj, hb, w = hr.take()
        step, end = (1, TL - 1) if kk < 2 else (-1, 0)
        for h in range(2):
            t = V.do(nc.vector.tensor_tensor_scan, hb[:, h, ::step], a[:, h, ::step], q[:, h, ::step],
                     0.0 if first else state[:, h, m:m + 1], ALU.mult, ALU.add, after=[ta, tq, *w, *st_t.get(m, [])])
        dA.held[j] = [t]
        dBu.held[i] = [t]
        r["h"] = (hj, hb, t, end)

    def outp(it):
        n, m = iters[it]
        b, kk, c, first = chunks[n]
        e, r = C_[n], E.pop(it)
        hj, hb, t, end = r["h"]
        ci, ct, t_ct = e["CT"]
        ai, acc, t_acc = e["acc"]
        ts = V.do(nc.vector.tensor_copy, state[:, :, m:m + 1], hb[:, :, end:end + 1], after=[t])
        st_t[m] = [ts]
        for g in range(NB // 2):
            i, p, w = hT.take()
            for j in range(2):
                for h in range(2):
                    l0 = (2 * g + j) * 128
                    tt = T.do(nc.tensor.transpose, p[:, j, h * 128:(h + 1) * 128], hb[:, h, l0:l0 + 128],
                              d["ident"], after=[*w, t])
            for j in range(2):
                q = 2 * g + j
                ty = V.do(nc.vector.scalar_tensor_tensor, out=acc[:, q, :], in0=p[:, j, :],
                          scalar=ct[:, q, 8 + m:9 + m], in1=acc[:, q, :], op0=ALU.mult, op1=ALU.add,
                          after=[tt, t_ct, e["acc_t"][q]])
                e["acc_t"][q] = ty
            hT.held[i] = [ty]
        hr.held[hj] = [tt, ts]
        if m == 15:
            CT.held[ci] = [ty]
            td = k.dma(cy[ai], y_rows(b, kk, c), acc, after=[ty])
            y_done[b, kk, c] = td
            accr.held[ai] = [td]

    NI = len(iters)
    fetch(0)
    for _ in prep(0):
        pass
    fetch(1)
    going = None
    for s in range(NI + 3):
        if s < NI:
            n, m = iters[s]
            if m == 3 and n + 1 < len(chunks):
                going = prep(n + 1)
            if going is not None:
                next(going, None)
            bc(s)
        if 0 <= s - 1 < NI:
            ex(s - 1)
        if 0 <= s - 2 < NI:
            scan(s - 2)
        if 0 <= s - 3 < NI:
            outp(s - 3)
        if s < NI and m == 15 and n + 2 < len(chunks):
            fetch(n + 2)
    k.phase()

    wz = k.buf(256)
    wo = k.buf(2, 128)
    lnp = k.buf(2, 2)
    c0 = k.chan()
    k.dma(c0, wz, I["winz"])
    k.dma(c0, wo.rearrange("p a b -> p (a b)"), I["wout"])
    t_c = k.dma(c0, lnp.rearrange("p a b -> p (a b)"), I["lnp"])
    N = 512
    xr = Ring([k.buf(N) for _ in range(6)])
    xnr = Ring([k.buf(N) for _ in range(2)])
    yr = Ring([k.buf(4, 256) for _ in range(5)])
    y2r = Ring([k.buf(4, 256) for _ in range(4)])
    bsr = Ring([(k.buf(4, 6), k.buf(4, 2), k.buf(4)) for _ in range(3)])
    gr = Ring([k.buf(2, N) for _ in range(3)])
    zr = Ring([k.buf(2, N) for _ in range(5)])
    outr = Ring([k.buf(N) for _ in range(3)])
    cx, cyr = [k.chan() for _ in range(6)], [k.chan() for _ in range(5)]
    cy2, co = [k.chan() for _ in range(4)], [k.chan() for _ in range(3)]
    bk = [ps[:, i, :] for i in range(8)]
    tp_, zp, op = Ring(bk[0:4]), Ring(bk[4:6]), Ring(bk[6:8])
    u = {}

    def g0(n):
        b, r = n // 32, n % 32
        i, x, w = xr.take()
        tx = k.dma(cx[i], x, xin[:, b, r * N:(r + 1) * N], after=w)
        j, y, w = yr.take()
        ty = k.dma(cyr[j], y, Y[0, b, r * N:(r + 1) * N, :].rearrange("(a p) d -> p a d", p=128), after=w)
        j2, y2, w = y2r.take()
        ty2 = k.dma(cy2[j2], y2, Y[1, b].rearrange("(w h) d -> w h d", h=128)[:, 4 * r:4 * r + 4, :], after=w)
        u[n] = {"x": (i, x, tx), "y": (j, y, ty), "y2": (j2, y2, ty2)}

    def g1(n):
        e, b = u[n], n // 32
        i, x, tx = e["x"]
        j, y, ty = e["y"]
        j2, y2, ty2 = e["y2"]
        t1 = P.do(nc.gpsimd.tensor_tensor, y, y, y2, ALU.add, after=[ty, ty2])
        y2r.held[j2] = [t1]
        e["y1"] = t1
        q, xn, w = xnr.take()
        t2 = V.do(nc.vector.tensor_scalar, xn, x, d["rs"][:, b:b + 1], d["nb"][:, b:b + 1], ALU.mult, ALU.add,
                  after=[tx, *w])
        zi, z, w = zr.take()
        for h in range(2):
            m, p, w2 = zp.take()
            tt = T.do(nc.tensor.matmul, p, wz[:, h * 128:(h + 1) * 128], xn, start=True, stop=True,
                      after=[t2, *w2, t_c])
            t3 = S.do(nc.scalar.activation, z[:, h, :], p, ACT.Silu, after=[tt, *w])
            zp.held[m] = [t3]
        xnr.held[q] = [tt]
        e["z"] = (zi, z, t3)

    def g2(n):
        e = u[n]
        j, y, ty = e["y"]
        si, (bs, mv, sd), w = bsr.take()
        for a in range(4):
            t1 = V.do(nc.vector.bn_stats, bs[:, a, :], y[:, a, :], after=[e["y1"], *w])
        for a in range(4):
            t1 = V.do(nc.vector.bn_aggr, mv[:, a, :], bs[:, a, :], after=[t1])
        t1 = V.do(nc.vector.tensor_scalar, sd, mv[:, :, 1], EPS, None, ALU.add, after=[t1])
        t1 = S.do(nc.scalar.activation, sd, sd, ACT.Sqrt, after=[t1])
        t1 = V.do(nc.vector.reciprocal, sd, sd, after=[t1])
        e["st"] = (si, mv, sd, t1)

    def g3(n):
        e = u[n]
        j, y, ty = e["y"]
        si, mv, sd, t1 = e["st"]
        for a in range(4):
            t2 = V.do(nc.vector.tensor_scalar, y[:, a, :], y[:, a, :], mv[:, a, 0:1], sd[:, a:a + 1],
                      ALU.subtract, ALU.mult, after=[t1])
        bsr.held[si] = [t2]
        gi, g, wg_ = gr.take()
        for h in range(2):
            m, p, w = tp_.take()
            for a in range(4):
                tt = T.do(nc.tensor.transpose, p[:, a * 128:(a + 1) * 128], y[:, a, h * 128:(h + 1) * 128],
                          d["ident"], after=[t2, *w])
            t3 = S.do(nc.scalar.activation, g[:, h, :], p, ACT.Identity, bias=lnp[:, h, 1:2],
                      scale=lnp[:, h, 0:1], after=[tt, t_c, *wg_])
            tp_.held[m] = [t3]
        yr.held[j] = [tt]
        zi, z, tz = e["z"]
        t4 = P.do(nc.gpsimd.tensor_tensor, z, z, g, ALU.mult, after=[t3, tz])
        gr.held[gi] = [t4]
        e["g"] = t4

    def g4(n):
        e, b = u.pop(n), n // 32
        zi, z, tz = e["z"]
        m, p, w = op.take()
        for h in range(2):
            tt = T.do(nc.tensor.matmul, p, wo[:, h, :], z[:, h, :], start=(h == 0), stop=(h == 1),
                      after=[e["g"], *w])
        zr.held[zi] = [tt]
        oi, o_, w = outr.take()
        xi, x, tx = e["x"]
        t7 = V.do(nc.vector.tensor_tensor, o_, x, p, ALU.add, after=[tt, *w])
        op.held[m] = [t7]
        xr.held[xi] = [t7]
        outr.held[oi] = [k.dma(co[oi], xout[:, b, (n % 32) * N:(n % 32 + 1) * N], o_, after=[t7])]

    for s in range(64 + 4):
        for lag, f in ((4, g4), (3, g3), (2, g2), (1, g1), (0, g0)):
            if 0 <= s - lag < 64:
                f(s - lag)
    return None


LAYERS = {0: layer0, 1: layer1, 2: layer2, 3: layer3}

def program(nc, I, xin, scratch, out, layers=(0, 1, 2, 3)):
    with ExitStack() as ctx:
        k = Core(nc, ctx)
        d = {}
        d["grp"] = k.buf(128)
        d["ident"] = k.buf(128)
        d["avg"] = k.buf(128)
        d["rs"] = k.buf(2)
        d["nb"] = k.buf(2)
        d["mv"] = k.buf(2, 2)
        d["sm"] = k.buf(8)
        d["stats"] = k.buf(2, 192)
        d["stats2"] = d["stats"]
        d["statp"] = d["stats"]
        d["U"] = nc.dram_tensor("U", (2, B, 2, 128, L), F32).ap()
        d["Y"] = nc.dram_tensor("Y", (2, B, L, 256), F32).ap()
        cc = k.chan()
        k.dma(cc, d["grp"], I["grp"])
        k.dma(cc, d["ident"], I["ident"])
        d["t_const"] = k.dma(cc, d["avg"], I["avg"])
        k.low = k.top
        t = first_stats(k, d, xin)
        t = norm_params(k, d, d["stats"], [t])
        x = xin
        fns = LAYERS
        for n, lay in enumerate(layers):
            k.phase()
            y = out if n == len(layers) - 1 else scratch[n % 2]
            t = fns[lay](k, d, I, x, y)
            if n < len(layers) - 1:
                k.phase()
                norm_params(k, d, d["stats"], [t], aggregate=lay != 2)
            x = y
        k.play()


def _rel_index():
    q = np.arange(256)
    o, cb, r, c = np.meshgrid(np.arange(4), np.arange(2), np.arange(8), np.arange(16), indexing="ij")
    rk, ck = (8 * o + r).ravel(), (16 * cb + c).ravel()
    rq, cq = 8 + q // 32, q % 32
    return (47 * (rq[:, None] - rk + 23) + cq[:, None] - ck + 23) % (47 * 47)


def _lay(inputs):
    g = {n: np.asarray(a) for n, a in inputs.items()}
    f = np.float32
    I = {"x": np.ascontiguousarray(g["x"].transpose(3, 0, 1, 2).reshape(128, B, L))}
    for n in "qkvp":
        I["w" + n] = np.ascontiguousarray(g[f"L0_conv_W{n}"].T)
    I["b0"] = np.stack([g[f"L0_conv_b{n}"] for n in "qkvp"], 1)
    t = g["L0_conv_bias_table"].T[:, _rel_index()]
    I["rel"] = np.ascontiguousarray(t.reshape(4, 2, 128, 1024).transpose(2, 1, 0, 3).reshape(128, 8192))
    a = np.arange(128)
    I["grp"] = (a[:, None] // 4 == a // 4).astype(f) / 4
    I["ident"] = np.eye(128, dtype=f)
    I["avg"] = np.full((128, 128), 1 / 128, f)
    I["wf"] = np.ascontiguousarray(np.stack([g[f"L1_conv_w{n}"].transpose(0, 2, 3, 1) for n in (1, 2)])
                                   .reshape(2, 128, 4096))
    y, m = np.arange(128), np.arange(16)
    th = 2 * np.pi * ((y[:, None] * m) % 128) / 128
    n_ = 128 ** -0.5
    I["dft"] = (np.stack([np.sin(th), np.cos(th), -np.sin(th)], 2).reshape(128, 48) * n_).astype(f)
    w = np.where(m == 0, 1.0, 2.0) * n_
    I["idft"] = np.stack([w * np.cos(th), -w * np.sin(th)], 2).reshape(128, 32).T.astype(f)
    I["ff0"] = g["L1_conv_ff_w0"]
    I["ff1"] = g["L1_conv_ff_w1"].reshape(4, 128, 128).transpose(1, 0, 2).reshape(128, 512)
    I["b1"] = np.concatenate([g["L1_conv_ff_b0"].reshape(4, 128).T] +
                             [g["L1_conv_" + n][:, None] for n in ("ff_b1", "ln_g", "ln_b")], 1)
    I["wg"] = np.concatenate([g[f"L2_conv_W{n}"] for n in "fid"], 1)
    bg = [g[f"L2_conv_b{n}"][64 * h:64 * h + 64] for n in "fid" for h in range(2)]
    I["bg"] = np.stack([np.concatenate([v, v]) for v in bg], 1)
    kern = np.zeros((128, 4, 2, 64), f)
    for i, n in enumerate("AB"):
        re, im = (g[f"L2_conv_{n}_{p}"].reshape(64, 49).T[:, None, :] for p in ("real", "imag"))
        kern[0:49, i], kern[64:113, i] = re, im
        kern[0:49, 2 + i], kern[64:113, 2 + i] = im, re
    I["kern"] = kern.reshape(128, 512)
    p, q = np.arange(49) // 7, np.arange(49) % 7
    u = np.arange(128)
    ph = (u[None, :, None] * (60 + p)[:, None, None] + u[None, None, :] * (60 + q)[:, None, None]) % 128
    ph = (2 * np.pi * ph / 128).reshape(49, L)
    basis = np.zeros((128, L), f)
    basis[0:49], basis[64:113] = np.cos(ph), np.sin(ph)
    I["basis"] = basis
    win = g["L3_conv_W_in"].T
    I["winx"], I["winz"] = win[:, 0:256], win[:, 256:512]
    I["convw"] = g["L3_conv_conv_w"].reshape(256, 9).T.reshape(2304)
    half = lambda v: v.reshape(2, 128, *v.shape[1:])
    I["convb"] = half(g["L3_conv_conv_b"]).T
    xp = np.zeros((4, 256, 120), f)
    pw = g["L3_conv_x_proj_w"].transpose(0, 2, 1)
    for q in range(3):
        xp[:, :, 32 * q:32 * q + 16] = pw[:, :, 8:24]
    xp[:, :, 96:104], xp[:, :, 104:120] = pw[:, :, 0:8], pw[:, :, 24:40]
    I["xproj"] = xp.reshape(4, 2, 128, 120).transpose(0, 2, 1, 3).reshape(4, 128, 240)
    I["ds"] = g["L3_conv_Ds"].reshape(4, 2, 128).transpose(2, 1, 0).reshape(128, 8)
    I["dtw"] = g["L3_conv_dt_proj_w"].transpose(0, 2, 1)
    par = np.concatenate([g["L3_conv_A_logs"].reshape(4, 256, 16), g["L3_conv_dt_proj_b"].reshape(4, 256, 1),
                          g["L3_conv_Ds"].reshape(4, 256, 1)], 2)
    I["par"] = par.reshape(4, 2, 128, 18).transpose(0, 2, 1, 3).reshape(4, 128, 36)
    sel = np.zeros((128, 16, 128), mybir.dt.np(BF16))
    for r in range(16):
        sel[[r, 32 + r, 64 + r], r, :] = 1
    I["sel"] = sel.reshape(128, 2048)
    I["lnp"] = np.stack([half(g["L3_conv_ln_w"]), half(g["L3_conv_ln_b"])], 2).transpose(1, 0, 2).reshape(128, 4)
    I["wout"] = g["L3_conv_W_out"].T.reshape(2, 128, 128).transpose(1, 0, 2).reshape(128, 256)
    return I


def _build(nc, arrays, layers=(0, 1, 2, 3)):
    I = {n[3:]: nc.dram_tensor(n, a.shape, mybir.dt.from_np(a.dtype), kind="ExternalInput").ap()
         for n, a in arrays.items()}
    out = nc.dram_tensor("out_dram", (128, B, L), F32, kind="ExternalOutput").ap()
    scratch = [nc.dram_tensor(f"scr{i}", (128, B, L), F32).ap() for i in range(2)]
    program(nc, I, I["x"], scratch, out, layers)


def kernel(**inputs):
    import concourse.bacc as _bacc
    from concourse.bass_utils import run_bass_kernel_spmd as _run

    arrays = {f"in_{n}": np.ascontiguousarray(a) for n, a in _lay(inputs).items()}
    nc = _bacc.Bacc("TRN2", target_bir_lowering=False, num_devices=1)
    _build(nc, arrays)
    r = _run(nc, [arrays], core_ids=[0])
    return np.ascontiguousarray(r.results[0]["out_dram"].reshape(128, B, HW, HW).transpose(1, 2, 3, 0))
```

```python
from contextlib import ExitStack

import numpy as np
import concourse.bass as bass
from concourse import mybir

F32 = mybir.dt.float32
FR = mybir.dt.float32r
BF16 = mybir.dt.bfloat16
ALU = mybir.AluOpType
ACT = mybir.ActivationFunctionType
AXX = mybir.AxisListType.X

B, HW, C = 2, 128, 128
L = HW * HW
EPS = 1e-5


class Lane:

    def __init__(self, sem):
        self.sem, self.items, self.first = sem, [], []
        self.linked = False

    def do(self, fn, *args, after=(), **kw):
        if self.linked and self.items:
            after = [*after, (self, len(self.items) - 1)]
        self.items.append([fn, args, kw, [*self.first, *after], False])
        self.first = []
        return (self, len(self.items) - 1)

    def number(self):
        self.count, n = [], 0
        for it in self.items:
            n += it[4]
            self.count.append(n)

    def play(self, eng):
        seen = {}
        for fn, args, kw, after, marked in self.items:
            need = {}
            for src, at in after:
                v = src.count[at] if isinstance(src, Lane) else at
                if v > need.get(src, 0):
                    need[src] = v
            for src, v in need.items():
                if v > seen.get(src, 0):
                    eng.wait_ge(src.sem, v)
                    seen[src] = v
            if fn is None:
                continue
            ins = fn(*args, **kw)
            if marked:
                ins.then_inc(self.sem, 1)


class Chan:

    def __init__(self, sem):
        self.sem, self.n = sem, 0


class Ring:

    def __init__(self, bufs):
        self.bufs, self.n = bufs, 0
        self.held = [[] for _ in bufs]

    def take(self):
        i = self.n % len(self.bufs)
        self.n += 1
        w, self.held[i] = self.held[i], []
        return i, self.bufs[i], w


class Core:
    def __init__(self, nc, ctx):
        self.nc, self.ctx = nc, ctx
        self.lanes = {}
        for n in ("pe", "act", "dve", "pool", "sp"):
            self.lanes[n] = Lane(ctx.enter_context(nc.semaphore(f"s_{n}")))
        self.chans = []
        self.words = 800
        self.mem = ctx.enter_context(nc.sbuf_tensor("base", [128, self.words], F32))
        self.held = None
        self.ps = ctx.enter_context(nc.psum_tensor("ps", [128, 8, 512], F32))
        self.low = self.top = 0
        self.nchan = 0

    def chan(self):
        self.nchan += 1
        c = Chan(self.ctx.enter_context(self.nc.semaphore(f"d{self.nchan}")))
        self.chans.append(c)
        return c

    def arena(self, name, words, rounded=0):
        if self.held is not None:
            self.held.close()
        self.held = ExitStack()
        self.words, self.low, self.top, self.rtop = words, 0, 0, 0
        self.mem = self.held.enter_context(self.nc.sbuf_tensor(name, [128, words], F32))
        if rounded:
            self.rmem = self.held.enter_context(self.nc.sbuf_tensor(name + "_r", [128, rounded], FR))

    def rbuf(self, *shape):
        n = int(np.prod(shape))
        a = self.rmem[:, self.rtop:self.rtop + n]
        self.rtop += n
        if len(shape) == 2:
            a = a.rearrange("p (a b) -> p a b", a=shape[0])
        elif len(shape) == 3:
            a = a.rearrange("p (a b c) -> p a b c", a=shape[0], b=shape[1])
        elif len(shape) == 4:
            a = a.rearrange("p (a b c d) -> p a b c d", a=shape[0], b=shape[1], c=shape[2])
        return a

    def buf(self, *shape, dt=F32, parts=128):
        n = int(np.prod(shape))
        words = n if dt == F32 else (n + 1) // 2
        assert self.top + words <= self.words, (self.top, words)
        a = self.mem[0:parts, self.top:self.top + words]
        self.top += words
        if dt != F32:
            a = a.bitcast(dt)
        if len(shape) == 2:
            a = a.rearrange("p (a b) -> p a b", a=shape[0])
        elif len(shape) == 3:
            a = a.rearrange("p (a b c) -> p a b c", a=shape[0], b=shape[1])
        return a

    def dma(self, chan, out, in_, after=(), lane="sp"):
        ln = self.lanes[lane]
        eng = {"sp": self.nc.sync, "pool": self.nc.gpsimd, "act": self.nc.scalar}[lane]
        chan.n += 16
        ln.do(lambda o=out, i=in_, s=chan.sem, e=eng: e.dma_start(o, i).then_inc(s, 16), after=after)
        return (chan, chan.n)

    def phase(self):
        ends = [(ln, len(ln.items) - 1) for ln in self.lanes.values()
                if ln.items and ln is not self.lanes["sp"]]
        ends += [(c, c.n) for c in self.chans if c.n]
        for ln in self.lanes.values():
            ln.first = list(ends)
        self.top = self.low

    def play(self):
        for ln in self.lanes.values():
            for it in ln.items:
                for src, at in it[3]:
                    if isinstance(src, Lane):
                        src.items[at][4] = True
        ends = [(c, c.n) for c in self.chans if c.n]
        self.lanes["sp"].do(None, after=ends)
        for ln in self.lanes.values():
            ln.number()
        with self.nc.Block() as block:
            @block.tensor
            def _(e):
                self.lanes["pe"].play(e)

            @block.scalar
            def _(e):
                self.lanes["act"].play(e)

            @block.vector
            def _(e):
                self.lanes["dve"].play(e)

            @block.gpsimd
            def _(e):
                self.lanes["pool"].play(e)

            @block.sync
            def _(e):
                self.lanes["sp"].play(e)


def norm_params(k, d, stats, ready, aggregate=True):
    nc, V, S, T = k.nc, k.lanes["dve"], k.lanes["act"], k.lanes["pe"]
    mv, sm = d["mv"], d["sm"]
    t = ready[0]
    for b in range(B) if aggregate else ():
        t = V.do(nc.vector.bn_aggr, mv[:, b, :], stats[:, b, :], after=ready)
    p = k.ps[:, 0, 0:2]
    t = T.do(nc.tensor.matmul, p, d["grp"], mv[:, :, 0], start=True, stop=True, after=[t, d["t_const"]])
    t = V.do(nc.vector.tensor_copy, sm[:, 0:2], p, after=[t])
    t = V.do(nc.vector.tensor_tensor, sm[:, 2:4], mv[:, :, 0], sm[:, 0:2], ALU.subtract, after=[t])
    t = V.do(nc.vector.tensor_tensor, sm[:, 4:6], sm[:, 2:4], sm[:, 2:4], ALU.mult, after=[t])
    t = V.do(nc.vector.tensor_tensor, sm[:, 6:8], sm[:, 4:6], mv[:, :, 1], ALU.add, after=[t])
    t = T.do(nc.tensor.matmul, p, d["grp"], sm[:, 6:8], start=True, stop=True, after=[t])
    t = V.do(nc.vector.tensor_scalar, sm[:, 2:4], p, EPS, None, ALU.add, after=[t])
    t = S.do(nc.scalar.activation, sm[:, 4:6], sm[:, 2:4], ACT.Sqrt, after=[t])
    t = V.do(nc.vector.reciprocal, d["rs"], sm[:, 4:6], after=[t])
    t = V.do(nc.vector.scalar_tensor_tensor, out=d["nb"], in0=sm[:, 0:2], scalar=-1.0, in1=d["rs"],
             op0=ALU.mult, op1=ALU.mult, after=[t])
    return t


def first_stats(k, d, xin):
    nc, V = k.nc, k.lanes["dve"]
    ring = Ring([k.buf(4096) for _ in range(4)])
    ch = [k.chan() for _ in range(4)]
    t = None
    for b in range(B):
        for n in range(4):
            i, x, w = ring.take()
            ld = k.dma(ch[i], x, xin[:, b, n * 4096:(n + 1) * 4096], after=w)
            for j in range(8):
                t = V.do(nc.vector.bn_stats, d["stats"][:, b, (n * 8 + j) * 6:(n * 8 + j) * 6 + 6],
                         x[:, j * 512:(j + 1) * 512], after=[ld])
            ring.held[i] = [t]
    return t


def layer0(k, d, I, xin, xout):
    nc = k.nc
    V, S, T, P_ = k.lanes["dve"], k.lanes["act"], k.lanes["pe"], k.lanes["pool"]
    ps = k.ps
    c0 = k.chan()
    w3, wp = k.buf(3, 128), k.buf(128)
    rel = k.buf(2, 4, 1024)
    for j, n in enumerate("qkv"):
        k.dma(c0, w3[:, j, :], I["w" + n])
    k.dma(c0, wp, I["wp"])
    bv4 = k.buf(5)
    tw0 = k.dma(c0, bv4[:, 0:4], I["b0"])
    tb = k.dma(k.chan(), rel, I["rel"].rearrange("p (a b c) -> p a b c", a=2, b=4))
    tq = S.do(nc.scalar.mul, bv4[:, 4:5], bv4[:, 0:1], 32 ** -0.5, after=[tw0])
    tq = S.do(nc.scalar.mul, w3[:, 0, :], w3[:, 0, :], 32 ** -0.5, after=[tw0, tq])
    wh, wl = k.rbuf(3, 128), k.rbuf(3, 128)
    tw = S.do(nc.scalar.copy, wh, w3, after=[tw0, tq])
    tw = V.do(nc.vector.tensor_tensor, wl, w3, wh.bitcast(F32), ALU.subtract, after=[tw])
    stats = d["stats2"]

    NO = 6
    raw = [k.buf(8, 72) for _ in range(NO)]
    Kp = [[k.rbuf(2, 640) for _ in range(NO // 2)] for _ in range(2)]
    Kh, Kl = [[p[i // 2][:, i % 2, :] for i in range(NO)] for p in Kp]
    Vb = [k.rbuf(5, 4, 2, 32) for _ in range(NO)]
    Qh, Ql = [k.rbuf(4, 128) for _ in range(NO)], [k.rbuf(4, 128) for _ in range(NO)]
    xf_ = k.buf(5, 8, 16)
    xnr = Ring([(k.rbuf(5, 8, 16), k.rbuf(5, 8, 16)) for _ in range(2)])
    chr_ = [k.chan() for _ in range(NO)]
    held = [[] for _ in range(NO)]
    xf_held = []
    Tr = Ring([k.buf(1024) for _ in range(2)])
    Pr = Ring([k.buf(1024) for _ in range(3)])
    PTr = Ring([k.rbuf(8, 2, 128) for _ in range(2)])
    Ar = Ring([k.buf(2, 128, parts=64) for _ in range(2)])
    mx = k.buf(4, 4)
    outr = Ring([k.buf(16, 64) for _ in range(2)])
    cho = [k.chan() for _ in range(2)]
    Osb = Ring([k.buf(128) for _ in range(2)])
    OT = Ring([k.buf(256) for _ in range(2)])
    rsum = Ring([k.buf(4) for _ in range(4)])
    rinv = Ring([k.buf(4) for _ in range(4)])
    Sp = Ring([ps[:, 0:2, :].rearrange("p a b -> p (a b)"), ps[:, 2:4, :].rearrange("p a b -> p (a b)")])
    PTp = Ring([ps[:, 4, :], ps[:, 5, :]])
    PV, Ob = Ring([ps[0:64, 6, :]]), Ring([ps[:, 7, :]])
    octs = {}
    loads = {}

    def slot(b, hf, o):
        return ((2 * b + hf) * 18 + o) % NO

    def load_oct(b, hf, o):
        i = slot(b, hf, o)
        r0 = 1 if o == 0 else 119 if o == 17 else 8 * o - 8
        w, held[i] = held[i], []
        loads[b, hf, o] = k.dma(chr_[i], raw[i], xin[:, b, :].rearrange("p (r c) -> p r c", c=128)
                                [:, r0:r0 + 8, 56 * hf:56 * hf + 72], after=w)

    def split(ph, pl, psum, bias, after, free):
        if bias is None:
            t1 = S.do(nc.scalar.copy, ph, psum, after=[*after, *free])
            t2 = V.do(nc.vector.tensor_tensor, pl, psum, ph.bitcast(F32), ALU.subtract, after=[t1])
        else:
            t1 = S.do(nc.scalar.activation, ph, psum, ACT.Identity, bias=bias, after=[*after, *free])
            t2 = V.do(nc.vector.scalar_tensor_tensor, out=pl, in0=psum, scalar=bias, in1=ph.bitcast(F32),
                      op0=ALU.add, op1=ALU.subtract, after=[t1])
        return t2

    def make_oct(b, hf, o):
        i = slot(b, hf, o)
        ld = loads.pop((b, hf, o))
        j, (xh, xl), w = xnr.take()
        src = raw[i][:, ::-1, :] if o in (0, 17) else raw[i]
        cen = src.rearrange("p r (a c) -> p r a c", c=8)
        x4 = xf_.rearrange("p cb r (h c) -> p r cb h c", h=2)
        rs, nb = d["rs"][:, b:b + 1], d["nb"][:, b:b + 1]
        if hf == 0:
            parts = [(x4[:, :, 0:5, 1, :], cen[:, :, 0::2, :]), (x4[:, :, 1:5, 0, :], cen[:, :, 1::2, :]),
                     (x4[:, :, 0, 0, :], src[:, :, 8:0:-1])]
        else:
            parts = [(x4[:, :, 0:5, 0, :], cen[:, :, 0::2, :]), (x4[:, :, 0:4, 1, :], cen[:, :, 1::2, :]),
                     (x4[:, :, 4, 1, :], src[:, :, 70:62:-1])]
        for dst, sr in parts:
            ts = S.do(nc.scalar.activation, dst, sr, ACT.Identity, bias=nb, scale=rs, after=[ld, *xf_held])
        t1 = S.do(nc.scalar.copy, xh, xf_, after=[ts, *w])
        t2 = V.do(nc.vector.tensor_tensor, xl, xf_, xh.bitcast(F32), ALU.subtract, after=[t1])
        xf_held[:] = [t1, t2]
        yield
        tk = []
        hi, lo = (x.rearrange("p a r c -> p a (r c)") for x in (xh, xl))
        m, p, w = Sp.take()
        for c2 in range(2):
            c = slice(320 * c2, 320 * c2 + 320)
            for n, (wt, x) in enumerate(((wh, hi), (wh, lo), (wl, hi))):
                t = T.do(nc.tensor.matmul, p[:, 512 * c2:512 * c2 + 320], wt[:, 1, :],
                         x.rearrange("p a b -> p (a b)")[:, c], start=(n == 0), stop=(n == 2), after=[*w, t2, tw])
        pv = p.rearrange("p (a b) -> p a b", a=2)[:, :, 0:320]
        t = split(Kh[i].rearrange("p (a b) -> p a b", a=2), Kl[i].rearrange("p (a b) -> p a b", a=2), pv,
                  bv4[:, 1:2], [t], [])
        Sp.held[m] = [t]
        tk.append(t)
        yield
        m, p, w = Sp.take()
        for a in range(5):
            at = 128 * a
            for n, (x, wt) in enumerate(((hi, wh), (hi, wl), (lo, wh))):
                t = T.do(nc.tensor.matmul, p[:, at:at + 128], x[:, a, :], wt[:, 2, :],
                         start=(n == 0), stop=(n == 2), after=w)
        for c0_, c1_ in ((0, 4), (4, 5)):
            pv = p[:, 128 * c0_:128 * c1_].rearrange("p (a h c) -> p a h c", h=4, c=32)
            t3 = split(Vb[i][:, c0_:c1_, :, 0, :], Vb[i][:, c0_:c1_, :, 1, :], pv, None, [t], [])
        Sp.held[m] = [t3]
        tk.append(t3)
        yield
        if 1 <= o <= 16:
            m, p, w = Sp.take()
            for hh in range(2):
                dst = p[:, 0:512].rearrange("p (a c) -> p a c", c=16)[:, :, 8 * hh:8 * hh + 8]
                for n, (wt, x) in enumerate(((wh, xh), (wh, xl), (wl, xh))):
                    sr = x[:, 0:4, :, 8:16] if hh == 0 else x[:, 1:5, :, 0:8]
                    t = T.do(nc.tensor.matmul, dst, wt[:, 0, :], sr.rearrange("p a r c -> p (a r) c"),
                             start=(n == 0), stop=(n == 2), after=w)
            t = split(Qh[i].rearrange("p a b -> p (a b)"), Ql[i].rearrange("p a b -> p (a b)"), p[:, 0:512],
                      bv4[:, 4:5], [t, tq], [])
            Sp.held[m] = [t]
            tk.append(t)
        xnr.held[j] = [t for t in tk]
        octs[b, hf, o] = (i, tk)

    units = [(b, hf, wi, wj, t, h) for b in range(B) for hf in range(2) for wi in range(8) for wj in range(4)
             for t in range(2) for h in range(4)]
    st = {}
    win = {}
    rows = {}
    going = []

    def stage_a(n):
        b, hf, wi, wj, t, h = units[n]
        if wj == 0 and t == 0 and h == 0:
            if wi == 0:
                for o in range(4):
                    load_oct(b, hf, o)
                for o in range(4):
                    for _ in make_oct(b, hf, o):
                        pass
        if wi < 7 and t == 0 and h == 0 and wj == 1:
            for o in (2 * wi + 4, 2 * wi + 5):
                load_oct(b, hf, o)
        if wi < 7 and wj >= 2:
            if t == 0 and h == 0:
                going[:] = [make_oct(b, hf, 2 * wi + wj + 2)]
            for q in going:
                next(q, None)
        i, s, w = Sp.take()
        qi, qt = octs[b, hf, 2 * wi + 1 + t]
        hp = slice(32 * h, 32 * h + 32)
        kc = slice(wj * 128, wj * 128 + 256)
        for o in range(2):
            ki, kt = octs[b, hf, 2 * wi + 2 * o]
            kt2 = octs[b, hf, 2 * wi + 2 * o + 1][1]
            for m, (q_, k_) in enumerate(((Qh, 0), (Qh, 1), (Ql, 0))):
                tt = T.do(nc.tensor.matmul, s[:, o * 512:(o + 1) * 512].rearrange("p (a b) -> p a b", a=2),
                          q_[qi][hp, wj, :], Kp[k_][ki // 2][hp, :, kc],
                          start=(m == 0), stop=(m == 2), after=[*w, *qt, *kt, *kt2])
        j, tl, w = Tr.take()
        m = n % 4
        mxc = mx[:, m, :]
        wm = st[n - 4]["exp"] if n >= 4 else None
        tm = V.do(nc.vector.tensor_tensor_reduce, tl, s, rel[:, t, h, :], 1.0, -3.0e38, ALU.add, ALU.max,
                  mxc[:, 0:1], after=[tt, tb, *w, *([wm] if wm else [])])
        Sp.held[i] = [tm]
        tn = P_.do(nc.gpsimd.tensor_scalar, mxc[:, 1:2], mxc[:, 0:1], -1.0, None, ALU.mult, after=[tm])
        st[n] = {"tn": tn, "T": (j, tl), "m": mxc}
        if h == 0:
            ri, r, w = rsum.take()
            win[b, hf, wi, wj, t] = {"rs": (ri, r), "rw": w}
        st[n]["win"] = win[b, hf, wi, wj, t]

    def stage_b(n):
        b, hf, wi, wj, t, h = units[n]
        u = st[n]
        j, tl = u["T"]
        pi, p, w = Pr.take()
        ri, r = u["win"]["rs"]
        te = S.do(nc.scalar.activation, p, tl, ACT.Exp, bias=u["m"][:, 1:2], scale=1.0,
                  accum_out=r[:, h:h + 1], after=[u["tn"], *w, *u["win"]["rw"]])
        Tr.held[j] = [te]
        u["exp"], u["P"] = te, (pi, p)

    def stage_c(n):
        u = st[n]
        pi, p = u["P"]
        j, pt, w2 = PTr.take()
        ready = []
        for g4 in range(2):
            i, q, w = PTp.take()
            for g in range(4):
                tt = T.do(nc.tensor.transpose, q[:, g * 128:(g + 1) * 128],
                          p[:, (4 * g4 + g) * 128:(4 * g4 + g + 1) * 128],
                          d["ident"], after=[u["exp"], *w, d["t_const"]])
            c = slice(4 * g4, 4 * g4 + 4)
            t2 = split(pt[:, c, 0, :], pt[:, c, 1, :], q.rearrange("p (a b) -> p a b", a=4), None, [tt], w2)
            PTp.held[i] = [t2]
            ready.append(t2)
        Pr.held[pi] = [tt]
        u["PT"] = (j, pt, ready)

    def stage_d(n):
        b, hf, wi, wj, t, h = units[n]
        u = st[n]
        j, pt, ready = u["PT"]
        wn = u["win"]
        if h % 2 == 0:
            wn["pv"] = PV.take()
        m, o_, w = wn["pv"]
        at = 256 * (h % 2)
        for g in range(8):
            ki, kt = octs[b, hf, 2 * wi + g // 2]
            tt = T.do(nc.tensor.matmul, o_[:, at:at + 256], Vb[ki][:, wj + g % 2, h, :, :].rearrange("p a b -> p (a b)"),
                      pt[:, g, :, :].rearrange("p a b -> p (a b)"), start=(g == 0), stop=(g == 7),
                      after=[*ready, *w, *kt])
        PTr.held[j] = [tt]
        if h % 2:
            ai, A_, w = Ar.take()
            o4 = o_.rearrange("p (h a x) -> p h a x", h=2, a=2)
            ta = S.do(nc.scalar.copy, A_, o4[:, :, 1, :], after=[tt, *w])
            ta = V.do(nc.vector.tensor_tensor, A_, A_, o4[:, :, 0, :], ALU.add, after=[ta])
            PV.held[m] = [ta]
            wn["A"] = (ai, A_, ta)
        if h == 3 and wj == 3 and t == 1:
            for o in (2 * wi, 2 * wi + 1) if wi < 7 else range(14, 18):
                held[octs[b, hf, o][0]].append(tt)

    def stage_f(n):
        b, hf, wi, wj, t, h = units[n]
        if h % 2 == 0:
            return
        u = st[n]
        wn = u["win"]
        if h == 1:
            wn["O"] = Ob.take()
        m, o_, w = wn["O"]
        ai, A_, ta = wn["A"]
        for e in range(2):
            at = 64 * (h - 1 + e)
            tt = T.do(nc.tensor.transpose, o_[:, at:at + 64], A_[:, e, :], d["ident"][0:64, 0:64], after=[*w, ta])
        Ar.held[ai] = [tt]
        if h == 3:
            ri, r = wn["rs"]
            vi, rv, w = rinv.take()
            t1 = V.do(nc.vector.reciprocal, rv, r, after=[u["exp"], *w])
            rsum.held[ri] = [t1]
            oi, ob, w = Osb.take()
            o4 = o_[:, 0:256].rearrange("p (h a x) -> p h a x", h=4, a=2)
            ob4 = ob.rearrange("p (h x) -> p h x", h=4)
            ta = S.do(nc.scalar.copy, ob4, o4[:, :, 1, :], after=[tt, *w])
            t1 = V.do(nc.vector.tensor_tensor, ob4, ob4, o4[:, :, 0, :], ALU.add, after=[t1, ta])
            t2 = V.do(nc.vector.tensor_tensor, ob4, ob4, rv.unsqueeze(2).broadcast_to([128, 4, 32]), ALU.mult,
                      after=[t1])
            rinv.held[vi] = [t2]
            wn["fin"] = (m, o_, oi, ob, t2)

    def stage_e(n):
        b, hf, wi, wj, t, h = units[n]
        if h != 3:
            return
        wn = st[n]["win"]
        m, o_, oi, ob, t2 = wn["fin"]
        tt = T.do(nc.tensor.transpose, o_[:, 256:384], ob, d["ident"], after=[t2])
        Osb.held[oi] = [tt]
        if t == 0:
            win[b, hf, wi, wj] = OT.take()
        ti, ot, w = win[b, hf, wi, wj]
        t3 = S.do(nc.scalar.activation, ot[:, 128 * t:128 * t + 128], o_[:, 256:384], ACT.Identity,
                  bias=bv4[:, 2:3], after=[tt, *w])
        Ob.held[m] = [t3]
        wn["t3"] = t3

    def stage_g(n):
        b, hf, wi, wj, t, h = units[n]
        if h == 3 and t == 1:
            t3 = st[n]["win"]["t3"]
            ti, ot, _ = win[b, hf, wi, wj]
            m, p, w = PTp.take()
            tt = T.do(nc.tensor.matmul, p[:, 0:256], wp, ot, start=True, stop=True, after=[*w, t3])
            OT.held[ti] = [tt]
            if wj == 0:
                rows[b, hf, wi] = outr.take()
            oi, ob, w = rows[b, hf, wi]
            for tt_ in range(2):
                ri = octs[b, hf, 2 * wi + 1 + tt_][0]
                c = 16 * wj + 8 * hf
                t4 = V.do(nc.vector.scalar_tensor_tensor, out=ob[:, 8 * tt_:8 * tt_ + 8, 16 * wj:16 * wj + 16],
                          in0=p[:, 128 * tt_:128 * tt_ + 128].rearrange("p (r c) -> p r c", r=8), scalar=bv4[:, 3:4],
                          in1=raw[ri][:, :, c:c + 16], op0=ALU.add, op1=ALU.add, after=[tt, *w])
            PTp.held[m] = [t4]
            if wj == 3:
                of = ob.rearrange("p a b -> p (a b)")
                for q in range(2):
                    at = ((hf * 8 + wi) * 2 + q) * 6
                    t5 = V.do(nc.vector.bn_stats, stats[:, b, at:at + 6], of[:, q * 512:(q + 1) * 512], after=[t4])
                dst = xout[:, b, :].rearrange("p (r c) -> p r c", c=128)
                ds = k.dma(cho[oi], dst[:, wi * 16:wi * 16 + 16, 64 * hf:64 * hf + 64], ob, after=[t4])
                outr.held[oi] = [t5, ds]
                d["t_stats"] = t5
                for o in (2 * wi, 2 * wi + 1) if wi < 7 else range(14, 18):
                    held[octs[b, hf, o][0]].append(t4)

    N = len(units) // (2 * B)
    for b in range(2 * B):
        for s in range(N + 6):
            for lag, f in ((6, stage_g), (0, stage_a), (1, stage_b), (5, stage_e), (2, stage_c), (4, stage_f),
                           (3, stage_d)):
                if 0 <= s - lag < N:
                    f(b * N + s - lag)
    return d["t_stats"]


def layer1(k, d, I, xin, xout):
    nc = k.nc
    V, S, T, G_ = k.lanes["dve"], k.lanes["act"], k.lanes["pe"], k.lanes["pool"]
    ps = k.ps
    stats = d["stats2"]
    xn = k.buf(128, 128)
    hs = k.buf(128, 128)
    W = k.buf(16, 2, 128)
    F = k.buf(16, 3, 128)
    Gm = k.buf(128, 16, 2)
    XT = Ring([k.buf(4, 128) for _ in range(2)])
    gT = Ring([k.buf(4, 128, parts=32) for _ in range(2)])
    dft = k.buf(48)
    idft = k.buf(128, parts=32)
    sm = k.buf(8)
    c0, cw = k.chan(), k.chan()
    k.dma(c0, dft, I["dft"])
    k.dma(c0, sm[:, 0:7], I["b1"])
    t_c = k.dma(c0, idft, I["idft"])
    Ff = F.rearrange("p a b c -> p (a b) c")
    xf = xn.rearrange("p a b -> p (a b)")
    hf = hs.rearrange("p a b -> p (a b)")
    at = [0]

    def over(n):
        at[0] += n
        return xf[:, at[0] - n:at[0]]

    w0 = over(512)
    w1 = over(512).rearrange("p (a b) -> p a b", a=4)
    h1r = Ring([over(2048).rearrange("p (a b) -> p a b", a=4) for _ in range(2)])
    h2r = Ring([over(512) for _ in range(2)])
    ddr = Ring([over(512) for _ in range(4)])
    sqr = Ring([over(512) for _ in range(2)])
    sdr = Ring([over(512) for _ in range(2)])
    yr = Ring([over(512) for _ in range(2)])
    xr = Ring([over(512) for _ in range(4)])
    outr = Ring([over(512) for _ in range(3)])
    cx = [k.chan() for _ in range(4)]
    cin = [k.chan() for _ in range(4)]
    cxr = [k.chan() for _ in range(4)]
    co = [k.chan() for _ in range(3)]
    cf = k.chan()
    w_free, x_free = [], []
    t_stat = None
    bank = [ps[:, i, :] for i in range(8)]
    XTp = op = Ring(bank[0:2])
    Fp, Gp, gp = Ring(bank[2:4]), Ring(bank[4:6]), Ring(bank[6:8])

    for b in range(B):
        rs, nb = d["rs"][:, b:b + 1], d["nb"][:, b:b + 1]
        tx = []
        for q in range(4):
            ld = k.dma(cin[q], xf[:, q * 4096:(q + 1) * 4096], xin[:, b, q * 4096:(q + 1) * 4096], after=x_free)
            for e, (ln, eng) in enumerate(((S, "a"), (V, "v"))):
                part = xf[:, q * 4096 + e * 2048:q * 4096 + (e + 1) * 2048]
                if eng == "a":
                    tx.append(S.do(nc.scalar.activation, part, part, ACT.Identity, bias=nb, scale=rs, after=[ld]))
                else:
                    tx.append(V.do(nc.vector.tensor_scalar, part, part, rs, nb, ALU.mult, ALU.add, after=[ld]))
        t_hs = []
        for dr in range(2):
            tw = k.dma(cw, W.rearrange("p a b c -> p (a b c)"), I["wf"][dr], after=w_free)
            tF = []
            pend = []
            slot = [None]

            def dft_mms(g, xi, xt, t_ev):
                if g % 2 == 0:
                    slot[0] = Fp.take()
                i, p, w = slot[0]
                for j in range(4):
                    c = (g % 2) * 4 + j
                    tt = T.do(nc.tensor.matmul, p[:, c * 48:(c + 1) * 48], xt[:, j, :], dft,
                              start=True, stop=True, after=[*w, t_ev, t_c])
                XT.held[xi] = [tt]
                if g % 2 == 1:
                    ev = V.do(nc.vector.tensor_copy, Ff[:, :, 4 * g - 4:4 * g + 4],
                              p[:, 0:384].rearrange("p (l k) -> p k l", l=8), after=[tt, *t_hs])
                    Fp.held[i] = [ev]
                    tF.append(ev)

            for g in range(32):
                i, p, w = XTp.take()
                for j in range(4):
                    ln_ = 4 * g + j
                    src = xn[:, ln_, :] if dr == 0 else xn[:, :, ln_]
                    tt = T.do(nc.tensor.transpose, p[:, j * 128:(j + 1) * 128], src, d["ident"],
                              after=[*w, *(tx if dr else tx[0:2 * (g // 8) + 2])])
                xi, xt, w2 = XT.take()
                ev = S.do(nc.scalar.copy, xt.rearrange("p a b -> p (a b)"), p, after=[tt, *w2])
                XTp.held[i] = [ev]
                pend.append((g, xi, xt, ev))
                if len(pend) > 1:
                    dft_mms(*pend.pop(0))
            dft_mms(*pend.pop(0))
            x_last = tt
            tG = []
            for ky in range(16):
                i, p, w = Gp.take()
                o_ = p[:, 0:256]
                T.do(nc.tensor.matmul, o_, W[:, ky, 0, :], F[:, ky, 1:3, :].rearrange("p a b -> p (a b)"),
                     start=True, stop=False, after=[*w, tw, tF[-1]])
                tt = T.do(nc.tensor.matmul, o_, W[:, ky, 1, :], F[:, ky, 0:2, :].rearrange("p a b -> p (a b)"),
                          start=False, stop=True)
                src = o_.rearrange("p (r l) -> p l r", r=2)
                if ky % 2:
                    ev = V.do(nc.vector.tensor_copy, Gm[:, :, ky, :], src, after=[tt])
                else:
                    ev = S.do(nc.scalar.copy, Gm[:, :, ky, :], src, after=[tt])
                Gp.held[i] = [ev]
                tG.append(ev)
            w_free = [tt]
            pend = []

            def inverse(g, gi, gt, t_ev):
                i, p, w = op.take()
                for j in range(4):
                    tt = T.do(nc.tensor.matmul, p[:, j * 128:(j + 1) * 128], gt[:, j, :], idft,
                              start=True, stop=True, after=[*w, t_ev])
                gT.held[gi] = [tt]
                if dr == 0:
                    ev = V.do(nc.vector.tensor_copy, hf[:, g * 512:(g + 1) * 512], p, after=[tt, *hs_free])
                else:
                    o_ = hs[:, :, 4 * g:4 * g + 4]
                    ev = V.do(nc.vector.tensor_tensor, o_, p.rearrange("p (w h) -> p h w", w=4), o_, ALU.add,
                              after=[tt, *t_hs])
                op.held[i] = [ev]
                last[0] = ev

            hs_free = x_free
            last = [None]
            for g in range(32):
                i, p, w = gp.take()
                for j in range(4):
                    tt = T.do(nc.tensor.transpose, p[0:32, j * 128:(j + 1) * 128],
                              Gm[:, 4 * g + j, :, :].rearrange("p a b -> p (a b)"), d["ident"],
                              after=[*w, tG[-1], tG[-2]])
                gi, gt, w2 = gT.take()
                ev = S.do(nc.scalar.copy, gt.rearrange("p a b -> p (a b)"), p[0:32, :], after=[tt, *w2])
                gp.held[i] = [ev]
                pend.append((g, gi, gt, ev))
                if len(pend) > 1:
                    inverse(*pend.pop(0))
            inverse(*pend.pop(0))
            t_hs = [last[0], tt]

        k.dma(cf, w0, I["ff0"], after=[x_last])
        tf = k.dma(cf, w1.rearrange("p a b -> p (a b)"), I["ff1"], after=[x_last])
        h1p, h2p, mp = Ring(bank[0:3]), Ring(bank[3:5]), Ring(bank[5:8])
        u = {n: {} for n in range(32)}
        start = [*op.held[0], *op.held[1], *gp.held[0], *gp.held[1], x_last, t_hs[0]]

        def f0(n):
            i, x, w = xr.take()
            u[n]["x"] = (i, x, k.dma(cxr[i], x, xin[:, b, n * 512:(n + 1) * 512], after=[*w, x_last]))

        def f1(n):
            hi, h1, w1_ = h1r.take()
            for m in range(4):
                i, p, w = h1p.take()
                tt = T.do(nc.tensor.matmul, p, w0[:, m * 128:(m + 1) * 128], hf[:, n * 512:(n + 1) * 512],
                          start=True, stop=True, after=[*w, tf, *start])
                if m < 3:
                    ev = S.do(nc.scalar.activation, h1[:, m, :], p, ACT.Relu, bias=sm[:, m:m + 1],
                              after=[tt, *w1_, t_c])
                else:
                    ev = V.do(nc.vector.tensor_scalar, h1[:, m, :], p, sm[:, m:m + 1], 0.0, ALU.add, ALU.max,
                              after=[tt, *w1_, t_c])
                h1p.held[i] = [ev]
                u[n][f"part{m}"] = ev
            u[n]["h1"] = (hi, h1)
            u[n]["rhs"] = tt

        def f2(n):
            hi, h1 = u[n]["h1"]
            i, p, w = h2p.take()
            for m in range(4):
                tt = T.do(nc.tensor.matmul, p, w1[:, m, :], h1[:, m, :], start=(m == 0), stop=(m == 3),
                          after=[*w, u[n][f"part{m}"]])
            h1r.held[hi] = [tt]
            j, h2, w2 = h2r.take()
            ev = S.do(nc.scalar.activation, h2, p, ACT.Identity, bias=sm[:, 4:5], after=[tt, *w2])
            h2p.held[i] = [ev]
            u[n]["h2"] = (j, h2, ev)

        def f3(n):
            j, h2, ev = u[n]["h2"]
            i, p, w = mp.take()
            tt = T.do(nc.tensor.matmul, p, d["avg"], h2, start=True, stop=True, after=[*w, ev])
            di, dd, w2 = ddr.take()
            t1 = V.do(nc.vector.tensor_tensor, dd, h2, p, ALU.subtract, after=[tt, ev, *w2])
            mp.held[i] = [t1]
            h2r.held[j] = [t1]
            qi, sq, w3 = sqr.take()
            t2 = S.do(nc.scalar.activation, sq, dd, ACT.Square, after=[t1, *w3])
            u[n]["dd"] = (di, dd, t1)
            u[n]["sq"] = (qi, sq, t2)

        def f4(n):
            qi, sq, t2 = u[n]["sq"]
            i, p, w = mp.take()
            tt = T.do(nc.tensor.matmul, p, d["avg"], sq, start=True, stop=True, after=[*w, t2])
            sqr.held[qi] = [tt]
            si, sd, w2 = sdr.take()
            t1 = V.do(nc.vector.tensor_scalar, sd, p, EPS, None, ALU.add, after=[tt, *w2])
            mp.held[i] = [t1]
            t2 = S.do(nc.scalar.activation, sd, sd, ACT.Sqrt, after=[t1])
            u[n]["sd"] = (si, sd, t2)

        def f5(n):
            si, sd, t2 = u[n]["sd"]
            di, dd, t1 = u[n]["dd"]
            yi, y, w = yr.take()
            t3 = V.do(nc.vector.reciprocal, sd, sd, after=[t2])
            t4 = V.do(nc.vector.tensor_tensor, y, dd, sd, ALU.mult, after=[t3, *w])
            sdr.held[si] = [t4]
            ddr.held[di] = [t4]
            t5 = V.do(nc.vector.tensor_scalar, y, y, sm[:, 5:6], sm[:, 6:7], ALU.mult, ALU.add, after=[t4])
            xi, x, tl = u[n]["x"]
            oi, o_, w = outr.take()
            t6 = G_.do(nc.gpsimd.tensor_tensor, o_, y, x, ALU.add, after=[t5, tl, *w])
            yr.held[yi] = [t6]
            xr.held[xi] = [t6]
            t7 = V.do(nc.vector.bn_stats, stats[:, b, n * 6:n * 6 + 6], o_, after=[t6])
            ds = k.dma(co[oi], xout[:, b, n * 512:(n + 1) * 512], o_, after=[t6])
            outr.held[oi] = [t7, ds]
            u[n]["end"] = [t6, t7, ds]

        for s in range(32 + 5):
            for lag, f in ((3, f0), (1, f1), (2, f2), (3, f3), (4, f4), (5, f5)):
                if 0 <= s - lag < 32:
                    f(s - lag)
        x_free = [c for n in (29, 30, 31) for c in u[n]["end"]] + [u[31]["rhs"]]
        t_stat = u[31]["end"][1]
    return t_stat


def layer2(k, d, I, xin, xout):
    nc = k.nc
    V, S, T, P = k.lanes["dve"], k.lanes["act"], k.lanes["pe"], k.lanes["pool"]
    stats = d["stats2"]
    N = 512
    WG = k.buf(3, 128)
    bg = k.buf(6)
    pk = k.buf(4)
    kern = k.buf(4, 128)
    nk = k.buf(2, 128)
    c0 = k.chan()
    k.dma(c0, WG.rearrange("p a b -> p (a b)"), I["wg"])
    k.dma(c0, bg, I["bg"])
    tc = k.dma(c0, kern.rearrange("p a b -> p (a b)"), I["kern"])
    t_k = V.do(nc.vector.tensor_copy, nk[0:64, :, :], kern[0:64, 2:4, :], after=[tc])
    t_k = V.do(nc.vector.tensor_scalar, nk[64:128, :, :], kern[64:128, 2:4, :], -1.0, None, ALU.mult, after=[tc])
    bank = [k.ps[:, i, :] for i in range(8)]
    V.linked = P.linked = True
    for b in range(B):
        for h in range(2):
            for j, s_ in enumerate((d["rs"], d["nb"])):
                t = T.do(nc.tensor.matmul, bank[0][64 * b:64 * b + 64, 2 * h + j:2 * h + j + 1],
                         d["ident"][:, 64 * h:64 * h + 64], s_[:, b:b + 1], start=True, stop=True, after=[tc])
    t_pk = V.do(nc.vector.tensor_copy, pk, bank[0][:, 0:4], after=[t])
    t_bg = V.do(nc.vector.tensor_scalar, bg[:, 0:2], bg[:, 0:2], 2.0, None, ALU.add, after=[tc])

    sets = []
    names2 = ("xp", "q2", "A", "f", "g", "e", "sp", "w2", "res")
    names1 = ("m2", "sg", "m11", "p12", "m21", "m22", "tau", "del", "u1", "u2", "u3", "u4", "u5",
              "a1", "b1", "a2", "b2", "p1", "p2")
    for _ in range(2):
        s = {n: k.buf(2, N) for n in names2}
        s.update({n: k.buf(N) for n in names1})
        s["xc"] = k.buf(2, N)
        s["bas"] = k.buf(N)
        s["ch"] = [k.chan() for _ in range(4)]
        sets.append(s)
    outs = Ring([k.buf(2, N) for _ in range(2)])
    couts = [k.chan() for _ in range(2)]
    done = [[], []]
    sr4, pr = bank[0:4], Ring(bank[4:8])
    sr_held = [[] for _ in range(4)]
    NC = L // N
    loads = {}

    def load(n):
        s, fr = sets[n % 2], done[n % 2]
        sl = slice(n * N, (n + 1) * N)
        c = s["ch"]
        t0 = k.dma(c[0], s["bas"], I["basis"][:, sl], after=fr)
        t1 = k.dma(c[1], s["xc"], xin[:, :, sl], after=fr)
        for b in range(B):
            for h in range(2):
                t2 = k.dma(c[2], s["xp"][64 * b:64 * b + 64, h, :], xin[64 * h:64 * h + 64, b, sl], after=fr)
        for b in range(B):
            for h in range(2):
                t3 = k.dma(c[3], s["res"][64 * b:64 * b + 64, h, :], xin[64 * h:64 * h + 64, b, sl], after=fr)
        loads[n] = (t0, t1, t2, t3)

    load(0)
    for n in range(NC):
        s, fr = sets[n % 2], done[n % 2]
        t_bas, t_xc, t_xp, tr = loads.pop(n)
        t = {}
        for ln in (V, S, T, P):
            ln.first = ln.first + list(fr)
        sp = {}
        for i, (nm, w) in enumerate((("Ar", kern[:, 0, :]), ("Ai", nk[:, 0, :]), ("Br", kern[:, 1, :]),
                                     ("Bi", nk[:, 1, :]))):
            p, wt = sr4[i], sr_held[i]
            sp[nm] = (i, p)
            t[nm] = T.do(nc.tensor.matmul, p, w, s["bas"], start=True, stop=True, after=[*wt, t_bas, t_k, t_pk])
        for b in range(B):
            t["xc"] = S.do(nc.scalar.activation, s["xc"][:, b, :], s["xc"][:, b, :], ACT.Identity,
                           bias=d["nb"][:, b:b + 1], scale=d["rs"][:, b:b + 1], after=[t_xc])
        S.do(nc.scalar.activation, s["q2"][:, 0, :], sp["Ar"][1], ACT.Square, after=[t["Ar"]])
        t["q2"] = S.do(nc.scalar.activation, s["q2"][:, 1, :], sp["Ai"][1], ACT.Square, after=[t["Ai"]])
        t["m2"] = V.do(nc.vector.scalar_tensor_tensor, out=s["m2"], in0=s["q2"][:, 0, :], scalar=1e-8,
                       in1=s["q2"][:, 1, :], op0=ALU.add, op1=ALU.add, after=[t["q2"]])
        t["mag"] = S.do(nc.scalar.activation, s["m2"], s["m2"], ACT.Sqrt, after=[t["m2"]])
        gates = {}
        for gi, gn in enumerate(("f", "g", "e")):
            for h in range(2):
                i, p, wt = pr.take()
                for b in range(B):
                    tt = T.do(nc.tensor.matmul, p[64 * b:64 * b + 64, :], WG[:, gi, 64 * h:64 * h + 64],
                              s["xc"][:, b, :], start=True, stop=True, after=[*wt, t["xc"]])
                if gn == "e":
                    ev = S.do(nc.scalar.activation, s["e"][:, h, :], p, ACT.Abs, bias=bg[:, 4 + h:5 + h], after=[tt])
                    ev2 = V.do(nc.vector.tensor_scalar, s["sp"][:, h, :], p, bg[:, 4 + h:5 + h], 0.0, ALU.add,
                               ALU.max, after=[tt, ev])
                    pr.held[i] = [ev, ev2]
                    t["relu"], t["abs"] = ev2, ev
                else:
                    ev = S.do(nc.scalar.activation, s[gn][:, h, :], p, ACT.Sigmoid,
                              bias=bg[:, 2 * gi + h:2 * gi + h + 1], after=[tt, t_bg])
                    pr.held[i] = [ev]
                    t[gn] = ev
        t["sg"] = S.do(nc.scalar.activation, s["sg"], s["m2"], ACT.Sigmoid, after=[t["mag"]])
        t["ex"] = S.do(nc.scalar.activation, s["e"], s["e"], ACT.Exp, scale=-1.0, after=[t["abs"]])
        t["ln"] = S.do(nc.scalar.activation, s["e"], s["e"], ACT.Ln, bias=1.0, after=[t["ex"]])
        for h in range(2):
            t["xp"] = S.do(nc.scalar.activation, s["xp"][:, h, :], s["xp"][:, h, :], ACT.Identity,
                           bias=pk[:, 2 * h + 1:2 * h + 2], scale=pk[:, 2 * h:2 * h + 1], after=[t_xp, t_pk])
        t["u1"] = V.do(nc.vector.tensor_scalar, s["u1"], s["m2"], 1e-8, None, ALU.add, after=[t["mag"], t["sg"]])
        t["u2"] = V.do(nc.vector.reciprocal, s["u2"], s["u1"], after=[t["u1"]])
        t["u3"] = V.do(nc.vector.scalar_tensor_tensor, out=s["u3"], in0=s["sg"], scalar=0.95, in1=s["u2"],
                       op0=ALU.mult, op1=ALU.mult, after=[t["u2"], t["sg"]])
        for h, nm in enumerate(("Ar", "Ai")):
            t["A"] = V.do(nc.vector.tensor_tensor, s["A"][:, h, :], s["u3"], sp[nm][1], ALU.mult, after=[t["u3"]])
            sr_held[sp[nm][0]] = [t["A"], t["q2"]]
        xr_, xi_ = s["xp"][:, 0, :], s["xp"][:, 1, :]
        V.do(nc.vector.tensor_tensor, s["p1"], xr_, sp["Br"][1], ALU.mult, after=[t["Br"], t["xp"]])
        t["p2"] = V.do(nc.vector.tensor_tensor, s["p2"], xi_, sp["Bi"][1], ALU.mult, after=[t["Bi"]])
        t["q0"] = V.do(nc.vector.tensor_tensor, s["q2"][:, 0, :], s["p1"], s["p2"], ALU.subtract, after=[t["p2"]])
        t["a1"] = V.do(nc.vector.tensor_tensor, s["a1"], xi_, sp["Br"][1], ALU.mult)
        t["b1"] = V.do(nc.vector.tensor_tensor, s["b1"], xr_, sp["Bi"][1], ALU.mult)
        sr_held[sp["Br"][0]] = [t["a1"]]
        sr_held[sp["Bi"][0]] = [t["b1"]]
        t["Bx"] = V.do(nc.vector.tensor_tensor, s["q2"][:, 1, :], s["a1"], s["b1"], ALU.add, after=[t["b1"]])
        t["sp"] = P.do(nc.gpsimd.tensor_tensor, s["sp"], s["sp"], s["e"], ALU.add, after=[t["relu"], t["ln"]])
        t["sg2"] = P.do(nc.gpsimd.tensor_tensor, s["sp"], s["sp"], s["g"], ALU.mult, after=[t["sp"], t["g"]])
        t["inp"] = V.do(nc.vector.scalar_tensor_tensor, out=s["sp"], in0=s["sp"], scalar=0.1, in1=s["q2"],
                        op0=ALU.mult, op1=ALU.mult, after=[t["sg2"], t["Bx"], t["q0"]])
        Ar, Ai, fr_, fi_ = s["A"][:, 0, :], s["A"][:, 1, :], s["f"][:, 0, :], s["f"][:, 1, :]

        def v(o, a, op, b_, *after):
            t[o] = V.do(nc.vector.tensor_tensor, s[o], s[a], s[b_], op, after=[t[x] for x in after])

        def g(o, a, op, b_, *after):
            t[o] = P.do(nc.gpsimd.tensor_tensor, s[o], s[a], s[b_], op, after=[t[x] for x in after])

        t["m11"] = V.do(nc.vector.tensor_tensor, s["m11"], fr_, Ar, ALU.mult, after=[t["A"], t["f"]])
        t["m22"] = V.do(nc.vector.tensor_tensor, s["m22"], fi_, Ar, ALU.mult, after=[t["A"], t["f"]])
        t["p12"] = P.do(nc.gpsimd.tensor_tensor, s["p12"], fr_, Ai, ALU.mult, after=[t["A"], t["f"]])
        t["m21"] = P.do(nc.gpsimd.tensor_tensor, s["m21"], fi_, Ai, ALU.mult, after=[t["A"], t["f"]])
        g("p1", "m11", ALU.mult, "m22", "m11", "m22", "q0")
        v("tau", "m11", ALU.add, "m22", "m11", "m22")
        g("p2", "p12", ALU.mult, "m21", "p12", "m21", "q0")
        g("del", "p1", ALU.add, "p2", "p1", "p2")
        ir, ii = s["sp"][:, 0, :], s["sp"][:, 1, :]
        P.do(nc.gpsimd.tensor_tensor, s["e"][:, 0, :], s["m11"], ir, ALU.mult, after=[t["inp"]])
        P.do(nc.gpsimd.tensor_tensor, s["e"][:, 1, :], s["m21"], ir, ALU.mult)
        P.do(nc.gpsimd.tensor_tensor, s["w2"][:, 0, :], s["p12"], ii, ALU.mult)
        t["w2"] = P.do(nc.gpsimd.tensor_tensor, s["w2"][:, 1, :], s["m22"], ii, ALU.mult)
        P.do(nc.gpsimd.tensor_tensor, s["w2"][:, 0, :], s["e"][:, 0, :], s["w2"][:, 0, :], ALU.subtract,
             after=[t["w2"]])
        t["Mv"] = P.do(nc.gpsimd.tensor_tensor, s["w2"][:, 1, :], s["e"][:, 1, :], s["w2"][:, 1, :], ALU.add)
        v("u1", "tau", ALU.mult, "tau", "tau")
        v("u2", "tau", ALU.mult, "del", "tau", "del")
        t["u3"] = V.do(nc.vector.tensor_scalar, s["u3"], s["del"], -1.0, 1.0, ALU.mult, ALU.add, after=[t["del"]])
        v("b1", "u3", ALU.subtract, "u2", "u3", "u2")
        v("a1", "u1", ALU.add, "tau", "u1")
        v("a1", "a1", ALU.add, "u3", "a1")
        t["u1"] = V.do(nc.vector.scalar_tensor_tensor, out=s["u1"], in0=s["del"], scalar=-2.0, in1=s["u1"],
                       op0=ALU.mult, op1=ALU.add, after=[t["u1"]])
        v("u2", "del", ALU.mult, "del", "del")
        v("u4", "u1", ALU.mult, "u1", "u1")
        t["u4"] = V.do(nc.vector.scalar_tensor_tensor, out=s["u4"], in0=s["u2"], scalar=-2.0, in1=s["u4"],
                       op0=ALU.mult, op1=ALU.add, after=[t["u4"], t["u2"]])
        v("u5", "u2", ALU.mult, "u2", "u2")
        v("m2", "u1", ALU.mult, "del", "u1")
        v("m2", "m2", ALU.add, "u2", "m2", "u2")
        v("u3", "u1", ALU.mult, "tau", "u1")
        v("a2", "u4", ALU.mult, "u4", "u4")
        v("a2", "a2", ALU.add, "u4", "a2")
        t["u2"] = V.do(nc.vector.tensor_scalar, s["u2"], s["u5"], -1.0, 1.0, ALU.mult, ALU.add, after=[t["u5"]])
        v("a2", "a2", ALU.add, "u2", "a2", "u2")
        v("b2", "u4", ALU.mult, "u5", "u5")
        v("b2", "u2", ALU.subtract, "b2", "b2", "u2")
        v("u1", "a2", ALU.mult, "u3", "a2", "u3")
        v("u2", "a2", ALU.mult, "m2", "a2", "m2")
        v("u2", "b2", ALU.subtract, "u2", "u2", "b2")
        v("u3", "a1", ALU.mult, "u1", "a1", "u1")
        v("u4", "u3", ALU.mult, "tau", "u3")
        v("u5", "a1", ALU.mult, "u2", "u2")
        v("m2", "b1", ALU.mult, "u1", "b1")
        v("u4", "u4", ALU.add, "u5", "u4", "u5")
        v("u4", "u4", ALU.add, "m2", "u4", "m2")
        v("b2", "b1", ALU.mult, "u2", "u2")
        v("u3", "u3", ALU.mult, "del", "u3")
        v("b2", "b2", ALU.subtract, "u3", "b2", "u3")
        al = s["u4"].unsqueeze(1).broadcast_to([128, 2, N])
        be = s["b2"].unsqueeze(1).broadcast_to([128, 2, N])
        t["r1"] = V.do(nc.vector.tensor_tensor, s["w2"], s["w2"], al, ALU.mult, after=[t["Mv"], t["u4"]])
        t["r2"] = P.do(nc.gpsimd.tensor_tensor, s["sp"], s["sp"], be, ALU.mult, after=[t["b2"], t["Mv"]])
        if n + 1 < NC:
            load(n + 1)
        t["r3"] = P.do(nc.gpsimd.tensor_tensor, s["w2"], s["w2"], s["sp"], ALU.add, after=[t["r1"], t["r2"]])
        oi, o_, w = outs.take()
        t["o"] = P.do(nc.gpsimd.tensor_tensor, o_, s["w2"], s["res"], ALU.add, after=[t["r3"], tr, *w])
        for h in range(2):
            t["st"] = V.do(nc.vector.bn_stats, d["statp"][:, h, n * 6:n * 6 + 6], o_[:, h, :], after=[t["o"]])
        for b in range(B):
            for h in range(2):
                td = k.dma(couts[oi], xout[64 * h:64 * h + 64, b, n * N:(n + 1) * N],
                           o_[64 * b:64 * b + 64, h, :], after=[t["o"]])
        outs.held[oi] = [t["st"], td]
        done[n % 2] = [t["st"], t["o"], t["xp"], tt]
    V.linked = P.linked = False
    mvp = k.buf(2, 2)
    for h in range(2):
        ta = V.do(nc.vector.bn_aggr, mvp[:, h, :], d["statp"][:, h, :], after=[t["st"]])
    for b in range(B):
        for h in range(2):
            tt = T.do(nc.tensor.matmul, bank[4][64 * h:64 * h + 64, 2 * b:2 * b + 2],
                      d["ident"][:, 64 * b:64 * b + 64], mvp[:, h, :], start=True, stop=True,
                      after=[ta, *pr.held[0]])
    return V.do(nc.vector.tensor_copy, d["mv"].rearrange("p a b -> p (a b)"), bank[4][:, 0:4], after=[tt])


def layer3(k, d, I, xin, xout):
    nc = k.nc
    V, S, T, P = k.lanes["dve"], k.lanes["act"], k.lanes["pe"], k.lanes["pool"]
    ps = k.ps
    U, Y = d["U"], d["Y"]
    win = k.buf(256)
    cwb = k.buf(9, 256)
    cb = k.buf(2)
    c0 = k.chan()
    k.dma(c0, win, I["winx"])
    k.dma(c0, cb, I["convb"])
    t_w = k.dma(c0, cwb.rearrange("p a b -> p (a b)"), I["convw"].partition_broadcast(128))
    for tap in range(9):
        t_cw = V.do(nc.vector.tensor_tensor, cwb[:, tap, :], cwb[:, tap, :], win, ALU.mult, after=[t_w])
    strips = Ring([k.buf(34, 130) for _ in range(2)])
    raws = Ring([k.buf(34, 128) for _ in range(2)])
    for st in strips.bufs:
        t_z = V.do(nc.vector.memset, st, 0.0)
    craw = [k.chan() for _ in range(2)]
    u1 = Ring([k.buf(4, 32, 32) for _ in range(2)])
    u2 = Ring([k.buf(4, 32, 32) for _ in range(2)])
    cu1 = [k.chan() for _ in range(2)]
    cu2 = [k.chan() for _ in range(2)]
    pr = Ring([ps[:, i, :] for i in range(8)])
    rl = {}
    order = [(b, g) for b in range(B) for g in range(4)]

    def load1(n):
        b, g = order[n]
        i, rw, w = raws.take()
        r0, r1 = max(32 * g - 1, 0), min(32 * g + 33, 128)
        o = r0 - (32 * g - 1)
        rl[n] = (i, rw, o, r1 - r0, k.dma(craw[i], rw[:, o:o + r1 - r0, :].rearrange("p a b -> p (a b)"),
                                          xin[:, b, r0 * 128:r1 * 128], after=w))

    load1(0)
    for n, (b, g) in enumerate(order):
        i, rw, o, nr, ld = rl.pop(n)
        j, st, w = strips.take()
        if g in (0, 3) and n > 1:
            t_z = V.do(nc.vector.memset, st[:, 0 if g == 0 else 33, :], 0.0, after=w)
        tn = S.do(nc.scalar.activation, st[:, o:o + nr, 1:129], rw[:, o:o + nr, :], ACT.Identity,
                  bias=d["nb"][:, b:b + 1], scale=d["rs"][:, b:b + 1], after=[ld, *w, t_z])
        raws.held[i] = [tn]
        if n + 1 < len(order):
            load1(n + 1)
        for h in range(2):
            a1, o1, w1 = u1.take()
            a2, o2, w2 = u2.take()
            for r4 in range(8):
                pi, p, wp_ = pr.take()
                for tap in range(9):
                    dy, dx = tap // 3, tap % 3
                    tt = T.do(nc.tensor.matmul, p.rearrange("p (r c) -> p r c", r=4),
                              cwb[:, tap, h * 128:(h + 1) * 128],
                              st[:, 4 * r4 + dy:4 * r4 + dy + 4, dx:dx + 128],
                              start=(tap == 0), stop=(tap == 8), after=[*wp_, tn, t_cw, t_z])
                ev = S.do(nc.scalar.activation, o1[:, :, 4 * r4:4 * r4 + 4, :],
                          p.rearrange("p (r a c) -> p a r c", r=4, a=4), ACT.Silu,
                          bias=cb[:, h:h + 1], after=[tt, *w1])
                pr.held[pi] = [ev]
            for a in range(4):
                ln, eng = (V, nc.vector) if a % 2 else (P, nc.gpsimd)
                t_c = ln.do(eng.tensor_copy, o2[:, a, :, :], o1[:, a, :, :].rearrange("p r c -> p c r"),
                            after=[ev, *w2])
                if a == 2:
                    t_c2 = t_c
            d1 = k.dma(cu1[a1], U[0, b, h, :, g * 4096:(g + 1) * 4096], o1.rearrange("p a r c -> p (a r c)"),
                       after=[ev])
            d2 = k.dma(cu2[a2], U[1, b, h].rearrange("p (a q l) -> p a q l", a=4, q=4)[:, :, g, :],
                       o2.rearrange("p a r c -> p a (r c)"), after=[t_c, t_c2])
            u1.held[a1] = [t_c, t_c2, d1]
            u2.held[a2] = [d2]
        strips.held[j] = [tt]
    k.phase()

    TL = 1024
    NCH, NB = L // TL, TL // 128
    selw = k.buf(16, 128, dt=BF16)
    c0 = k.chan()
    t_sel = k.dma(c0, selw.rearrange("p a b -> p (a b)"), I["sel"])
    par = Ring([(k.buf(2, 120), k.buf(256), k.buf(2, 18), k.buf(2, 16)) for _ in range(2)])
    cpar = [k.chan() for _ in range(2)]
    dsum = k.buf(2, 4)
    cds = k.chan()
    t_ds = k.dma(cds, dsum.rearrange("p a b -> p (a b)"), I["ds"])
    ur = Ring([k.buf(2, TL) for _ in range(2)])
    cu = [k.chan() for _ in range(2)]
    X = k.buf(TL)
    R1 = k.buf(TL)
    Mb = k.buf(TL, dt=BF16)
    S3r = Ring([k.buf(TL, dt=BF16) for _ in range(2)])
    dl = Ring([k.buf(2, TL) for _ in range(2)])
    du = Ring([k.buf(2, TL) for _ in range(2)])
    tmp = k.buf(2, TL)
    CT = Ring([k.buf(NB, 24) for _ in range(2)])
    Bb = Ring([k.buf(TL) for _ in range(3)])
    dA = Ring([k.buf(2, TL) for _ in range(3)])
    dBu = Ring([k.buf(2, TL) for _ in range(3)])
    hr = Ring([k.buf(2, TL) for _ in range(3)])
    accr = Ring([k.buf(NB, 256) for _ in range(2)])
    cacc, cy = [k.chan() for _ in range(2)], [k.chan() for _ in range(2)]
    state = k.buf(2, 16)
    SB = 4
    hsr = Ring([k.buf(SB, 256) for _ in range(2)])
    pp = Ring([ps[:, 0:2, :].rearrange("p a b -> p (a b)"), ps[:, 2:4, :].rearrange("p a b -> p (a b)")])
    hT = Ring([ps[:, 4 + i, :].rearrange("p (j c) -> p j c", j=2) for i in range(4)])
    chunks = []
    for b in range(B):
        for kk in range(4):
            cs = range(NCH) if kk < 2 else range(NCH - 1, -1, -1)
            chunks += [(b, kk, c, n == 0) for n, c in enumerate(cs)]
    C_ = {}
    held_X, held_M, held_tmp = [], [], []
    parn = {}
    y_done = {}
    for o in range(2):
        t_D = V.do(nc.vector.tensor_tensor, dsum[:, :, o:o + 1], dsum[:, :, o:o + 1], dsum[:, :, o + 2:o + 3],
                   ALU.add, after=[t_ds])

    def fetch(n):
        b, kk, c, first = chunks[n]
        e = C_[n] = {}
        if first:
            i, bufs, w = par.take()
            k.dma(cpar[i], bufs[0].rearrange("p a b -> p (a b)"), I["xproj"][kk], after=w)
            k.dma(cpar[i], bufs[1][96:104, :], I["dtw"][kk], after=w)
            tp = k.dma(cpar[i], bufs[2].rearrange("p a b -> p (a b)"), I["par"][kk], after=w)
            ta = S.do(nc.scalar.activation, bufs[3], bufs[2][:, :, 0:16], ACT.Exp, after=[tp, *w])
            ta = V.do(nc.vector.tensor_scalar, bufs[3], bufs[3], -1.0, None, ALU.mult, after=[ta])
            parn[b, kk] = (i, bufs, tp, ta)
        e["par"] = parn[b, kk]
        i, u, w = ur.take()
        for h in range(2):
            t = k.dma(cu[i], u[:, h, :], U[kk % 2, b, h, :, c * TL:(c + 1) * TL], after=w)
        e["u"] = (i, u, t)

    def y_rows(b, kk, c):
        return Y[kk % 2, b, c * TL:(c + 1) * TL, :].rearrange("(j p) d -> p j d", p=128)

    def prep(n):
        b, kk, c, first = chunks[n]
        e = C_[n]
        pi, (xp, dtw, pc, A), tp, ta = e["par"]
        ui, u, tu = e["u"]
        ai, acc, w_acc = accr.take()
        if kk >= 2:
            t_acc = k.dma(cacc[ai], acc, y_rows(b, kk, c), after=[*w_acc, y_done[b, kk - 2, c]])
        i, p, w = pp.take()
        for q in range(2):
            for h in range(2):
                tt = T.do(nc.tensor.matmul, p[0:120, q * 512:(q + 1) * 512], xp[:, h, :],
                          u[:, h, q * 512:(q + 1) * 512], start=(h == 0), stop=(h == 1), after=[*w, tu, tp])
        tX = S.do(nc.scalar.copy, X[0:120, :], p[0:120, :], after=[tt, *held_X])
        si, S3, w3 = S3r.take()
        t1 = S.do(nc.scalar.copy, S3[0:96, :], p[0:96, :], after=[*w3])
        pp.held[i] = [t1]
        yield
        t2 = V.do(nc.vector.tensor_tensor, R1[64:96, :], X[64:96, :], S3[64:96, :], ALU.subtract,
                  after=[t1, tX, *held_M])
        t3 = S.do(nc.scalar.copy, Mb[64:96, :], R1[64:96, :], after=[t2, *held_M])
        t4 = V.do(nc.vector.tensor_tensor, S3[32:64, :], X[32:64, :], S3[32:64, :], ALU.subtract, after=[t1, tX])
        yield
        t5 = V.do(nc.vector.tensor_tensor, S3[64:96, :], R1[64:96, :], Mb[64:96, :], ALU.subtract,
                  after=[t3, t2])
        e["S3"] = (si, S3, [t1, t4, t5])
        held_M[:] = [t5]
        yield
        i, p, w = pp.take()
        for j in range(NB):
            tt = T.do(nc.tensor.transpose, p[:, 24 * j:24 * j + 24], X[96:120, j * 128:(j + 1) * 128],
                      d["ident"][96:120, 96:120], after=[*w, tX])
        ci, ct, w = CT.take()
        t6 = S.do(nc.scalar.copy, ct.rearrange("p a b -> p (a b)"), p[:, 0:24 * NB], after=[tt, *w])
        pp.held[i] = [t6]
        e["CT"] = (ci, ct, t6)
        t_ct = tt
        yield
        di, de, wd = dl.take()
        for h in range(2):
            i, p, w = pp.take()
            for q in range(2):
                tt = T.do(nc.tensor.matmul, p[:, q * 512:(q + 1) * 512], dtw[96:104, h * 128:(h + 1) * 128],
                          X[96:104, q * 512:(q + 1) * 512], start=True, stop=True, after=[*w, tX])
            bias = pc[:, h, 16:17]
            t7 = S.do(nc.scalar.activation, tmp[:, h, :], p, ACT.Abs, bias=bias, after=[tt, *held_tmp])
            t8 = V.do(nc.vector.tensor_scalar, de[:, h, :], p, bias, 0.0, ALU.add, ALU.max, after=[tt, t7, *wd])
            pp.held[i] = [t8]
            yield
        held_X[:] = [tt, t2, t4, t_ct]
        t9 = S.do(nc.scalar.activation, tmp, tmp, ACT.Exp, scale=-1.0, after=[t7])
        t10 = S.do(nc.scalar.activation, tmp, tmp, ACT.Ln, bias=1.0, after=[t9])
        yield
        t11 = P.do(nc.gpsimd.tensor_tensor, de, de, tmp, ALU.add, after=[t10, t8])
        held_tmp[:] = [t11]
        yield
        qi, dq, wq_ = du.take()
        t12 = P.do(nc.gpsimd.tensor_tensor, dq, de, u, ALU.mult, after=[t11, tu, *wq_])
        e["dl"], e["du"] = (di, de, t11), (qi, dq, t12)
        last_u = [t12, tt]
        yield
        if kk < 2:
            for h in range(2):
                t13 = S.do(nc.scalar.mul, tmp[:, h, :], u[:, h, :], dsum[:, h, kk:kk + 1], after=[t11, t_D, tu])
            for g in range(2):
                yield
                i, p, w = pp.take()
                for j in range(4):
                    for h in range(2):
                        tt = T.do(nc.tensor.transpose, p[:, j * 256 + h * 128:j * 256 + h * 128 + 128],
                                  tmp[:, h, (4 * g + j) * 128:(4 * g + j + 1) * 128], d["ident"], after=[*w, t13])
                t_acc = S.do(nc.scalar.copy, acc[:, 4 * g:4 * g + 4, :].rearrange("p a b -> p (a b)"), p,
                             after=[tt, *w_acc])
                pp.held[i] = [t_acc]
            held_tmp[:] = [t11, tt]
            last_u.append(t13)
        ur.held[ui] = last_u
        e["acc"] = (ai, acc, t_acc)
        e["acc_t"] = [t_acc] * NB

    iters = [(n, m) for n in range(len(chunks)) for m in range(16)]
    E = {}

    def bc(it):
        n, m = iters[it]
        si, S3, ts = C_[n]["S3"]
        i, p, w = pp.take()
        for q in range(2):
            tt = T.do(nc.tensor.matmul, p[:, q * 512:(q + 1) * 512], selw[0:96, m, :],
                      S3[0:96, q * 512:(q + 1) * 512], start=True, stop=True, after=[*w, *ts, t_sel])
        j, o_, w2 = Bb.take()
        ev = S.do(nc.scalar.copy, o_, p, after=[tt, *w2])
        pp.held[i] = [ev]
        E[it] = {"B": (j, o_, ev)}
        if m == 15:
            S3r.held[si] = [tt]

    def ex(it):
        n, m = iters[it]
        e, r = C_[n], E[it]
        pi, (xp, dtw, pc, A), tp, ta = e["par"]
        di, de, td = e["dl"]
        j, a, w = dA.take()
        for h in range(2):
            t = S.do(nc.scalar.activation, a[:, h, :], de[:, h, :], ACT.Exp, scale=A[:, h, m:m + 1],
                     after=[td, ta, *w])
        r["dA"] = (j, a, t)
        qi, dq, tq = e["du"]
        bj, bb, tb = r["B"]
        j, q, w = dBu.take()
        t2 = P.do(nc.gpsimd.tensor_tensor, q, dq, bb.unsqueeze(1).broadcast_to([128, 2, TL]), ALU.mult,
                  after=[tq, tb, *w])
        Bb.held[bj] = [t2]
        r["dBu"] = (j, q, t2)
        if m == 15:
            dl.held[di] = [t]
            du.held[qi] = [t2]
            par.held[pi] = [t]

    st_t = {}

    def scan(it):
        n, m = iters[it]
        b, kk, c, first = chunks[n]
        r = E[it]
        j, a, ta = r["dA"]
        i, q, tq = r["dBu"]
        hj, hb, w = hr.take()
        step, end = (1, TL - 1) if kk < 2 else (-1, 0)
        for h in range(2):
            t = V.do(nc.vector.tensor_tensor_scan, hb[:, h, ::step], a[:, h, ::step], q[:, h, ::step],
                     0.0 if first else state[:, h, m:m + 1], ALU.mult, ALU.add, after=[ta, tq, *w, *st_t.get(m, [])])
        dA.held[j] = [t]
        dBu.held[i] = [t]
        r["h"] = (hj, hb, t, end)

    def outp(it):
        n, m = iters[it]
        b, kk, c, first = chunks[n]
        e, r = C_[n], E[it]
        hj, hb, t, end = r["h"]
        ci, ct, t_ct = e["CT"]
        ai, acc, t_acc = e["acc"]
        ts = V.do(nc.vector.tensor_copy, state[:, :, m:m + 1], hb[:, :, end:end + 1], after=[t])
        st_t[m] = [ts]
        xi, xs, wx = hsr.take()
        for g in (0, 2, 1, 3):
            i, p, w = hT.take()
            for j in range(2):
                for h in range(2):
                    l0 = (2 * g + j) * 128
                    tt = T.do(nc.tensor.transpose, p[:, j, h * 128:(h + 1) * 128], hb[:, h, l0:l0 + 128],
                              d["ident"], after=[*w, t])
            for j in range(2):
                q = 2 * g + j
                if q < SB:
                    ty = S.do(nc.scalar.mul, xs[:, q, :], p[:, j, :], ct[:, q, 8 + m:9 + m],
                              after=[tt, t_ct, *wx])
                    t_xs = ty
                else:
                    ty = V.do(nc.vector.scalar_tensor_tensor, out=acc[:, q, :], in0=p[:, j, :],
                              scalar=ct[:, q, 8 + m:9 + m], in1=acc[:, q, :], op0=ALU.mult, op1=ALU.add,
                              after=[tt, t_ct, e["acc_t"][q]])
                    e["acc_t"][q] = ty
            hT.held[i] = [ty]
        r["hs"] = (xi, xs, t_xs, ty)
        hr.held[hj] = [tt, ts]

    def addp(it):
        n, m = iters[it]
        b, kk, c, first = chunks[n]
        e, r = C_[n], E.pop(it)
        xi, xs, t_xs, ty = r["hs"]
        ci = e["CT"][0]
        ai, acc, t_acc = e["acc"]
        ty2 = V.do(nc.vector.tensor_tensor, acc[:, 0:SB, :], acc[:, 0:SB, :], xs, ALU.add,
                   after=[t_xs, e["acc_t"][0]])
        e["acc_t"][0] = ty2
        hsr.held[xi] = [ty2]
        if m == 15:
            CT.held[ci] = [ty, t_xs]
            td = k.dma(cy[ai], y_rows(b, kk, c), acc, after=[ty, ty2])
            y_done[b, kk, c] = td
            accr.held[ai] = [td]

    NI = len(iters)
    fetch(0)
    for _ in prep(0):
        pass
    fetch(1)
    going = None
    for s in range(NI + 4):
        if s < NI:
            n, m = iters[s]
            if m == 4 and n + 1 < len(chunks):
                going = prep(n + 1)
            if going is not None:
                next(going, None)
            bc(s)
        if 0 <= s - 1 < NI:
            ex(s - 1)
        if 0 <= s - 2 < NI:
            scan(s - 2)
        if 0 <= s - 4 < NI:
            addp(s - 4)
        if 0 <= s - 3 < NI:
            outp(s - 3)
        if s < NI and m == 15 and n + 2 < len(chunks):
            fetch(n + 2)
    k.phase()

    wz = k.buf(256)
    wo = k.buf(2, 128)
    lnp = k.buf(2, 2)
    c0 = k.chan()
    k.dma(c0, wz, I["winz"])
    k.dma(c0, wo.rearrange("p a b -> p (a b)"), I["wout"])
    t_c = k.dma(c0, lnp.rearrange("p a b -> p (a b)"), I["lnp"])
    N = 512
    xr = Ring([k.buf(N) for _ in range(6)])
    xnr = Ring([k.buf(N) for _ in range(2)])
    yr = Ring([k.buf(4, 256) for _ in range(5)])
    y2r = Ring([k.buf(4, 256) for _ in range(4)])
    bsr = Ring([(k.buf(4, 6), k.buf(4, 2), k.buf(4)) for _ in range(3)])
    gr = Ring([k.buf(2, N) for _ in range(3)])
    zr = Ring([k.buf(2, N) for _ in range(5)])
    outr = Ring([k.buf(N) for _ in range(3)])
    cx, cyr = [k.chan() for _ in range(6)], [k.chan() for _ in range(5)]
    cy2, co = [k.chan() for _ in range(4)], [k.chan() for _ in range(3)]
    bk = [ps[:, i, :] for i in range(8)]
    tp_, zp, op = Ring(bk[0:4]), Ring(bk[4:6]), Ring(bk[6:8])
    u = {}

    def g0(n):
        b, r = n // 32, n % 32
        i, x, w = xr.take()
        tx = k.dma(cx[i], x, xin[:, b, r * N:(r + 1) * N], after=w)
        j, y, w = yr.take()
        ty = k.dma(cyr[j], y, Y[0, b, r * N:(r + 1) * N, :].rearrange("(a p) d -> p a d", p=128), after=w)
        j2, y2, w = y2r.take()
        ty2 = k.dma(cy2[j2], y2, Y[1, b].rearrange("(w h) d -> w h d", h=128)[:, 4 * r:4 * r + 4, :], after=w)
        u[n] = {"x": (i, x, tx), "y": (j, y, ty), "y2": (j2, y2, ty2)}

    def g1(n):
        e, b = u[n], n // 32
        i, x, tx = e["x"]
        j, y, ty = e["y"]
        j2, y2, ty2 = e["y2"]
        t1 = P.do(nc.gpsimd.tensor_tensor, y, y, y2, ALU.add, after=[ty, ty2])
        y2r.held[j2] = [t1]
        e["y1"] = t1
        q, xn, w = xnr.take()
        t2 = V.do(nc.vector.tensor_scalar, xn, x, d["rs"][:, b:b + 1], d["nb"][:, b:b + 1], ALU.mult, ALU.add,
                  after=[tx, *w])
        zi, z, w = zr.take()
        for h in range(2):
            m, p, w2 = zp.take()
            tt = T.do(nc.tensor.matmul, p, wz[:, h * 128:(h + 1) * 128], xn, start=True, stop=True,
                      after=[t2, *w2, t_c])
            t3 = S.do(nc.scalar.activation, z[:, h, :], p, ACT.Silu, after=[tt, *w])
            zp.held[m] = [t3]
        xnr.held[q] = [tt]
        e["z"] = (zi, z, t3)

    def g2(n):
        e = u[n]
        j, y, ty = e["y"]
        si, (bs, mv, sd), w = bsr.take()
        for a in range(4):
            t1 = V.do(nc.vector.bn_stats, bs[:, a, :], y[:, a, :], after=[e["y1"], *w])
        for a in range(4):
            t1 = V.do(nc.vector.bn_aggr, mv[:, a, :], bs[:, a, :], after=[t1])
        t1 = V.do(nc.vector.tensor_scalar, sd, mv[:, :, 1], EPS, None, ALU.add, after=[t1])
        t1 = S.do(nc.scalar.activation, sd, sd, ACT.Sqrt, after=[t1])
        t1 = V.do(nc.vector.reciprocal, sd, sd, after=[t1])
        e["st"] = (si, mv, sd, t1)

    def g3(n):
        e = u[n]
        j, y, ty = e["y"]
        si, mv, sd, t1 = e["st"]
        for a in range(4):
            t2 = V.do(nc.vector.tensor_scalar, y[:, a, :], y[:, a, :], mv[:, a, 0:1], sd[:, a:a + 1],
                      ALU.subtract, ALU.mult, after=[t1])
        bsr.held[si] = [t2]
        gi, g, wg_ = gr.take()
        for h in range(2):
            m, p, w = tp_.take()
            for a in range(4):
                tt = T.do(nc.tensor.transpose, p[:, a * 128:(a + 1) * 128], y[:, a, h * 128:(h + 1) * 128],
                          d["ident"], after=[t2, *w])
            t3 = S.do(nc.scalar.activation, g[:, h, :], p, ACT.Identity, bias=lnp[:, h, 1:2],
                      scale=lnp[:, h, 0:1], after=[tt, t_c, *wg_])
            tp_.held[m] = [t3]
        yr.held[j] = [tt]
        zi, z, tz = e["z"]
        t4 = P.do(nc.gpsimd.tensor_tensor, z, z, g, ALU.mult, after=[t3, tz])
        gr.held[gi] = [t4]
        e["g"] = t4

    def g4(n):
        e, b = u.pop(n), n // 32
        zi, z, tz = e["z"]
        m, p, w = op.take()
        for h in range(2):
            tt = T.do(nc.tensor.matmul, p, wo[:, h, :], z[:, h, :], start=(h == 0), stop=(h == 1),
                      after=[e["g"], *w])
        zr.held[zi] = [tt]
        oi, o_, w = outr.take()
        xi, x, tx = e["x"]
        t7 = V.do(nc.vector.tensor_tensor, o_, x, p, ALU.add, after=[tt, *w])
        op.held[m] = [t7]
        xr.held[xi] = [t7]
        outr.held[oi] = [k.dma(co[oi], xout[:, b, (n % 32) * N:(n % 32 + 1) * N], o_, after=[t7])]

    for s in range(64 + 4):
        for lag, f in ((4, g4), (3, g3), (2, g2), (1, g1), (0, g0)):
            if 0 <= s - lag < 64:
                f(s - lag)
    return None


LAYERS = {0: layer0, 1: layer1, 2: layer2, 3: layer3}

def program(nc, I, xin, scratch, out, layers=(0, 1, 2, 3)):
    with ExitStack() as ctx:
        k = Core(nc, ctx)
        d = {}
        d["grp"] = k.buf(128)
        d["ident"] = k.buf(128)
        d["avg"] = k.buf(128)
        d["rs"] = k.buf(2)
        d["nb"] = k.buf(2)
        d["mv"] = k.buf(2, 2)
        d["sm"] = k.buf(8)
        d["stats"] = k.buf(2, 192)
        d["stats2"] = d["stats"]
        d["statp"] = d["stats"]
        d["U"] = nc.dram_tensor("U", (2, B, 2, 128, L), F32).ap()
        d["Y"] = nc.dram_tensor("Y", (2, B, L, 256), F32).ap()
        cc = k.chan()
        k.dma(cc, d["grp"], I["grp"])
        k.dma(cc, d["ident"], I["ident"])
        d["t_const"] = k.dma(cc, d["avg"], I["avg"])
        k.arena("mem0", 21800, 28928)
        t = first_stats(k, d, xin)
        t = norm_params(k, d, d["stats"], [t])
        x = xin
        fns = LAYERS
        for n, lay in enumerate(layers):
            k.phase()
            if lay and n <= 1:
                k.arena("mem", 50800)
            y = out if n == len(layers) - 1 else scratch[n % 2]
            t = fns[lay](k, d, I, x, y)
            if n < len(layers) - 1:
                k.phase()
                norm_params(k, d, d["stats"], [t], aggregate=lay != 2)
            x = y
        k.play()
        k.held.close()


def _rel_index():
    q = np.arange(256)
    o, cb, r, c = np.meshgrid(np.arange(4), np.arange(2), np.arange(8), np.arange(16), indexing="ij")
    rk, ck = (8 * o + r).ravel(), (16 * cb + c).ravel()
    rq, cq = 8 + q // 32, q % 32
    return (47 * (rq[:, None] - rk + 23) + cq[:, None] - ck + 23) % (47 * 47)


def _lay(inputs):
    g = {n: np.asarray(a) for n, a in inputs.items()}
    f = np.float32
    I = {"x": np.ascontiguousarray(g["x"].transpose(3, 0, 1, 2).reshape(128, B, L))}
    for n in "qkvp":
        I["w" + n] = np.ascontiguousarray(g[f"L0_conv_W{n}"].T)
    I["b0"] = np.stack([g[f"L0_conv_b{n}"] for n in "qkvp"], 1)
    t = g["L0_conv_bias_table"].T[:, _rel_index()]
    I["rel"] = np.ascontiguousarray(t.reshape(4, 2, 128, 1024).transpose(2, 1, 0, 3).reshape(128, 8192))
    a = np.arange(128)
    I["grp"] = (a[:, None] // 4 == a // 4).astype(f) / 4
    I["ident"] = np.eye(128, dtype=f)
    I["avg"] = np.full((128, 128), 1 / 128, f)
    I["wf"] = np.ascontiguousarray(np.stack([g[f"L1_conv_w{n}"].transpose(0, 2, 3, 1) for n in (1, 2)])
                                   .reshape(2, 128, 4096))
    y, m = np.arange(128), np.arange(16)
    th = 2 * np.pi * ((y[:, None] * m) % 128) / 128
    n_ = 128 ** -0.5
    I["dft"] = (np.stack([np.sin(th), np.cos(th), -np.sin(th)], 2).reshape(128, 48) * n_).astype(f)
    w = np.where(m == 0, 1.0, 2.0) * n_
    I["idft"] = np.stack([w * np.cos(th), -w * np.sin(th)], 2).reshape(128, 32).T.astype(f)
    I["ff0"] = g["L1_conv_ff_w0"]
    I["ff1"] = g["L1_conv_ff_w1"].reshape(4, 128, 128).transpose(1, 0, 2).reshape(128, 512)
    I["b1"] = np.concatenate([g["L1_conv_ff_b0"].reshape(4, 128).T] +
                             [g["L1_conv_" + n][:, None] for n in ("ff_b1", "ln_g", "ln_b")], 1)
    I["wg"] = np.concatenate([g[f"L2_conv_W{n}"] for n in "fid"], 1)
    bg = [g[f"L2_conv_b{n}"][64 * h:64 * h + 64] for n in "fid" for h in range(2)]
    I["bg"] = np.stack([np.concatenate([v, v]) for v in bg], 1)
    kern = np.zeros((128, 4, 2, 64), f)
    for i, n in enumerate("AB"):
        re, im = (g[f"L2_conv_{n}_{p}"].reshape(64, 49).T[:, None, :] for p in ("real", "imag"))
        kern[0:49, i], kern[64:113, i] = re, im
        kern[0:49, 2 + i], kern[64:113, 2 + i] = im, re
    I["kern"] = kern.reshape(128, 512)
    p, q = np.arange(49) // 7, np.arange(49) % 7
    u = np.arange(128)
    ph = (u[None, :, None] * (60 + p)[:, None, None] + u[None, None, :] * (60 + q)[:, None, None]) % 128
    ph = (2 * np.pi * ph / 128).reshape(49, L)
    basis = np.zeros((128, L), f)
    basis[0:49], basis[64:113] = np.cos(ph), np.sin(ph)
    I["basis"] = basis
    win = g["L3_conv_W_in"].T
    I["winx"], I["winz"] = win[:, 0:256], win[:, 256:512]
    I["convw"] = g["L3_conv_conv_w"].reshape(256, 9).T.reshape(2304)
    half = lambda v: v.reshape(2, 128, *v.shape[1:])
    I["convb"] = half(g["L3_conv_conv_b"]).T
    xp = np.zeros((4, 256, 120), f)
    pw = g["L3_conv_x_proj_w"].transpose(0, 2, 1)
    for q in range(3):
        xp[:, :, 32 * q:32 * q + 16] = pw[:, :, 8:24]
    xp[:, :, 96:104], xp[:, :, 104:120] = pw[:, :, 0:8], pw[:, :, 24:40]
    I["xproj"] = xp.reshape(4, 2, 128, 120).transpose(0, 2, 1, 3).reshape(4, 128, 240)
    I["ds"] = g["L3_conv_Ds"].reshape(4, 2, 128).transpose(2, 1, 0).reshape(128, 8)
    I["dtw"] = g["L3_conv_dt_proj_w"].transpose(0, 2, 1)
    par = np.concatenate([g["L3_conv_A_logs"].reshape(4, 256, 16), g["L3_conv_dt_proj_b"].reshape(4, 256, 1),
                          g["L3_conv_Ds"].reshape(4, 256, 1)], 2)
    I["par"] = par.reshape(4, 2, 128, 18).transpose(0, 2, 1, 3).reshape(4, 128, 36)
    sel = np.zeros((128, 16, 128), mybir.dt.np(BF16))
    for r in range(16):
        sel[[r, 32 + r, 64 + r], r, :] = 1
    I["sel"] = sel.reshape(128, 2048)
    I["lnp"] = np.stack([half(g["L3_conv_ln_w"]), half(g["L3_conv_ln_b"])], 2).transpose(1, 0, 2).reshape(128, 4)
    I["wout"] = g["L3_conv_W_out"].T.reshape(2, 128, 128).transpose(1, 0, 2).reshape(128, 256)
    return I


def _build(nc, arrays, layers=(0, 1, 2, 3)):
    I = {n[3:]: nc.dram_tensor(n, a.shape, mybir.dt.from_np(a.dtype), kind="ExternalInput").ap()
         for n, a in arrays.items()}
    out = nc.dram_tensor("out_dram", (128, B, L), F32, kind="ExternalOutput").ap()
    scratch = [nc.dram_tensor(f"scr{i}", (128, B, L), F32).ap() for i in range(2)]
    program(nc, I, I["x"], scratch, out, layers)


def kernel(**inputs):
    import concourse.bacc as _bacc
    from concourse.bass_utils import run_bass_kernel_spmd as _run

    arrays = {f"in_{n}": np.ascontiguousarray(a) for n, a in _lay(inputs).items()}
    nc = _bacc.Bacc("TRN2", target_bir_lowering=False, num_devices=1)
    _build(nc, arrays)
    r = _run(nc, [arrays], core_ids=[0])
    return np.ascontiguousarray(r.results[0]["out_dram"].reshape(128, B, HW, HW).transpose(1, 2, 3, 0))
```
